# Optimizing a Trainium2 kernel written in Bass

```python
import numpy as np
import jax
import jax.numpy as jnp

def _softmax(x, axis=-1):
    return jax.nn.softmax(x, axis=axis)

def _gelu(x):
    return jax.nn.gelu(x, approximate=True)

def _silu(x):
    return jax.nn.silu(x)

def _sigmoid(x):
    return jax.nn.sigmoid(x)

def _layernorm(x, axis=-1, eps=1e-05):
    m = jnp.mean(x, axis=axis, keepdims=True)
    v = jnp.var(x, axis=axis, keepdims=True)
    return (x - m) / jnp.sqrt(v + eps)

def _scatter_add(tgt, idx, src, axis=0):
    return tgt.at[idx].add(src)

def _segment_sum(src, seg, n):
    return jax.ops.segment_sum(src, seg, n)
kernel_name = 'mk_macaron_d2_jaxref_r8_67fc8e'

def setup_inputs(seed: int=0):
    np.random.seed(seed)
    _w = jnp.asarray

    def _L0_attn_setup():
        import jax, jax.numpy as jnp
        import numpy as np
        NUM_HEADS = 16
        key = jax.random.key(seed)
        k1, k2, k3, k4 = jax.random.split(key, 4)
        d_model = 128
        B, S = (4, 256)
        scale = 1.0 / np.sqrt(d_model)
        x = jax.random.normal(k1, (B, S, d_model), dtype=jnp.float32)
        W_k = jax.random.normal(k2, (d_model, d_model), dtype=jnp.float32) * scale
        W_v = jax.random.normal(k3, (d_model, d_model), dtype=jnp.float32) * scale
        W_o = jax.random.normal(k4, (d_model, d_model), dtype=jnp.float32) * scale
        return {'x': x, 'W_k': W_k, 'W_v': W_v, 'W_o': W_o}
    _L0_attn_in = _L0_attn_setup()

    def _L0_ffn_setup():
        import jax, jax.numpy as jnp
        import numpy as np
        N_EMBD = 128
        N_STATE = 512
        key = jax.random.key(seed)
        k_x, k_w1, k_b1, k_w2, k_b2 = jax.random.split(key, 5)
        x = jax.random.normal(k_x, (4, 256, N_EMBD), dtype=jnp.float32)
        w1 = jax.random.normal(k_w1, (N_EMBD, N_STATE), dtype=jnp.float32) * (1.0 / np.sqrt(N_EMBD))
        b1 = jax.random.normal(k_b1, (N_STATE,), dtype=jnp.float32) * 0.02
        w2 = jax.random.normal(k_w2, (N_STATE, N_EMBD), dtype=jnp.float32) * (1.0 / np.sqrt(N_STATE))
        b2 = jax.random.normal(k_b2, (N_EMBD,), dtype=jnp.float32) * 0.02
        return {'x': x, 'w1': w1, 'b1': b1, 'w2': w2, 'b2': b2}
    _L0_ffn_in = _L0_ffn_setup()

    def _L1_attn_setup():
        import jax, jax.numpy as jnp
        import numpy as np
        DIM = 128
        HEADS = 16
        DIM_HEAD = 64
        INNER = HEADS * DIM_HEAD

        def _attention(x, ln_gamma, ln_beta, w_qkv, w_out, b_out):
            b, n, _ = x.shape
            scale = DIM_HEAD ** (-0.5)
            mu = jnp.mean(x, axis=-1, keepdims=True)
            var = jnp.var(x, axis=-1, keepdims=True)
            xn = (x - mu) / jnp.sqrt(var + 1e-05) * ln_gamma + ln_beta
            qkv = jnp.einsum('bnd,ed->bne', xn, w_qkv)
            q, k, v = jnp.split(qkv, 3, axis=-1)
            reshape = lambda t: t.reshape(b, n, HEADS, DIM_HEAD).transpose(0, 2, 1, 3)
            q, k, v = (reshape(q) * scale, reshape(k), reshape(v))
            sim = jnp.einsum('bhid,bhjd->bhij', q, k)
            mask_value = -jnp.finfo(sim.dtype).max
            causal = jnp.triu(jnp.ones((n, n), dtype=bool), k=1)
            sim = jnp.where(causal, mask_value, sim)
            sim = sim - jax.lax.stop_gradient(jnp.max(sim, axis=-1, keepdims=True))
            attn = jax.nn.softmax(sim, axis=-1)
            out = jnp.einsum('bhij,bhjd->bhid', attn, v)
            out = out.transpose(0, 2, 1, 3).reshape(b, n, INNER)
            return jnp.einsum('bne,de->bnd', out, w_out) + b_out
        key = jax.random.key(seed)
        ks = jax.random.split(key, 6)
        x = jax.random.normal(ks[0], (2, 256, DIM), dtype=jnp.float32)
        ln_gamma = jnp.ones((DIM,), dtype=jnp.float32)
        ln_beta = jnp.zeros((DIM,), dtype=jnp.float32)
        w_qkv = jax.random.normal(ks[1], (3 * INNER, DIM), dtype=jnp.float32) * DIM ** (-0.5)
        w_out = jax.random.normal(ks[2], (DIM, INNER), dtype=jnp.float32) * INNER ** (-0.5)
        b_out = jax.random.normal(ks[3], (DIM,), dtype=jnp.float32) * 0.02
        return {'x': x, 'ln_gamma': ln_gamma, 'ln_beta': ln_beta, 'w_qkv': w_qkv, 'w_out': w_out, 'b_out': b_out}
    _L1_attn_in = _L1_attn_setup()

    def _L1_ffn_setup():
        import jax, jax.numpy as jnp
        import numpy as np
        DIM = 128
        DEPTH = 2
        HEADS = 8
        DIM_HEAD = 64
        WINDOW = 64
        INNER = HEADS * DIM_HEAD
        HID = int(DIM * 4 * 2 / 3)
        B, N = (2, 1024)
        QK_SCALE = 8.0

        def shift_token(t):
            t1, t2 = jnp.split(t, 2, axis=-1)
            t2 = jnp.pad(t2, ((0, 0), (1, 0), (0, 0)))[:, :-1]
            return jnp.concatenate([t1, t2], axis=-1)

        def l2norm(t):
            return t / jnp.clip(jnp.linalg.norm(t, axis=-1, keepdims=True), 1e-12)

        def rotate_half(x):
            x1, x2 = jnp.split(x, 2, axis=-1)
            return jnp.concatenate([-x2, x1], axis=-1)

        def rotary_xpos(q, k):
            n = q.shape[-2]
            half_idx = jnp.arange(0, DIM_HEAD, 2, dtype=jnp.float32)
            inv_freq = 1.0 / 10000.0 ** (half_idx / DIM_HEAD)
            t = jnp.arange(n, dtype=jnp.float32)
            freqs = t[:, None] * inv_freq[None, :]
            freqs = jnp.concatenate([freqs, freqs], axis=-1)
            base = (half_idx + 0.4 * DIM_HEAD) / (1.4 * DIM_HEAD)
            power = (t - n // 2) / float(WINDOW // 2)
            scale = base[None, :] ** power[:, None]
            scale = jnp.concatenate([scale, scale], axis=-1)
            cos, sin = (jnp.cos(freqs), jnp.sin(freqs))
            q = q * cos * scale + rotate_half(q) * sin * scale
            k = k * cos / scale + rotate_half(k) * sin / scale
            return (q, k)

        def local_attention(q, k, v):
            b, h, n, d = q.shape
            w = n // WINDOW
            bq = q.reshape(b, h, w, WINDOW, d) * QK_SCALE
            bk = k.reshape(b, h, w, WINDOW, d)
            bv = v.reshape(b, h, w, WINDOW, d)

            def look_around(t):
                p = jnp.pad(t, ((0, 0), (0, 0), (1, 0), (0, 0), (0, 0)))
                return jnp.concatenate([p[:, :, :w], p[:, :, 1:]], axis=3)
            bk, bv = (look_around(bk), look_around(bv))
            bt = jnp.arange(n).reshape(w, WINDOW)
            btp = jnp.pad(bt, ((1, 0), (0, 0)), constant_values=-1)
            btk = jnp.concatenate([btp[:w], btp[1:]], axis=1)
            sim = jnp.einsum('bhwid,bhwjd->bhwij', bq, bk)
            i = bt[:, :, None]
            j = btk[:, None, :]
            mask = (i < j) | (i > j + WINDOW) | (j == -1)
            sim = jnp.where(mask, -jnp.finfo(sim.dtype).max, sim)
            attn = jax.nn.softmax(sim, axis=-1)
            out = jnp.einsum('bhwij,bhwjd->bhwid', attn, bv)
            return out.reshape(b, h, n, d)

        def _layer(x, wqkv, qs, ksc, wo, lg, lb, w1, b1, w2, b2):
            b, n, _ = x.shape
            h = shift_token(x)
            qkv = h @ wqkv
            q, k, v = jnp.split(qkv, 3, axis=-1)
            to_heads = lambda t: t.reshape(b, n, HEADS, DIM_HEAD).transpose(0, 2, 1, 3)
            q, k, v = (to_heads(q), to_heads(k), to_heads(v))
            q = l2norm(q) * qs
            k = l2norm(k) * ksc
            q, k = rotary_xpos(q, k)
            o = local_attention(q, k, v)
            o = o.transpose(0, 2, 1, 3).reshape(b, n, INNER)
            x = x + o @ wo
            h = shift_token(x)
            mu = h.mean(-1, keepdims=True)
            var = h.var(-1, keepdims=True)
            h = (h - mu) / jnp.sqrt(var + 1e-05) * lg + lb
            h = h @ w1 + b1
            a, g = jnp.split(h, 2, axis=-1)
            h = a * jax.nn.gelu(g, approximate=False)
            x = x + h @ w2 + b2
            return x
        key = jax.random.key(seed)
        ks = jax.random.split(key, 6)
        return {'x': jax.random.normal(ks[0], (B, N, DIM), jnp.float32), 'wqkv': jax.random.normal(ks[1], (DEPTH, DIM, 3 * INNER), jnp.float32) * 0.02, 'q_scale': jnp.ones((DEPTH, DIM_HEAD), jnp.float32), 'k_scale': jnp.ones((DEPTH, DIM_HEAD), jnp.float32), 'wo': jax.random.normal(ks[2], (DEPTH, INNER, DIM), jnp.float32) * 0.02, 'ln_g': jnp.ones((DEPTH, DIM), jnp.float32), 'ln_b': jnp.zeros((DEPTH, DIM), jnp.float32), 'w1': jax.random.normal(ks[3], (DEPTH, DIM, 2 * HID), jnp.float32) * 0.02, 'b1': jnp.zeros((DEPTH, 2 * HID), jnp.float32), 'w2': jax.random.normal(ks[4], (DEPTH, HID, DIM), jnp.float32) * 0.02, 'b2': jnp.zeros((DEPTH, DIM), jnp.float32)}
    _L1_ffn_in = _L1_ffn_setup()
    _d = {'L0_attn_x': _L0_attn_in['x'], 'L0_attn_W_k': _L0_attn_in['W_k'], 'L0_attn_W_v': _L0_attn_in['W_v'], 'L0_attn_W_o': _L0_attn_in['W_o'], 'L0_ffn_w1': _L0_ffn_in['w1'], 'L0_ffn_b1': _L0_ffn_in['b1'], 'L0_ffn_w2': _L0_ffn_in['w2'], 'L0_ffn_b2': _L0_ffn_in['b2'], 'L1_attn_ln_gamma': _L1_attn_in['ln_gamma'], 'L1_attn_ln_beta': _L1_attn_in['ln_beta'], 'L1_attn_w_qkv': _L1_attn_in['w_qkv'], 'L1_attn_w_out': _L1_attn_in['w_out'], 'L1_attn_b_out': _L1_attn_in['b_out'], 'L1_ffn_wqkv': _L1_ffn_in['wqkv'], 'L1_ffn_q_scale': _L1_ffn_in['q_scale'], 'L1_ffn_k_scale': _L1_ffn_in['k_scale'], 'L1_ffn_wo': _L1_ffn_in['wo'], 'L1_ffn_ln_g': _L1_ffn_in['ln_g'], 'L1_ffn_ln_b': _L1_ffn_in['ln_b'], 'L1_ffn_w1': _L1_ffn_in['w1'], 'L1_ffn_b1': _L1_ffn_in['b1'], 'L1_ffn_w2': _L1_ffn_in['w2'], 'L1_ffn_b2': _L1_ffn_in['b2']}
    _x0 = _d['L0_attn_x']
    _d['L0_attn_x'] = jax.random.normal(jax.random.fold_in(jax.random.key(seed), 1), (4, 1024, 128), dtype=_x0.dtype)
    del _x0
    return _d

def reference(L0_attn_x, L0_attn_W_k, L0_attn_W_v, L0_attn_W_o, L0_ffn_w1, L0_ffn_b1, L0_ffn_w2, L0_ffn_b2, L1_attn_ln_gamma, L1_attn_ln_beta, L1_attn_w_qkv, L1_attn_w_out, L1_attn_b_out, L1_ffn_wqkv, L1_ffn_q_scale, L1_ffn_k_scale, L1_ffn_wo, L1_ffn_ln_g, L1_ffn_ln_b, L1_ffn_w1, L1_ffn_b1, L1_ffn_w2, L1_ffn_b2):

    def _L0_attn_ref(x, W_k, W_v, W_o):
        import jax, jax.numpy as jnp
        import numpy as np
        NUM_HEADS = 16
        B, S, D = x.shape
        H = NUM_HEADS
        dk = D // H
        inv_sqrt_dk = 1.0 / jnp.sqrt(jnp.asarray(dk, dtype=x.dtype))
        Q = (x @ W_k.T).reshape(B, S, H, dk).transpose(0, 2, 1, 3)
        sq_norm = jnp.sum(Q * Q, axis=-1, keepdims=True)
        dot = jnp.einsum('bhsk,bhtk->bhst', Q, Q)
        squared_dist = sq_norm - 2.0 * dot + sq_norm.transpose(0, 1, 3, 2)
        scores = -squared_dist * inv_sqrt_dk
        attn = jax.nn.softmax(scores, axis=-1)
        context_q = jnp.einsum('bhst,bhtk->bhsk', attn, Q)
        Wq_h = W_k.reshape(H, dk, D)
        Wv_h = W_v.reshape(H, dk, D)
        merged = jnp.einsum('hkd,hvd->hkv', Wq_h, Wv_h)
        attn_out = jnp.einsum('bhsk,hkv->bhsv', context_q, merged) * inv_sqrt_dk
        attn_out = attn_out.transpose(0, 2, 1, 3).reshape(B, S, D)
        return attn_out @ W_o.T

    def _L0_ffn_ref(x, w1, b1, w2, b2):
        import jax, jax.numpy as jnp
        import numpy as np
        N_EMBD = 128
        N_STATE = 512
        h = jax.nn.gelu(jnp.einsum('bse,eh->bsh', x, w1) + b1, approximate=False)
        return jnp.einsum('bsh,he->bse', h, w2) + b2

    def _L1_attn_ref(x, ln_gamma, ln_beta, w_qkv, w_out, b_out):
        import jax, jax.numpy as jnp
        import numpy as np
        DIM = 128
        HEADS = 16
        DIM_HEAD = 64
        INNER = HEADS * DIM_HEAD

        def _attention(x, ln_gamma, ln_beta, w_qkv, w_out, b_out):
            b, n, _ = x.shape
            scale = DIM_HEAD ** (-0.5)
            mu = jnp.mean(x, axis=-1, keepdims=True)
            var = jnp.var(x, axis=-1, keepdims=True)
            xn = (x - mu) / jnp.sqrt(var + 1e-05) * ln_gamma + ln_beta
            qkv = jnp.einsum('bnd,ed->bne', xn, w_qkv)
            q, k, v = jnp.split(qkv, 3, axis=-1)
            reshape = lambda t: t.reshape(b, n, HEADS, DIM_HEAD).transpose(0, 2, 1, 3)
            q, k, v = (reshape(q) * scale, reshape(k), reshape(v))
            sim = jnp.einsum('bhid,bhjd->bhij', q, k)
            mask_value = -jnp.finfo(sim.dtype).max
            causal = jnp.triu(jnp.ones((n, n), dtype=bool), k=1)
            sim = jnp.where(causal, mask_value, sim)
            sim = sim - jax.lax.stop_gradient(jnp.max(sim, axis=-1, keepdims=True))
            attn = jax.nn.softmax(sim, axis=-1)
            out = jnp.einsum('bhij,bhjd->bhid', attn, v)
            out = out.transpose(0, 2, 1, 3).reshape(b, n, INNER)
            return jnp.einsum('bne,de->bnd', out, w_out) + b_out
        return _attention(x, ln_gamma, ln_beta, w_qkv, w_out, b_out)

    def _L1_ffn_ref(x, wqkv, q_scale, k_scale, wo, ln_g, ln_b, w1, b1, w2, b2):
        import jax, jax.numpy as jnp
        import numpy as np
        DIM = 128
        DEPTH = 2
        HEADS = 8
        DIM_HEAD = 64
        WINDOW = 64
        INNER = HEADS * DIM_HEAD
        HID = int(DIM * 4 * 2 / 3)
        B, N = (2, 1024)
        QK_SCALE = 8.0

        def shift_token(t):
            t1, t2 = jnp.split(t, 2, axis=-1)
            t2 = jnp.pad(t2, ((0, 0), (1, 0), (0, 0)))[:, :-1]
            return jnp.concatenate([t1, t2], axis=-1)

        def l2norm(t):
            return t / jnp.clip(jnp.linalg.norm(t, axis=-1, keepdims=True), 1e-12)

        def rotate_half(x):
            x1, x2 = jnp.split(x, 2, axis=-1)
            return jnp.concatenate([-x2, x1], axis=-1)

        def rotary_xpos(q, k):
            n = q.shape[-2]
            half_idx = jnp.arange(0, DIM_HEAD, 2, dtype=jnp.float32)
            inv_freq = 1.0 / 10000.0 ** (half_idx / DIM_HEAD)
            t = jnp.arange(n, dtype=jnp.float32)
            freqs = t[:, None] * inv_freq[None, :]
            freqs = jnp.concatenate([freqs, freqs], axis=-1)
            base = (half_idx + 0.4 * DIM_HEAD) / (1.4 * DIM_HEAD)
            power = (t - n // 2) / float(WINDOW // 2)
            scale = base[None, :] ** power[:, None]
            scale = jnp.concatenate([scale, scale], axis=-1)
            cos, sin = (jnp.cos(freqs), jnp.sin(freqs))
            q = q * cos * scale + rotate_half(q) * sin * scale
            k = k * cos / scale + rotate_half(k) * sin / scale
            return (q, k)

        def local_attention(q, k, v):
            b, h, n, d = q.shape
            w = n // WINDOW
            bq = q.reshape(b, h, w, WINDOW, d) * QK_SCALE
            bk = k.reshape(b, h, w, WINDOW, d)
            bv = v.reshape(b, h, w, WINDOW, d)

            def look_around(t):
                p = jnp.pad(t, ((0, 0), (0, 0), (1, 0), (0, 0), (0, 0)))
                return jnp.concatenate([p[:, :, :w], p[:, :, 1:]], axis=3)
            bk, bv = (look_around(bk), look_around(bv))
            bt = jnp.arange(n).reshape(w, WINDOW)
            btp = jnp.pad(bt, ((1, 0), (0, 0)), constant_values=-1)
            btk = jnp.concatenate([btp[:w], btp[1:]], axis=1)
            sim = jnp.einsum('bhwid,bhwjd->bhwij', bq, bk)
            i = bt[:, :, None]
            j = btk[:, None, :]
            mask = (i < j) | (i > j + WINDOW) | (j == -1)
            sim = jnp.where(mask, -jnp.finfo(sim.dtype).max, sim)
            attn = jax.nn.softmax(sim, axis=-1)
            out = jnp.einsum('bhwij,bhwjd->bhwid', attn, bv)
            return out.reshape(b, h, n, d)

        def _layer(x, wqkv, qs, ksc, wo, lg, lb, w1, b1, w2, b2):
            b, n, _ = x.shape
            h = shift_token(x)
            qkv = h @ wqkv
            q, k, v = jnp.split(qkv, 3, axis=-1)
            to_heads = lambda t: t.reshape(b, n, HEADS, DIM_HEAD).transpose(0, 2, 1, 3)
            q, k, v = (to_heads(q), to_heads(k), to_heads(v))
            q = l2norm(q) * qs
            k = l2norm(k) * ksc
            q, k = rotary_xpos(q, k)
            o = local_attention(q, k, v)
            o = o.transpose(0, 2, 1, 3).reshape(b, n, INNER)
            x = x + o @ wo
            h = shift_token(x)
            mu = h.mean(-1, keepdims=True)
            var = h.var(-1, keepdims=True)
            h = (h - mu) / jnp.sqrt(var + 1e-05) * lg + lb
            h = h @ w1 + b1
            a, g = jnp.split(h, 2, axis=-1)
            h = a * jax.nn.gelu(g, approximate=False)
            x = x + h @ w2 + b2
            return x
        for l in range(DEPTH):
            x = _layer(x, wqkv[l], q_scale[l], k_scale[l], wo[l], ln_g[l], ln_b[l], w1[l], b1[l], w2[l], b2[l])
        return x
    x = L0_attn_x
    x = x + 0.5 * _L0_ffn_ref(_layernorm(x, axis=-1), L0_ffn_w1, L0_ffn_b1, L0_ffn_w2, L0_ffn_b2)
    x = x + _L0_attn_ref(_layernorm(x, axis=-1), L0_attn_W_k, L0_attn_W_v, L0_attn_W_o)
    x = x + 0.5 * _L0_ffn_ref(_layernorm(x, axis=-1), L0_ffn_w1, L0_ffn_b1, L0_ffn_w2, L0_ffn_b2)
    x = x + 0.5 * _L1_ffn_ref(_layernorm(x, axis=-1), L1_ffn_wqkv, L1_ffn_q_scale, L1_ffn_k_scale, L1_ffn_wo, L1_ffn_ln_g, L1_ffn_ln_b, L1_ffn_w1, L1_ffn_b1, L1_ffn_w2, L1_ffn_b2)
    x = x + _L1_attn_ref(_layernorm(x, axis=-1), L1_attn_ln_gamma, L1_attn_ln_beta, L1_attn_w_qkv, L1_attn_w_out, L1_attn_b_out)
    x = x + 0.5 * _L1_ffn_ref(_layernorm(x, axis=-1), L1_ffn_wqkv, L1_ffn_q_scale, L1_ffn_k_scale, L1_ffn_wo, L1_ffn_ln_g, L1_ffn_ln_b, L1_ffn_w1, L1_ffn_b1, L1_ffn_w2, L1_ffn_b2)
    return x

_drawn_inputs = setup_inputs


def setup_inputs(seed=0):
    import zlib

    import numpy as np

    out = dict(_drawn_inputs(seed))
    spreads = {'L1_attn_ln_gamma': (1.0, 0.6),
     'L1_attn_ln_beta': (0.0, 0.563),
     'L1_ffn_q_scale': (1.0, 0.6),
     'L1_ffn_k_scale': (1.0, 0.6),
     'L1_ffn_ln_g': (1.0, 0.6),
     'L1_ffn_ln_b': (0.0, 0.8),
     'L1_ffn_b1': (0.0, 0.8),
     'L1_ffn_b2': (0.0, 0.415)}
    factors = {'L0_ffn_b1': 4.787,
     'L0_ffn_b2': 2.768,
     'L1_attn_b_out': 22.033,
     'L1_ffn_w1': 6.399,
     'L1_ffn_w2': 6.32}
    for name, (base, spread) in spreads.items():
        noise = np.random.default_rng([zlib.crc32(name.encode()), seed]).standard_normal(out[name].shape)
        drawn = base * np.exp(spread * noise) if base else spread * noise
        out[name] = jnp.asarray(drawn.astype(out[name].dtype))
    for name, factor in factors.items():
        out[name] = (out[name] * factor).astype(out[name].dtype)
    return out
```

```python
from contextlib import ExitStack

import concourse.bass as bass
from concourse import mybir
import numpy as np

F32 = mybir.dt.float32
F32R = mybir.dt.float32r
BF16 = mybir.dt.bfloat16
ALU = mybir.AluOpType
ACT = mybir.ActivationFunctionType
AX = mybir.AxisListType

P = 128
B, S = 4, 1024
TPB = S // P
NT = B * TPB
EPS = 1e-5
BIG = -1e30


class Ctx:
    pass


def semaphores(nc, stack, first=100):
    made = []

    def sem(name):
        made.append(stack.enter_context(nc.semaphore(name, num=first + len(made))))
        return made[-1]

    def clear():
        nc.all_engine_barrier(sems_to_clear=range(first, first + len(made)))
    return sem, clear


def row_statistics(nc, c, twice=False):
    with ExitStack() as st:
        sem, clear = semaphores(nc, st, first=200)
        stats_ready = sem("stats_ready")
        moments_ready = sem("moments_ready")
        deviation_ready = sem("deviation_ready")
        rstd_ready = sem("rstd_ready")
        with nc.Block() as block:
            @block.vector
            def _(dve):
                for t in range(NT):
                    dve.bn_stats(c.stats[:, t, :], c.X[:, t, :]).then_inc(stats_ready, 1)
                for t in range(NT):
                    dve.wait_ge(stats_ready, t + 1)
                    dve.bn_aggr(c.moments[:, t, :], c.stats[:, t, :]).then_inc(moments_ready, 1)
                dve.wait_ge(deviation_ready, 1)
                dve.reciprocal(c.rstd[:], c.deviation[:]).then_inc(rstd_ready, 1)
                if twice:
                    dve.wait_ge(rstd_ready, 1)
                    dve.tensor_tensor(c.second[:], c.moments[:, :, 1], c.rstd[:], ALU.mult).then_inc(rstd_ready, 1)
                    dve.wait_ge(rstd_ready, 2)
                    dve.tensor_tensor(c.second[:], c.second[:], c.rstd[:], ALU.mult).then_inc(rstd_ready, 1)
                    dve.wait_ge(deviation_ready, 2)
                    dve.reciprocal(c.second[:], c.deviation[:]).then_inc(rstd_ready, 1)
                    dve.wait_ge(rstd_ready, 4)
                    dve.tensor_tensor(c.rstd[:], c.rstd[:], c.second[:], ALU.mult).then_inc(rstd_ready, 1)

            @block.scalar
            def _(act):
                act.preload_act_table(ACT.Sqrt)
                act.wait_ge(moments_ready, NT)
                act.activation(c.deviation[:], c.moments[:, :, 1], ACT.Sqrt, bias=c.eps[:]).then_inc(deviation_ready, 1)
                if twice:
                    act.wait_ge(rstd_ready, 3)
                    act.activation(c.deviation[:], c.second[:], ACT.Sqrt, bias=c.eps[:]).then_inc(deviation_ready, 1)
        clear()


def normalise(dve, c, t, dst):
    return dve.tensor_scalar(dst, c.X[:, t, :], c.moments[:, t, 0:1], c.rstd[:, bass.ds(t, 1)], ALU.subtract, ALU.mult)


def gelu_ffn(nc, c, w1_d, b1_d, w2_d, b2_d):
    HID = 512
    CH = HID // P
    G = 4
    W = G * P
    STEPS = NT // G
    with ExitStack() as st:
        def sb(name, shape, dt=F32):
            return st.enter_context(nc.sbuf_tensor(c.fresh(name), shape, dt))

        w1 = sb("w1", [P, HID])
        b1 = sb("b1", [P, CH])
        w2 = sb("w2", [P, CH, P])
        half_b2 = sb("half_b2", [P, P])
        xn = sb("xn", [P, G, P])
        xnT = sb("xnT", [P, W])
        hid = sb("hid", [P, CH, W])
        x_b2 = sb("x_b2", [P, G, P])
        tr, up0, up1, down = c.slots
        sem, clear = semaphores(nc, st)
        weights = sem("weights")
        half_b2_ready = sem("half_b2_ready")
        xn_ready = sem("xn_ready")
        tr_ready = sem("tr_ready")
        xnT_ready = sem("xnT_ready")
        up_ready = sem("up_ready")
        hid_ready = sem("hid_ready")
        down_ready = sem("down_ready")
        x_b2_ready = sem("x_b2_ready")
        x_ready = sem("x_ready")

        row_statistics(nc, c)
        with nc.Block() as block:
            @block.sync
            def _(sp):
                sp.dma_start(w1[:], w1_d).then_inc(weights, 16)
                sp.dma_start(b1[:], b1_d).then_inc(weights, 16)
                sp.dma_start(w2[:], w2_d.rearrange("(c p) e -> p c e", p=P)).then_inc(weights, 16)
                sp.dma_start(half_b2[:], b2_d).then_inc(weights, 16)

            @block.gpsimd
            def _(pool):
                pool.wait_ge(weights, 64)
                pool.tensor_scalar(half_b2[:], half_b2[:], 0.5, None, ALU.mult).then_inc(half_b2_ready, 1)
                pool.wait_ge(half_b2_ready, 1)
                bias = half_b2[:].rearrange("p (g e) -> p g e", g=1).broadcast_to([P, G, P])
                with pool.Fori(0, STEPS) as i:
                    pool.wait_ge(x_ready, i + 1)
                    pool.tensor_tensor(x_b2[:], c.X[:, bass.ds(i * G, G), :], bias, ALU.add).then_inc(x_b2_ready, 1)

            @block.vector
            def _(dve):
                def norm(i):
                    for j in range(G):
                        normalise(dve, c, i * G + j, xn[:, j, :]).then_inc(xn_ready, 1)

                def step(i, more):
                    dve.wait_ge(tr_ready, i + 1)
                    dve.tensor_copy(xnT[:], tr[:, 0, :]).then_inc(xnT_ready, 1)
                    if more:
                        norm(i + 1)
                    dve.wait_ge(down_ready, i + 1)
                    dve.wait_ge(x_b2_ready, i + 1)
                    dve.scalar_tensor_tensor(c.X[:, bass.ds(i * G, G), :].rearrange("p g e -> p (g e)"), down[:, 0, :], 0.5,
                                             x_b2[:].rearrange("p g e -> p (g e)"),
                                             ALU.mult, ALU.add).then_inc(x_ready, 1)

                dve.sem_inc(x_ready, 1)
                norm(0)
                with dve.Fori(0, STEPS - 1) as i:
                    step(i, True)
                step(STEPS - 1, False)

            @block.tensor
            def _(pe):
                pe.wait_ge(weights, 64)
                with pe.Fori(0, STEPS) as i:
                    pe.wait_ge(xn_ready, i * G + G)
                    for j in range(G):
                        m = pe.transpose(tr[:, 0, j * P:(j + 1) * P], xn[:, j, :], c.ident[:])
                    m.then_inc(tr_ready, 1)
                    pe.wait_ge(xnT_ready, i + 1)
                    for k in range(CH):
                        up = (up0, up1)[k // 2]
                        pe.wait_ge(hid_ready, i * CH + k + 1)
                        pe.matmul(up[:, k % 2, :], w1[:, k * P:(k + 1) * P], xnT[:],
                                  start=True, stop=True).then_inc(up_ready, 1)
                    pe.wait_ge(x_ready, i + 1)
                    for j in range(G):
                        for k in range(CH):
                            if j == 0:
                                pe.wait_ge(hid_ready, i * CH + CH + k + 1)
                            m = pe.matmul(down[:, 0, j * P:(j + 1) * P], hid[:, k, j * P:(j + 1) * P],
                                          w2[:, k, :], start=(k == 0), stop=(k == CH - 1))
                    m.then_inc(down_ready, 1)

            @block.scalar
            def _(act):
                act.wait_ge(weights, 64)
                act.sem_inc(hid_ready, CH)
                act.preload_act_table(ACT.Gelu)
                with act.Fori(0, STEPS) as i:
                    for k in range(CH):
                        up = (up0, up1)[k // 2]
                        act.wait_ge(up_ready, i * CH + k + 1)
                        act.activation(hid[:, k, :], up[:, k % 2, :], ACT.Gelu,
                                       bias=b1[:, k:k + 1]).then_inc(hid_ready, 1)
        clear()


def distance_attention(nc, c, wk_d, wv_d, wo_d, rep_d, sel_d, masks_d):
    HEADS, D = 16, 8
    SCALE = float(np.float32(1) / np.sqrt(np.float32(D)))
    GROUP = 4
    UNITS = B * HEADS // GROUP
    JOBS = TPB * GROUP
    PV_LAG = 6
    with ExitStack() as st:
        def sb(name, shape, dt=F32):
            return st.enter_context(nc.sbuf_tensor(c.fresh(name), shape, dt))

        wk = sb("wk", [P, P])
        wo_eff = sb("w_eff", [P, P])
        xT = sb("xT", [P, NT * P])
        sqT = sb("sqT", [P, NT * P])
        q_all = sb("q_all", [P, NT, HEADS, D])
        bias_all = sb("bias_all", [P, NT, HEADS])
        rep = [sb(f"rep{k}", [P, 2, P]) for k in range(2)]
        sel = [sb(f"sel{k}", [P, 2, P]) for k in range(2)]
        masks = sb("masks", [P, 8])
        key_parts = sb("key_parts", [P, S], F32R)
        query = [[sb(f"query{k}{p}", [P, S], F32R) for p in range(2)] for k in range(2)]
        keys = [[sb(f"keys{k}{j}", [P, S], F32R) for j in range(GROUP)] for k in range(2)]
        v = [sb(f"v{k}", [P, TPB, GROUP, 32]) for k in range(2)]
        bias = [sb(f"bias{k}", [P, TPB, GROUP]) for k in range(2)]
        e = [sb(f"e{r}", [P, S]) for r in range(2 * GROUP)]
        oT = sb("oT", [P, S])
        inv = sb("inv", [P, TPB, GROUP])
        ctx_all = sb("ctx_all", [P, NT, P])
        flat = "p a n -> p (a n)"

        normalised_columns(nc, c, xT)

        with ExitStack() as st2:
            sem, clear = semaphores(nc, st2)
            loaded = sem("loaded")
            q_ready = sem("q_ready")
            q_out = sem("q_out")
            qT_ready = sem("qT_ready")
            sqT_ready = sem("sqT_ready")
            sq_ready = sem("sq_ready")
            norm_ready = sem("norm_ready")
            bias_ready = sem("bias_ready")
            cross_ready = sem("cross_ready")
            merged_ready = sem("merged_ready")
            eff_ready = sem("eff_ready")
            eff_out = sem("eff_out")
            v_clear = sem("v_clear")
            wv = st2.enter_context(nc.sbuf_tensor(c.fresh("wv"), [P, P], F32))
            wo = st2.enter_context(nc.sbuf_tensor(c.fresh("wo"), [P, P], F32))
            block_mask = st2.enter_context(nc.sbuf_tensor(c.fresh("block_mask"), [P, P], F32))
            merged = st2.enter_context(nc.sbuf_tensor(c.fresh("merged"), [P, P], F32))
            sq = e[0]
            with nc.Block() as block:
                @block.sync
                def _(sp):
                    sp.dma_start(wk[:], wk_d).then_inc(loaded, 16)
                    sp.dma_start(wv[:], wv_d).then_inc(loaded, 16)
                    sp.dma_start(wo[:], wo_d).then_inc(loaded, 16)
                    sp.dma_start(block_mask[:], c.const["block_mask"]).then_inc(loaded, 16)
                    sp.dma_start(masks[:], masks_d).then_inc(loaded, 16)
                    sp.wait_ge(loaded, 80)

                @block.gpsimd
                def _(pool):
                    for k in range(2):
                        pool.memset(v[k][:], 0.0).then_inc(v_clear, 1)
                    pool.wait_ge(v_clear, 2)
                    for k in range(2):
                        pool.memset(v[k][:, :, :, D:D + 1], 1.0).then_inc(v_clear, 1)

                @block.tensor
                def _(pe):
                    pe.wait_ge(loaded, 80)
                    pe.matmul(c.slots[2][:, 0, 0:P], wv[:], wk[:], start=True, stop=True).then_inc(cross_ready, 1)
                    for b in range(B):
                        if b:
                            pe.wait_ge(q_out, b)
                        for t in range(TPB):
                            m = pe.matmul(c.slots[0][:, t // 4, (t % 4) * P:(t % 4 + 1) * P],
                                          xT[:, (b * TPB + t) * P:(b * TPB + t + 1) * P], wk[:], start=True, stop=True)
                        m.then_inc(q_ready, 1)
                        if b:
                            pe.wait_ge(sqT_ready, b)
                        for half in range(2):
                            m = pe.matmul(c.slots[1][:, half, :], wk[:], xT[:, b * S + half * 512:b * S + half * 512 + 512],
                                          start=True, stop=True)
                        m.then_inc(qT_ready, 1)
                        if b == 0:
                            pe.wait_ge(merged_ready, 1)
                            pe.matmul(c.slots[3][:, 0, 0:P], merged[:], wo[:], start=True, stop=True).then_inc(eff_ready, 1)

                @block.scalar
                def _(act):
                    for b in range(B):
                        act.wait_ge(q_ready, b + 1)
                        act.activation(q_all[:, b * TPB:(b + 1) * TPB, :, :].rearrange("p t h d -> p (t h d)"),
                                       c.slots[0][:].rearrange(flat), ACT.Copy).then_inc(q_out, 1)
                        act.wait_ge(qT_ready, b + 1)
                        act.activation(sqT[:, b * S:(b + 1) * S], c.slots[1][:].rearrange(flat), ACT.Square).then_inc(sqT_ready, 1)

                @block.vector
                def _(dve):
                    dve.wait_ge(cross_ready, 1)
                    dve.wait_ge(loaded, 80)
                    dve.scalar_tensor_tensor(merged[:], c.slots[2][:, 0, 0:P], SCALE, block_mask[:], ALU.mult, ALU.mult)\
                       .then_inc(merged_ready, 1)
                    dve.wait_ge(eff_ready, 1)
                    dve.tensor_copy(wo_eff[:], c.slots[3][:, 0, 0:P]).then_inc(eff_out, 1)
                    for b in range(B):
                        tiles = slice(b * TPB, (b + 1) * TPB)
                        rows = q_all[:, tiles, :, :].rearrange("p t h d -> p (t h d)")
                        dve.wait_ge(q_out, b + 1)
                        if b:
                            dve.wait_ge(norm_ready, b)
                        dve.tensor_tensor(sq[:], rows, rows, ALU.mult).then_inc(sq_ready, 1)
                        dve.wait_ge(sq_ready, b + 1)
                        dve.tensor_reduce(bias_all[:, tiles, :].rearrange("p t h -> p (t h)"),
                                          sq[:].rearrange("p (g d) -> p g d", d=D), AX.X, ALU.add).then_inc(norm_ready, 1)
                    dve.wait_ge(norm_ready, B)
                    dve.tensor_scalar(bias_all[:], bias_all[:], -SCALE, None, ALU.mult).then_inc(bias_ready, 1)
            clear()

        with ExitStack() as st2:
            sem, clear = semaphores(nc, st2)
            w_loaded = sem("w_loaded")
            p_ready = sem("p_ready")
            step_dve = sem("step_dve")
            p_out = sem("p_out")
            sides_ready = sem("sides_ready")
            v_ready = sem("v_ready")
            s_ready = sem("s_ready")
            e_ready = sem("e_ready")
            o_ready = sem("o_ready")
            o_out = sem("o_out")
            oT_ready = sem("oT_ready")
            inv_ready = sem("inv_ready")
            ctx_ready = sem("ctx_ready")

            with nc.Block() as block:
                @block.sync
                def _(sp):
                    def load(u, k):
                        sp.dma_start(rep[k][:], rep_d[bass.ds(u % 4, 1)].rearrange("a p c m -> (a p) c m")).then_inc(w_loaded, 16)
                        sp.dma_start(sel[k][:], sel_d[bass.ds(u % 4, 1)].rearrange("a p c m -> (a p) c m")).then_inc(w_loaded, 16)

                    load(0, 0)
                    with sp.Fori(0, UNITS // 2) as i:
                        for k in range(2):
                            sp.wait_ge(p_ready, 4 * i + 2 * k + 2)
                            load(2 * i + k + 1, 1 - k)

                @block.gpsimd
                def _(pool):
                    def rows(u, k, count):
                        tiles = bass.ds((u // 4 % B) * TPB, TPB)
                        pool.tensor_copy(v[k][:, :, :, 0:D], q_all[:, tiles, bass.ds(u % 4 * GROUP, GROUP), :]).then_inc(v_ready, 1)
                        pool.tensor_copy(bias[k][:], bias_all[:, tiles, bass.ds(u % 4 * GROUP, GROUP)]).then_inc(v_ready, 1)

                    rows(0, 0, 0)
                    with pool.Fori(0, UNITS // 2) as i:
                        for k in range(2):
                            pool.wait_ge(o_ready, 2 * i + k + 1)
                            rows(2 * i + k + 1, 1 - k, 0)

                @block.tensor
                def _(pe):
                    def sides(u, k, p):
                        if p == 0:
                            pe.wait_ge(w_loaded, 32 * u + 32)
                        pe.wait_ge(p_out, 2 * u + p + 1)
                        cols = (u // 4 % B) * S
                        for half in range(2):
                            pe.matmul(c.slots[2][:, half, :], rep[k][:, p, :], xT[:, bass.ds(cols + half * 512, 512)],
                                      start=True, stop=False)
                            m = pe.matmul(c.slots[2][:, half, :], sel[k][:, p, :], sqT[:, bass.ds(cols + half * 512, 512)],
                                          start=False, stop=True)
                        m.then_inc(p_ready, 1)

                    def scores(u, k, n):
                        t, j = n // GROUP, n % GROUP
                        if n in (0, 2):
                            pe.wait_ge(sides_ready, 2 * u + n // 2 + 2)
                        pe.wait_ge(e_ready, JOBS * u + n + 1)
                        for half in range(2):
                            m = pe.matmul(c.slots[n % 2][:, half, :], keys[k][j][:, t * P:(t + 1) * P],
                                          query[k][j // 2][:, half * 512:half * 512 + 512], start=True, stop=True)
                        m.then_inc(s_ready, 1)

                    def values(u, k, t):
                        pe.wait_ge(e_ready, JOBS * u + 2 + GROUP * t + GROUP)
                        if t == 0:
                            pe.wait_ge(v_ready, 2 * u + 2)
                            pe.wait_ge(ctx_ready, u + 1)
                        for half in range(2):
                            for j in range(GROUP):
                                m = pe.matmul(c.slots[3][32 * j:32 * j + 32, half, :], v[k][:, t, j, :],
                                              e[GROUP * (t % 2) + j][:, half * 512:half * 512 + 512],
                                              start=(t == 0), stop=(t == TPB - 1), skip_group_check=True)
                        if t == TPB - 1:
                            m.then_inc(o_ready, 1)

                    def turn(u):
                        pe.wait_ge(o_out, u + 1)
                        for t in range(TPB):
                            m = pe.transpose(c.slots[3][:, t // 4, (t % 4) * P:(t % 4 + 1) * P], oT[:, t * P:(t + 1) * P], c.ident[:])
                        m.then_inc(oT_ready, 1)

                    pe.sem_inc(o_ready, 1)
                    sides(0, 0, 0)
                    sides(0, 0, 1)
                    with pe.Fori(0, UNITS // 2) as i:
                        for k in range(2):
                            u = 2 * i + k
                            for n in range(JOBS):
                                scores(u, k, n)
                                if n >= PV_LAG and (n - PV_LAG) % GROUP == 0:
                                    values(u, k, (n - PV_LAG) // GROUP)
                                if n == 16:
                                    sides(u + 1, 1 - k, 0)
                            sides(u + 1, 1 - k, 1)
                            values(u, k, TPB - 1)
                            turn(u)

                @block.scalar
                def _(act):
                    act.sem_inc(e_ready, 2)
                    act.preload_act_table(ACT.Exp)
                    with act.Fori(0, UNITS // 2) as i:
                        for k in range(2):
                            u = 2 * i + k
                            act.wait_ge(v_ready, 2 * u + 2)
                            for n in range(JOBS):
                                t, j = n // GROUP, n % GROUP
                                act.wait_ge(s_ready, JOBS * u + n + 1)
                                act.activation(e[n % (2 * GROUP)][:], c.slots[n % 2][:].rearrange(flat), ACT.Exp,
                                               bias=bias[k][:, t, j:j + 1]).then_inc(e_ready, 1)

                @block.vector
                def _(dve):
                    OWN = 5

                    def sides(u, k, p):
                        slot = c.slots[2][:].rearrange(flat)
                        quarter = query[k][p]
                        own = OWN * (2 * u + p)
                        dve.wait_ge(p_ready, 2 * u + p + 1)
                        dve.wait_ge(sides_ready, 2 * u + p + 1)
                        dve.tensor_scalar(key_parts[:], slot, 2 * SCALE, None, ALU.mult).then_inc(step_dve, 1)
                        dve.tensor_scalar(quarter[:], slot, masks[:, 6:7], None, ALU.mult).then_inc(step_dve, 1)
                        dve.wait_ge(step_dve, own + 1)
                        dve.scalar_tensor_tensor(key_parts[64:P, :], slot[64:P, :], 2 * SCALE, key_parts[64:P, :].bitcast(F32),
                                                 ALU.mult, ALU.subtract).then_inc(step_dve, 1)
                        dve.wait_ge(step_dve, own + 2)
                        for r in (32, 96):
                            dve.scalar_tensor_tensor(quarter[r:r + 32, :], slot[r:r + 32, :], masks[r:r + 32, 6:7],
                                                     quarter[r:r + 32, :].bitcast(F32), ALU.mult, ALU.subtract)\
                               .then_inc(step_dve if r == 32 else p_out, 1)
                        dve.wait_ge(step_dve, own + 3)
                        for j in range(2):
                            m = dve.tensor_scalar(keys[k][2 * p + j][:], key_parts[:].bitcast(F32), masks[:, 2 * j:2 * j + 1],
                                                  masks[:, 2 * j + 1:2 * j + 2], ALU.mult, ALU.add)
                            m.then_inc(step_dve if j == 0 else sides_ready, 1)

                    dve.sem_inc(p_out, 1)
                    dve.sem_inc(ctx_ready, 1)
                    dve.sem_inc(sides_ready, 1)
                    sides(0, 0, 0)
                    sides(0, 0, 1)
                    with dve.Fori(0, UNITS // 2) as i:
                        for k in range(2):
                            u = 2 * i + k
                            sides(u + 1, 1 - k, 0)
                            sides(u + 1, 1 - k, 1)
                            dve.wait_ge(o_ready, u + 2)
                            dve.tensor_copy(oT[:], c.slots[3][:].rearrange(flat)).then_inc(o_out, 1)
                            dve.wait_ge(oT_ready, u + 1)
                            rows = c.slots[3][:].rearrange("p a (t j d) -> p (a t) j d", j=GROUP, d=32)
                            dve.reciprocal(inv[:], rows[:, :, :, D]).then_inc(inv_ready, 1)
                            dve.wait_ge(inv_ready, u + 1)
                            dst = ctx_all[:, bass.ds((u // 4) * TPB, TPB), bass.ds(u % 4 * 32, 32)]
                            dve.tensor_tensor(dst.rearrange("p t (j d) -> p t j d", d=D), rows[:, :, :, 0:D],
                                              inv[:].unsqueeze(3).broadcast_to([P, TPB, GROUP, D]), ALU.mult).then_inc(ctx_ready, 1)
            clear()

        with ExitStack() as st2:
            sem, clear = semaphores(nc, st2)
            turned = sem("turned")
            cT_ready = sem("cT_ready")
            y_ready = sem("y_ready")
            x_ready = sem("x_ready")
            cT = [oT[:, 512 * k:512 * k + 512] for k in range(2)]
            G = 4
            with nc.Block() as block:
                @block.tensor
                def _(pe):
                    for i in range(NT // G + 1):
                        if i < NT // G:
                            if i >= 2:
                                pe.wait_ge(cT_ready, i - 1)
                            for j in range(G):
                                m = pe.transpose(c.slots[i % 2][:, 0, j * P:(j + 1) * P], ctx_all[:, i * G + j, :], c.ident[:])
                            m.then_inc(turned, 1)
                        if i >= 1:
                            pe.wait_ge(cT_ready, i)
                            if i >= 3:
                                pe.wait_ge(x_ready, i - 2)
                            for j in range(G):
                                m = pe.matmul(c.slots[2 + (i - 1) % 2][:, 0, j * P:(j + 1) * P],
                                              cT[(i - 1) % 2][:, j * P:(j + 1) * P], wo_eff[:], start=True, stop=True)
                            m.then_inc(y_ready, 1)

                @block.scalar
                def _(act):
                    for i in range(NT // G):
                        act.wait_ge(turned, i + 1)
                        if i >= 2:
                            act.wait_ge(y_ready, i - 1)
                        act.activation(cT[i % 2], c.slots[i % 2][:, 0, :], ACT.Copy).then_inc(cT_ready, 1)

                @block.vector
                def _(dve):
                    for i in range(NT // G):
                        xs = c.X[:, i * G:(i + 1) * G, :].rearrange("p t d -> p (t d)")
                        dve.wait_ge(y_ready, i + 1)
                        dve.tensor_tensor(xs, c.slots[2 + i % 2][:, 0, :], xs, ALU.add).then_inc(x_ready, 1)
            clear()


def local_layers(nc, c, d):
    HEADS, D, WIN = 8, 64, 64
    PAIRS = HEADS // 2
    G = 4
    STEPS = NT // G
    W = G * P
    CH = 3
    JOBS = ["tq0", "tq1", "tq2", "tq3", "s0", "s1", "s2", "s3", "pt0", "pt1", "pt2", "pt3", "o0", "o1", "o2", "o3",
            "t1", "qk0", "v0", "t2", "qk1", "v1", "hc", "qk2", "v2", "t3", "qk3", "v3", "up0", "up1", "up2", "down"]
    flat = "p a n -> p (a n)"
    FIRST = 0

    def slot(job):
        return c.slots[JOBS.index(job) % 4]

    with ExitStack() as st:
        def sb(name, shape, dt=F32):
            return st.enter_context(nc.sbuf_tensor(c.fresh(name), shape, dt))

        H = sb("H", [P, NT, P])
        w_qk = sb("w_qk", [P, 2 * HEADS * D])
        w_v = sb("w_v", [P, HEADS * D])
        w_o = sb("w_o", [P, PAIRS, P])
        w1 = sb("w1", [P, 2, CH, P])
        w2 = sb("w2", [P, CH, P])
        small = sb("small", [P, 8])
        b2 = sb("b2", [P, P])
        scales = sb("scales", [P, 2, 2, D])
        angles = sb("angles", [P, TPB, 2, 2, D])
        tables = sb("tables", [P, TPB, 2, 2, D])
        centre = sb("centre", [P, P])
        flags = sb("flags", [P, 2])
        band = sb("band", [P, 2, 512], BF16)
        hs = sb("hs", [P, G, P])
        hT = sb("hT", [P, WIN + W + 1])
        sq = [sb(f"sq{k}", [P, 1024]) for k in range(2)]
        cosine = sb("cosine", [P, 1024])
        sine = sb("sine", [P, 1024])
        rot = sb("rot", [P, G, 2 * HEADS, D])
        norm2 = sb("norm2", [P, G, 2 * HEADS])
        norm = sb("norm", [P, G, 2 * HEADS])
        inv_norm = sb("inv_norm", [P, G, 2 * HEADS])
        v = sb("v", [P, G, 2, HEADS * D])
        qT = sb("qT", [P, G, PAIRS, P])
        kz = sb("kz", [P, PAIRS, 2, WIN + W])
        top = sb("top", [P, G, HEADS])
        prob = sb("prob", [P, G, HEADS, P])
        total = sb("total", [P, G, HEADS])
        inv_total = sb("inv_total", [P, G, HEADS])
        probT = sb("probT", [P, G, HEADS, P])
        attn = sb("attn", [P, G, HEADS * D])
        attnT = sb("attnT", [P, G, PAIRS, P])
        h1 = sb("h1", [P, G, P])
        h1_b2 = sb("h1_b2", [P, G, P])
        h1T = sb("h1T", [P, W + 1])
        dev2 = sb("dev2", [P, G])
        dev = sb("dev", [P, G])
        inv_dev = sb("inv_dev", [P, G])
        scrap = sb("scrap", [P, G, P])
        z = sb("z", [P, G, P])
        zT = sb("zT", [P, W])
        gate = [prob[:, k // 2, k % 2 * 4:k % 2 * 4 + 4, :].rearrange("p h k -> p (h k)") for k in range(CH)]
        hid = [prob[:, 2 + k // 2, k % 2 * 4:k % 2 * 4 + 4, :].rearrange("p h k -> p (h k)") for k in range(CH)]

        row_statistics(nc, c)
        with ExitStack() as st2:
            sem, clear = semaphores(nc, st2)
            h_ready = sem("h_ready")
            loaded = sem("loaded")
            zeroed = sem("zeroed")
            band_ready = sem("band_ready")
            with nc.Block() as block:
                @block.sync
                def _(sp):
                    sp.dma_start(angles[:], c.const["angles"]).then_inc(loaded, 16)
                    sp.dma_start(centre[:], c.const["centre"]).then_inc(loaded, 16)
                    sp.dma_start(flags[:], c.const["flags"]).then_inc(loaded, 16)
                    sp.dma_start(sq[0][:], c.const["band"].rearrange(flat)).then_inc(loaded, 16)

                @block.vector
                def _(dve):
                    dve.wait_ge(loaded, 64)
                    dve.tensor_copy(band[:].rearrange(flat), sq[0][:]).then_inc(band_ready, 1)
                    for t in range(NT):
                        normalise(dve, c, t, H[:, t, :]).then_inc(h_ready, 1)

                @block.gpsimd
                def _(pool):
                    pool.memset(hT[:], 0.0).then_inc(zeroed, 1)
                    pool.memset(kz[:], 0.0).then_inc(zeroed, 1)
                    pool.memset(h1T[:], 0.0).then_inc(zeroed, 1)
            clear()

        sem, clear = semaphores(nc, st)
        w_loaded = sem("w_loaded")
        tables_ready = sem("tables_ready")
        hs_ready = sem("hs_ready")
        hT_carried = sem("hT_carried")
        hT_edge = sem("hT_edge")
        t1_ready = sem("t1_ready")
        hT_low = sem("hT_low")
        hT_high = sem("hT_high")
        qk_ready = sem("qk_ready")
        sq_ready = sem("sq_ready")
        norm2_ready = sem("norm2_ready")
        turn_ready = sem("turn_ready")
        rot_ready = sem("rot_ready")
        v_ready = sem("v_ready")
        v_out = sem("v_out")
        norm_ready = sem("norm_ready")
        inv_step = sem("inv_step")
        unit_ready = sem("unit_ready")
        kz_carried = sem("kz_carried")
        tq_ready = sem("tq_ready")
        tq_act = sem("tq_act")
        tq_dve = sem("tq_dve")
        s_ready = sem("s_ready")
        top_ready = sem("top_ready")
        less_top = sem("less_top")
        exp_ready = sem("exp_ready")
        total_ready = sem("total_ready")
        inv_total_ready = sem("inv_total_ready")
        pt_ready = sem("pt_ready")
        probT_ready = sem("probT_ready")
        o_ready = sem("o_ready")
        attn_ready = sem("attn_ready")
        ot_ready = sem("ot_ready")
        attnT_ready = sem("attnT_ready")
        y_ready = sem("y_ready")
        h1_ready = sem("h1_ready")
        h1_b2_ready = sem("h1_b2_ready")
        t2_ready = sem("t2_ready")
        h1T_edge = sem("h1T_edge")
        h1T_low = sem("h1T_low")
        h1T_high = sem("h1T_high")
        hc_ready = sem("hc_ready")
        dev2_ready = sem("dev2_ready")
        dev_ready = sem("dev_ready")
        inv_dev_ready = sem("inv_dev_ready")
        z_ready = sem("z_ready")
        t3_ready = sem("t3_ready")
        zT_ready = sem("zT_ready")
        up_ready = sem("up_ready")
        gate_ready = sem("gate_ready")
        hid_ready = sem("hid_ready")
        down_ready = sem("down_ready")
        layer_out = sem("layer_out")

        def layer(depth):
            with nc.Block() as block:
                @block.sync
                def _(sp):
                    at = bass.ds(depth, 1)
                    sp.dma_start(w_qk[:], d["w_qk"][at].rearrange("a p n -> (a p) n")).then_inc(w_loaded, 16)
                    sp.dma_start(w_v[:], d["w_v"][at].rearrange("a p n -> (a p) n")).then_inc(w_loaded, 16)
                    sp.dma_start(scales[:], d["scales"][at].rearrange("a p x y n -> (a p) x y n")).then_inc(w_loaded, 16)
                    sp.dma_start(w_o[:], d["w_o"][at].rearrange("a p c n -> (a p) c n")).then_inc(w_loaded, 16)
                    sp.dma_start(w1[:], d["w1"][at].rearrange("a p g c n -> (a p) g c n")).then_inc(w_loaded, 16)
                    sp.dma_start(w2[:], d["w2"][at].rearrange("a p c n -> (a p) c n")).then_inc(w_loaded, 16)
                    sp.dma_start(small[:], d["small"][at].rearrange("a p n -> (a p) n")).then_inc(w_loaded, 16)
                    sp.dma_start(b2[:], d["b2"][at].rearrange("a p n -> (a p) n")).then_inc(w_loaded, 16)

                @block.gpsimd
                def _(pool):
                    def before_projections(u):
                        if u is not FIRST:
                            pool.wait_ge(t1_ready, u)
                        pool.tensor_copy(hs[:], H[:, bass.ds(u % STEPS * G, G), :]).then_inc(hs_ready, 1)
                        if u is not FIRST:
                            pool.wait_ge(v_ready, G * u)
                        pool.tensor_tensor(hT[:, WIN:WIN + 1], hT[:, WIN + W:WIN + W + 1],
                                           flags[:, bass.ds(u % 2, 1)], ALU.mult).then_inc(hT_edge, 1)

                    before_projections(FIRST)
                    pool.wait_ge(w_loaded, 128)
                    with pool.Fori(0, STEPS) as i:
                        before_projections(i + 1)
                        pool.wait_ge(h1_ready, G * i + G)
                        pool.wait_ge(layer_out, i + 1)
                        pool.tensor_tensor(h1_b2[:], h1[:], b2[:].unsqueeze(1).broadcast_to([P, G, P]),
                                           ALU.add).then_inc(h1_b2_ready, 1)

                @block.tensor
                def _(pe):
                    def t1(u):
                        pe.wait_ge(hs_ready, u + 1)
                        if u is not FIRST:
                            pe.wait_ge(h1_ready, G * u - 3)
                        for j in range(G):
                            m = pe.transpose(slot("t1")[:, 0, j * P:(j + 1) * P], hs[:, j, :], c.ident[:])
                        m.then_inc(t1_ready, 1)

                    def qkv(u, j):
                        job = f"qk{j}"
                        if j == 0:
                            pe.wait_ge(hT_low, u + 1)
                            pe.wait_ge(hT_high, u + 1)
                            if u is not FIRST:
                                pe.wait_ge(h1_ready, G * u - 2)
                        if j == 3 and u is FIRST:
                            pe.wait_ge(v_out, 1)
                        own = hT[:, WIN + j * P:WIN + (j + 1) * P]
                        for half in range(2):
                            m = pe.matmul(slot(job)[:, half, :], own, w_qk[:, half * 512:half * 512 + 512], start=True, stop=True)
                        m.then_inc(qk_ready, 1)
                        job = f"v{j}"
                        if j == 0 and u is not FIRST:
                            pe.wait_ge(h1_ready, G * u - 1)
                        if j > 0:
                            pe.wait_ge(turn_ready, 3 * (G * u + j))
                        pe.matmul(slot(job)[:, 0, :], hT[:, j * P:j * P + P], w_v[:], start=True, stop=True)
                        pe.matmul(slot(job)[:, 1, :], own, w_v[:], start=True, stop=True).then_inc(v_ready, 1)

                    def attention(i):
                        for j in range(G):
                            job = f"tq{j}"
                            pe.wait_ge(unit_ready, G * i + j + 1)
                            if j == 0:
                                pe.wait_ge(v_out, G * i + G)
                            if j < CH:
                                pe.wait_ge(hid_ready, CH * i + j + 1)
                            else:
                                pe.wait_ge(layer_out, i + 1)
                            for s in range(2 * PAIRS):
                                m = pe.transpose(slot(job)[:, s // PAIRS, (s % PAIRS) * P:(s % PAIRS + 1) * P],
                                                 rot[:, j, 2 * s:2 * s + 2, :].rearrange("p h d -> p (h d)"), c.ident[:])
                            m.then_inc(tq_ready, 1)
                        for j in range(G):
                            job = f"s{j}"
                            pe.wait_ge(tq_act, 2 * (G * i + j) + 2)
                            pe.wait_ge(tq_dve, G * i + j + 1)
                            for bank in range(2):
                                mask = band[:, 1, :] if j else band[:, bass.ds(i % 2, 1), :].rearrange("p a n -> p (a n)")
                                pe.matmul(slot(job)[:, bank, :], c.ident_bf[:], mask, start=True, stop=False,
                                          skip_group_check=True)
                                for p in range(2 * bank, 2 * bank + 2):
                                    for a in range(2):
                                        at = (2 * j + a) * WIN
                                        m = pe.matmul(slot(job)[64 * a:64 * a + 64, bank, (p % 2) * 256:(p % 2) * 256 + 256],
                                                      qT[:, j, p, 64 * a:64 * a + 64], kz[:, p, :, at:at + 2 * WIN],
                                                      start=False, stop=True, skip_group_check=True)
                            m.then_inc(s_ready, 1)
                        for j in range(G):
                            job = f"pt{j}"
                            pe.wait_ge(exp_ready, G * i + j + 1)
                            for h in range(HEADS):
                                m = pe.transpose(slot(job)[:, h // 4, (h % 4) * P:(h % 4 + 1) * P], prob[:, j, h, :], c.ident[:])
                            m.then_inc(pt_ready, 1)
                        for j in range(G):
                            job = f"o{j}"
                            pe.wait_ge(probT_ready, G * i + j + 1)
                            for h in range(HEADS):
                                for a in range(2):
                                    m = pe.matmul(slot(job)[64 * a:64 * a + 64, 0, h * D:(h + 1) * D],
                                                  probT[:, j, h, 64 * a:64 * a + 64], v[:, j, a, h * D:(h + 1) * D],
                                                  start=True, stop=True, skip_group_check=True)
                            m.then_inc(o_ready, 1)
                        for j in range(G):
                            pe.wait_ge(attn_ready, G * i + j + 1)
                            for s in range(PAIRS):
                                m = pe.transpose(slot(f"o{j}")[:, 1, s * P:(s + 1) * P], attn[:, j, s * P:(s + 1) * P], c.ident[:])
                            m.then_inc(ot_ready, 1)
                        for j in range(G):
                            pe.wait_ge(attnT_ready, G * i + j + 1)
                            for s in range(PAIRS):
                                m = pe.matmul(slot(f"o{j}")[:, 0, 0:P], attnT[:, j, s, :], w_o[:, s, :],
                                              start=(s == 0), stop=(s == PAIRS - 1))
                            m.then_inc(y_ready, 1)

                    def t2(i):
                        pe.wait_ge(h1_ready, G * i + G)
                        for j in range(G):
                            m = pe.transpose(slot("t2")[:, 0, j * P:(j + 1) * P], h1[:, j, :], c.ident[:])
                        m.then_inc(t2_ready, 1)

                    def centred(i):
                        pe.wait_ge(h1T_low, i + 1)
                        pe.wait_ge(h1T_high, i + 1)
                        pe.wait_ge(v_out, G * (i + 1) + 1)
                        for j in range(G):
                            m = pe.matmul(slot("hc")[:, 0, j * P:(j + 1) * P], h1T[:, j * P:(j + 1) * P], centre[:],
                                          start=True, stop=True)
                        m.then_inc(hc_ready, 1)

                    def t3(i):
                        pe.wait_ge(z_ready, G * i + G)
                        pe.wait_ge(v_out, G * (i + 1) + 2)
                        for j in range(G):
                            m = pe.transpose(slot("t3")[:, 0, j * P:(j + 1) * P], z[:, j, :], c.ident[:])
                        m.then_inc(t3_ready, 1)

                    def up_down(i):
                        for k in range(CH):
                            job = f"up{k}"
                            if k == 0:
                                pe.wait_ge(zT_ready, i + 1)
                                pe.wait_ge(v_out, G * (i + 1) + 3)
                            if k == 2:
                                pe.wait_ge(turn_ready, 3 * G * (i + 2))
                            for g in (1, 0):
                                m = pe.matmul(slot(job)[:, g, :], w1[:, g, k, :], zT[:], start=True, stop=True)
                            m.then_inc(up_ready, 1)
                        pe.wait_ge(v_out, G * (i + 1) + 4)
                        pe.wait_ge(hid_ready, CH * i + 2 * CH)
                        for j in range(G):
                            for k in range(CH):
                                m = pe.matmul(slot("down")[:, 0, j * P:(j + 1) * P], hid[k][:, j * P:(j + 1) * P], w2[:, k, :],
                                              start=(k == 0), stop=(k == CH - 1))
                        m.then_inc(down_ready, 1)

                    pe.sem_inc(s_ready, 1)
                    pe.wait_ge(w_loaded, 128)
                    t1(FIRST)
                    for j in range(G):
                        qkv(FIRST, j)
                    with pe.Fori(0, STEPS) as i:
                        attention(i)
                        t1(i + 1)
                        qkv(i + 1, 0)
                        t2(i)
                        qkv(i + 1, 1)
                        centred(i)
                        qkv(i + 1, 2)
                        t3(i)
                        qkv(i + 1, 3)
                        up_down(i)

                @block.scalar
                def _(act):
                    def t1(u):
                        if u is not FIRST:
                            act.wait_ge(v_ready, G * u)
                        act.activation(hT[:, 0:WIN], hT[:, W:W + WIN], ACT.Copy).then_inc(hT_carried, 1)
                        act.wait_ge(t1_ready, u + 1)
                        act.wait_ge(hT_carried, u + 1)
                        act.wait_ge(hT_edge, u + 1)
                        act.activation(hT[0:64, WIN:WIN + W], slot("t1")[0:64, 0, :], ACT.Copy).then_inc(hT_low, 1)

                    def qkv(u, j):
                        act.wait_ge(qk_ready, G * u + j + 1)
                        act.wait_ge(norm2_ready, G * u + j + 1)
                        act.activation(sq[j % 2][:], slot(f"qk{j}")[:].rearrange(flat), ACT.Square).then_inc(sq_ready, 1)
                        act.wait_ge(v_ready, G * u + j + 1)
                        act.activation(v[:, j, :, :].rearrange(flat), slot(f"v{j}")[:].rearrange(flat), ACT.Copy).then_inc(v_out, 1)

                    def norms(u):
                        act.wait_ge(norm2_ready, G * u + G + 2)
                        act.activation(norm[:], norm2[:], ACT.Sqrt).then_inc(norm_ready, 1)

                    def attention(i):
                        act.wait_ge(s_ready, G * i + 1)
                        act.activation(kz[:, :, :, 0:WIN], kz[:, :, :, W:W + WIN], ACT.Copy).then_inc(kz_carried, 1)
                        for j in range(G):
                            act.wait_ge(tq_ready, G * i + j + 1)
                            if j == 0:
                                act.wait_ge(kz_carried, i + 1)
                            at = WIN + j * P
                            act.activation(qT[:, j, :, :].rearrange(flat), slot(f"tq{j}")[:, 0, :], ACT.Copy).then_inc(tq_act, 1)
                            act.activation(kz[0:64, :, 0, at:at + P], slot(f"tq{j}")[0:64, 1, :].rearrange("p (s t) -> p s t", t=P),
                                           ACT.Copy).then_inc(tq_act, 1)
                        for j in range(G):
                            act.wait_ge(less_top, G * i + j + 1)
                            rows = prob[:, j, :, :].rearrange(flat)
                            act.activation(rows, rows, ACT.Exp).then_inc(exp_ready, 1)
                        for j in range(G):
                            act.wait_ge(pt_ready, G * i + j + 1)
                            act.activation(probT[:, j, :, :].rearrange(flat), slot(f"pt{j}")[:].rearrange(flat),
                                           ACT.Copy).then_inc(probT_ready, 1)
                        for j in range(G):
                            act.wait_ge(ot_ready, G * i + j + 1)
                            act.activation(attnT[:, j, :, :].rearrange(flat), slot(f"o{j}")[:, 1, :], ACT.Copy).then_inc(attnT_ready, 1)

                    def t2(i):
                        act.wait_ge(t2_ready, i + 1)
                        act.activation(h1T[0:64, 0:W], slot("t2")[0:64, 0, :], ACT.Copy).then_inc(h1T_low, 1)

                    def deviation(i):
                        act.wait_ge(hc_ready, i + 1)
                        act.wait_ge(inv_dev_ready, i + 1)
                        for j in range(G):
                            act.activation(scrap[:, j, :], slot("hc")[:, 0, j * P:(j + 1) * P], ACT.Square,
                                           accum_out=dev2[:, j:j + 1]).then_inc(dev2_ready, 1)
                        act.wait_ge(dev2_ready, G * i + G)
                        act.activation(dev[:], dev2[:], ACT.Sqrt, scale=1.0 / P, bias=c.eps[:]).then_inc(dev_ready, 1)

                    def t3(i):
                        act.wait_ge(t3_ready, i + 1)
                        act.activation(zT[:], slot("t3")[:, 0, :], ACT.Identity, bias=small[:, 1:2], scale=small[:, 0:1])\
                           .then_inc(zT_ready, 1)

                    def gates(i):
                        for k in range(CH):
                            act.wait_ge(up_ready, CH * i + k + 1)
                            act.activation(gate[k], slot(f"up{k}")[:, 1, :], ACT.Gelu,
                                           bias=small[:, 5 + k:6 + k]).then_inc(gate_ready, 1)

                    act.wait_ge(w_loaded, 128)
                    t1(0)
                    for j in range(G):
                        qkv(0, j)
                    norms(0)
                    with act.Fori(0, STEPS) as i:
                        attention(i)
                        t1(i + 1)
                        qkv(i + 1, 0)
                        t2(i)
                        qkv(i + 1, 1)
                        deviation(i)
                        qkv(i + 1, 2)
                        t3(i)
                        qkv(i + 1, 3)
                        gates(i)
                        norms(i + 1)

                @block.vector
                def _(dve):
                    def t1(u):
                        dve.wait_ge(t1_ready, u + 1)
                        dve.wait_ge(hT_carried, u + 1)
                        dve.wait_ge(hT_edge, u + 1)
                        dve.tensor_copy(hT[64:P, WIN + 1:WIN + W + 1], slot("t1")[64:P, 0, :]).then_inc(hT_high, 1)

                    def rotate(u, j):
                        qk = slot(f"qk{j}")[:].rearrange("p a (h d) -> p a h d", d=D)
                        place = bass.ds(u % 2 * G + j, 1)

                        def table(kind, lo, hi):
                            t = tables[:, place, kind, :, lo:hi].rearrange("p x y d -> p (x y) d")
                            return t.unsqueeze(2).broadcast_to([P, 2, HEADS, hi - lo])
                        cos4 = cosine[:].rearrange("p (a h d) -> p a h d", a=2, d=D)
                        sin4 = sine[:].rearrange("p (a h d) -> p a h d", a=2, d=D)
                        dve.wait_ge(sq_ready, G * u + j + 1)
                        dve.wait_ge(rot_ready, G * u + j + 1)
                        dve.tensor_tensor(cos4, qk, table(0, 0, D), ALU.mult).then_inc(turn_ready, 1)
                        dve.tensor_tensor(sin4[:, :, :, 0:32], qk[:, :, :, 32:64], table(1, 0, 32), ALU.mult).then_inc(turn_ready, 1)
                        dve.tensor_tensor(sin4[:, :, :, 32:64], qk[:, :, :, 0:32], table(1, 32, 64), ALU.mult).then_inc(turn_ready, 1)
                        dve.tensor_reduce(norm2[:, j, :], sq[j % 2][:].rearrange("p (h d) -> p h d", d=D), AX.X, ALU.add)\
                           .then_inc(norm2_ready, 1)
                        dve.wait_ge(turn_ready, 3 * (G * u + j) + 3)
                        dve.tensor_tensor(rot[:, j, :, :].rearrange(flat), cosine[:], sine[:], ALU.add).then_inc(rot_ready, 1)

                    def attention(i):
                        dve.wait_ge(norm_ready, i + 1)
                        dve.tensor_scalar(norm[:], norm[:], 1e-12, None, ALU.max).then_inc(inv_step, 1)
                        dve.wait_ge(inv_step, 2 * i + 1)
                        dve.reciprocal(inv_norm[:], norm[:]).then_inc(inv_step, 1)
                        dve.wait_ge(inv_step, 2 * i + 2)
                        for j in range(G):
                            dve.wait_ge(rot_ready, G * i + j + 2)
                            dve.tensor_tensor(rot[:, j, :, :], rot[:, j, :, :], inv_norm[:, j, :].unsqueeze(2).broadcast_to(
                                [P, 2 * HEADS, D]), ALU.mult).then_inc(unit_ready, 1)
                        for j in range(G):
                            dve.wait_ge(tq_ready, G * i + j + 1)
                            if j == 0:
                                dve.wait_ge(kz_carried, i + 1)
                            at = WIN + j * P
                            dve.tensor_copy(kz[64:P, :, 1, at:at + P], slot(f"tq{j}")[64:P, 1, :].rearrange("p (s t) -> p s t", t=P))\
                               .then_inc(tq_dve, 1)
                        for j in range(G):
                            scores = slot(f"s{j}")[:].rearrange("p a (h k) -> p (a h) k", k=P)
                            dve.wait_ge(s_ready, G * i + j + 2)
                            dve.tensor_reduce(top[:, j, :], scores, AX.X, ALU.max).then_inc(top_ready, 1)
                            dve.wait_ge(top_ready, G * i + j + 1)
                            dve.tensor_tensor(prob[:, j, :, :], scores, top[:, j, :].unsqueeze(2).broadcast_to([P, HEADS, P]),
                                              ALU.subtract).then_inc(less_top, 1)
                        for j in range(G):
                            dve.wait_ge(exp_ready, G * i + j + 1)
                            dve.tensor_reduce(total[:, j, :], prob[:, j, :, :], AX.X, ALU.add).then_inc(total_ready, 1)
                            dve.wait_ge(total_ready, G * i + j + 1)
                            dve.reciprocal(inv_total[:, j, :], total[:, j, :]).then_inc(inv_total_ready, 1)
                        for j in range(G):
                            dve.wait_ge(o_ready, G * i + j + 1)
                            dve.wait_ge(inv_total_ready, G * i + j + 1)
                            dve.tensor_tensor(attn[:, j, :].rearrange("p (h d) -> p h d", d=D),
                                              slot(f"o{j}")[:, 0, :].rearrange("p (h d) -> p h d", d=D),
                                              inv_total[:, j, :].unsqueeze(2).broadcast_to([P, HEADS, D]), ALU.mult)\
                               .then_inc(attn_ready, 1)
                        for j in range(G):
                            dve.wait_ge(y_ready, G * i + j + 1)
                            dve.tensor_tensor(h1[:, j, :], slot(f"o{j}")[:, 0, 0:P],
                                              H[:, bass.ds(i * G + j, 1), :].rearrange(flat), ALU.add).then_inc(h1_ready, 1)

                    def t2(i):
                        dve.tensor_tensor(h1T[64:P, 0:1], h1T[64:P, W:W + 1], flags[64:P, bass.ds(i % 2, 1)], ALU.mult)\
                           .then_inc(h1T_edge, 1)
                        dve.wait_ge(h1T_edge, i + 1)
                        dve.wait_ge(t2_ready, i + 1)
                        dve.wait_ge(h1T_low, i + 1)
                        dve.tensor_copy(h1T[64:P, 1:W + 1], slot("t2")[64:P, 0, :]).then_inc(h1T_high, 1)

                    def normalised(i):
                        dve.wait_ge(dev_ready, i + 1)
                        dve.reciprocal(inv_dev[:], dev[:]).then_inc(inv_dev_ready, 1)
                        dve.wait_ge(inv_dev_ready, i + 2)
                        for j in range(G):
                            dve.tensor_scalar(z[:, j, :], slot("hc")[:, 0, j * P:(j + 1) * P], inv_dev[:, j:j + 1], None, ALU.mult)\
                               .then_inc(z_ready, 1)

                    def out(i):
                        for k in range(CH):
                            dve.wait_ge(gate_ready, CH * i + k + 1)
                            dve.scalar_tensor_tensor(hid[k], slot(f"up{k}")[:, 0, :], small[:, 2 + k:3 + k], gate[k],
                                                     ALU.add, ALU.mult).then_inc(hid_ready, 1)
                        dve.wait_ge(down_ready, i + 1)
                        dve.wait_ge(h1_b2_ready, i + 1)
                        dve.tensor_tensor(H[:, bass.ds(i * G, G), :].rearrange(flat), slot("down")[:, 0, :],
                                          h1_b2[:].rearrange(flat), ALU.add).then_inc(layer_out, 1)

                    for s, n in ((norm2_ready, 2), (rot_ready, 1), (inv_dev_ready, 1), (layer_out, 1), (hid_ready, CH)):
                        dve.sem_inc(s, n)
                    dve.wait_ge(w_loaded, 128)
                    dve.tensor_tensor(tables[:].rearrange("p t x y d -> p t (x y d)"), angles[:].rearrange("p t x y d -> p t (x y d)"),
                                      scales[:].rearrange("p x y d -> p (x y d)").unsqueeze(1).broadcast_to([P, TPB, 4 * D]),
                                      ALU.mult).then_inc(tables_ready, 1)
                    dve.wait_ge(tables_ready, 1)
                    t1(0)
                    for j in range(G):
                        rotate(0, j)
                    with dve.Fori(0, STEPS) as i:
                        attention(i)
                        t1(i + 1)
                        rotate(i + 1, 0)
                        t2(i)
                        rotate(i + 1, 1)
                        normalised(i)
                        rotate(i + 1, 2)
                        rotate(i + 1, 3)
                        out(i)
            clear()

        with nc.Fori(0, 2) as depth:
            layer(depth)

        with ExitStack() as st2:
            sem, clear = semaphores(nc, st2, first=200)
            x_ready = sem("x_ready")
            with nc.Block() as block:
                @block.vector
                def _(dve):
                    for b in range(B):
                        tiles = slice(b * TPB, (b + 1) * TPB)
                        xs = c.X[:, tiles, :].rearrange(flat)
                        dve.scalar_tensor_tensor(xs, H[:, tiles, :].rearrange(flat), 0.5, xs, ALU.mult, ALU.add).then_inc(x_ready, 1)
            clear()


def normalised_columns(nc, c, dst, gain=None, shift=None, twice=False):
    G = 4
    STEPS = NT // G
    row_statistics(nc, c, twice)
    with ExitStack() as st:
        xn = st.enter_context(nc.sbuf_tensor(c.fresh("xn"), [P, 2, G, P], F32))
        sem, clear = semaphores(nc, st)
        xn_ready = sem("xn_ready")
        turned = sem("turned")
        columns_ready = sem("columns_ready")
        with nc.Block() as block:
            @block.vector
            def _(dve):
                for i in range(STEPS):
                    if i >= 2:
                        dve.wait_ge(turned, i - 1)
                    for j in range(G):
                        normalise(dve, c, i * G + j, xn[:, i % 2, j, :]).then_inc(xn_ready, 1)

            @block.tensor
            def _(pe):
                for i in range(STEPS):
                    pe.wait_ge(xn_ready, G * (i + 1))
                    if i >= 2:
                        pe.wait_ge(columns_ready, i - 1)
                    for j in range(G):
                        m = pe.transpose(c.slots[i % 2][:, 0, j * P:(j + 1) * P], xn[:, i % 2, j, :], c.ident[:])
                    m.then_inc(turned, 1)

            @block.scalar
            def _(act):
                for i in range(STEPS):
                    act.wait_ge(turned, i + 1)
                    out = dst[:, i * G * P:(i + 1) * G * P]
                    if gain is None:
                        act.activation(out, c.slots[i % 2][:, 0, :], ACT.Copy).then_inc(columns_ready, 1)
                    else:
                        act.activation(out, c.slots[i % 2][:, 0, :], ACT.Identity, bias=shift,
                                       scale=gain).then_inc(columns_ready, 1)
        clear()


def causal_attention(nc, c, gain_d, shift_d, w_d, wo_d, bias_d):
    HEADS, D = 16, 64
    PAIRS = HEADS // 2
    UNITS = B * PAIRS
    JOBS = 2 * TPB
    RING = 4
    T_LAG, PV_LAG = 3, 5
    with ExitStack() as st:
        def sb(name, shape, dt=F32):
            return st.enter_context(nc.sbuf_tensor(c.fresh(name), shape, dt))

        gain = sb("gain", [P, 1])
        shift = sb("shift", [P, 1])
        bias = sb("bias", [P, P])
        xT = sb("xT", [P, NT * P])
        w = sb("w_qkv", [P, 5, P])
        wo = sb("w_out", [P, P])
        q = [sb(f"q{h}", [P, S], F32R) for h in range(2)]
        k_hi = [sb(f"k_hi{h}", [P, S], F32R) for h in range(2)]
        k_lo = [sb(f"k_lo{h}", [P, S], F32R) for h in range(2)]
        v = sb("v", [P, TPB, P])
        xv = sb("x_batch", [P, S])
        e = [sb(f"e{r}", [P, S]) for r in range(RING)]
        eT = [sb(f"eT{r}", [P, S]) for r in range(RING)]
        nmax = sb("nmax", [P, JOBS])
        total = sb("total", [P, JOBS])
        inv = sb("inv", [P, JOBS])
        oT = sb("oT", [P, S])
        turn = c.slots[2]
        o = c.slots[3]

        with ExitStack() as st2:
            sem2, clear2 = semaphores(nc, st2)
            loaded = sem2("loaded")
            with nc.Block() as block:
                @block.sync
                def _(sp):
                    sp.dma_start(gain[:], gain_d).then_inc(loaded, 16)
                    sp.dma_start(shift[:], shift_d).then_inc(loaded, 16)
                    sp.dma_start(bias[:], bias_d).then_inc(loaded, 16)
                    sp.wait_ge(loaded, 48)
            clear2()
        normalised_columns(nc, c, xT, gain[:], shift[:], twice=True)

        sem, clear = semaphores(nc, st)
        w_loaded = sem("w_loaded")
        wo_loaded = sem("wo_loaded")
        x_ready = sem("x_ready")
        p_ready = sem("p_ready")
        hi_ready = sem("hi_ready")
        lo_ready = sem("lo_ready")
        xv_ready = sem("xv_ready")
        vp_ready = sem("vp_ready")
        v_ready = sem("v_ready")
        s_ready = sem("s_ready")
        max_ready = sem("max_ready")
        e_ready = sem("e_ready")
        inv_ready = sem("inv_ready")
        scaled_dve = sem("scaled_dve")
        scaled_act = sem("scaled_act")
        turned = sem("turned")
        eT_dve = sem("eT_dve")
        eT_act = sem("eT_act")
        o_ready = sem("o_ready")
        oT_ready = sem("oT_ready")
        y_ready = sem("y_ready")

        with nc.Block() as block:
            @block.sync
            def _(sp):
                sp.dma_start(w[:], w_d[0]).then_inc(w_loaded, 16)
                with sp.Fori(0, UNITS) as u:
                    sp.wait_ge(y_ready, u + 1)
                    sp.dma_start(wo[:], wo_d[bass.ds(u % PAIRS, 1)].rearrange("a p e -> (a p) e")).then_inc(wo_loaded, 16)
                    sp.wait_ge(vp_ready, u + 1)
                    sp.dma_start(w[:], w_d[bass.ds((u + 1) % PAIRS, 1)].rearrange("a p c e -> (a p) c e")).then_inc(w_loaded, 16)

            @block.tensor
            def _(pe):
                def project(u, i):
                    if i == 0:
                        pe.wait_ge(w_loaded, 16 * u + 16)
                        pe.wait_ge(xv_ready, u + 1)
                        pe.wait_ge(e_ready, JOBS * u + JOBS - 1)
                    if i == 1:
                        pe.wait_ge(e_ready, JOBS * u + JOBS)
                    if i >= 2:
                        pe.wait_ge(lo_ready, 4 * u + i - 1)
                    which = (0, 2, 1, 3)[i]
                    for half in range(2):
                        m = pe.matmul(c.slots[i % 2][:, half, :], w[:, which, :],
                                      xv[:, half * 512:half * 512 + 512], start=True, stop=True)
                    m.then_inc(p_ready, 1)

                def project_v(u):
                    pe.wait_ge(lo_ready, 4 * u + 3)
                    for t in range(TPB):
                        m = pe.matmul(c.slots[0][:, t // 4, (t % 4) * P:(t % 4 + 1) * P],
                                      xv[:, t * P:(t + 1) * P], w[:, 4, :], start=True, stop=True)
                    m.then_inc(vp_ready, 1)

                def scores(u, n):
                    i, h = n // 2, n % 2
                    if n < 2:
                        pe.wait_ge(lo_ready, 4 * u + 2 * h + 2)
                    if n == 0:
                        pe.wait_ge(v_ready, u + 1)
                    if n == 1:
                        pe.wait_ge(x_ready, u + 1)
                    if n >= 2:
                        pe.wait_ge(e_ready, JOBS * (u + 1) + n - 1)
                    qi = q[h][:, i * P:(i + 1) * P]
                    for bank in range(i // 4 + 1):
                        lo, hi = bank * 512, min((i + 1) * P, bank * 512 + 512)
                        out = c.slots[h][:, bank, 0:hi - lo]
                        pe.matmul(out, qi, k_hi[h][:, lo:hi], start=True, stop=False)
                        if bank == i // 4:
                            pe.matmul(c.slots[h][:, bank, hi - lo - P:hi - lo], c.ident_bf[:], c.causal[:],
                                      start=False, stop=False, skip_group_check=True)
                        m = pe.matmul(out, qi, k_lo[h][:, lo:hi], start=False, stop=True)
                    m.then_inc(s_ready, 1)

                def transpose(u, n):
                    i, r = n // 2, n % RING
                    pe.wait_ge((scaled_dve, scaled_act)[n % 2], TPB * u + i + 1)
                    if n % 2 == 0:
                        pe.wait_ge(eT_act, TPB * u + i + 1)
                    else:
                        pe.wait_ge(eT_dve, TPB * u + i + 1)
                    for t in range(i + 1):
                        m = pe.transpose(turn[:, t // 4, (t % 4) * P:(t % 4 + 1) * P], e[r][:, t * P:(t + 1) * P], c.ident[:])
                    m.then_inc(turned, 1)

                def values(u, i):
                    pe.wait_ge(eT_dve, TPB * u + i + 1)
                    pe.wait_ge(eT_act, TPB * u + i + 2)
                    for t in range(i + 1):
                        for h in range(2):
                            m = pe.matmul(o[64 * h:64 * h + 64, i // 4, (i % 4) * P:(i % 4 + 1) * P],
                                          v[:, t, 64 * h:64 * h + 64], eT[(2 * i + h) % RING][:, t * P:(t + 1) * P],
                                          start=(t == 0), stop=(t == i), skip_group_check=True)
                    if i == TPB - 1:
                        m.then_inc(o_ready, 1)

                def output(u):
                    pe.wait_ge(lo_ready, 4 * u + 8)
                    pe.wait_ge(wo_loaded, 16 * u + 16)
                    pe.wait_ge(oT_ready, u + 1)
                    for t in range(TPB):
                        m = pe.matmul(c.slots[1][:, t // 4, (t % 4) * P:(t % 4 + 1) * P], oT[:, t * P:(t + 1) * P],
                                      wo[:], start=True, stop=True)
                    m.then_inc(y_ready, 1)

                def tick(u, n):
                    if n < JOBS:
                        scores(u, n)
                    if 0 <= n - T_LAG < JOBS:
                        transpose(u, n - T_LAG)
                    if n - PV_LAG >= 0 and (n - PV_LAG) % 2 == 1 and n - PV_LAG < JOBS:
                        values(u, (n - PV_LAG) // 2)

                pe.sem_inc(y_ready, 1)
                for i in range(4):
                    project(0, i)
                project_v(0)
                with pe.Fori(0, UNITS) as u:
                    for n in range(JOBS):
                        tick(u, n)
                    for i in range(4):
                        project(u + 1, i)
                        tick(u, JOBS + i)
                    tick(u, JOBS + 4)
                    project_v(u + 1)
                    output(u)

            @block.vector
            def _(dve):
                def low_part(u, i):
                    slot, h = c.slots[i % 2], i // 2
                    dve.wait_ge(hi_ready, 4 * u + i + 1)
                    if i % 2 == 0:
                        dve.scalar_tensor_tensor(q[h][64:P, :], slot[64:P].rearrange("p a n -> p (a n)"), D ** -0.5,
                                                 q[h][64:P, :].bitcast(F32), ALU.mult, ALU.subtract).then_inc(lo_ready, 1)
                    else:
                        dve.tensor_tensor(k_lo[h][:], slot[:].rearrange("p a n -> p (a n)"), k_hi[h][:].bitcast(F32),
                                          ALU.subtract).then_inc(lo_ready, 1)

                def tick(u, n):
                    if n < JOBS:
                        i, h = n // 2, n % 2
                        dve.wait_ge(s_ready, JOBS * u + n + 1)
                        dve.tensor_reduce(nmax[:, n:n + 1], c.slots[h][:].rearrange("p a n -> p (a n)")[:, 0:(i + 1) * P],
                                          AX.X, ALU.max, negate=True).then_inc(max_ready, 1)
                    if 0 <= n - 1 < JOBS:
                        dve.wait_ge(e_ready, JOBS * (u + 1) + n)
                        dve.reciprocal(inv[:, n - 1:n], total[:, n - 1:n]).then_inc(inv_ready, 1)
                        if n % 2 == 1:
                            dve.wait_ge(inv_ready, JOBS * u + n)
                            part = e[(n - 1) % RING][:, 0:((n - 1) // 2 + 1) * P]
                            dve.tensor_scalar(part, part, inv[:, n - 1:n], None, ALU.mult).then_inc(scaled_dve, 1)
                    m = n - T_LAG
                    if 0 <= m < JOBS and m % 2 == 0:
                        dve.wait_ge(turned, JOBS * u + m + 1)
                        width = (m // 2 + 1) * P
                        dve.tensor_copy(eT[m % RING][:, 0:width], turn[:].rearrange("p a n -> p (a n)")[:, 0:width])\
                           .then_inc(eT_dve, 1)

                for i in range(4):
                    low_part(0, i)
                with dve.Fori(0, UNITS) as u:
                    for n in range(JOBS):
                        tick(u, n)
                    for i in range(4):
                        tick(u, JOBS + i)
                        low_part(u + 1, i)
                    dve.wait_ge(o_ready, u + 1)
                    dve.tensor_copy(oT[:], o[:].rearrange("p a n -> p (a n)")).then_inc(oT_ready, 1)
                    dve.wait_ge(y_ready, u + 2)
                    xs = c.X[:, bass.ds((u // PAIRS) * TPB, TPB), :].rearrange("p t d -> p (t d)")
                    dve.wait_ge(x_ready, u + 1)
                    dve.tensor_tensor(xs, c.slots[1][:].rearrange("p a n -> p (a n)"), xs, ALU.add).then_inc(x_ready, 1)

            @block.scalar
            def _(act):
                def high_part(u, i):
                    slot, h = c.slots[i % 2], i // 2
                    act.wait_ge(p_ready, 4 * u + i + 1)
                    dst, scale = (q[h], D ** -0.5) if i % 2 == 0 else (k_hi[h], 1.0)
                    act.activation(dst[:], slot[:].rearrange("p a n -> p (a n)"), ACT.Copy, scale=scale).then_inc(hi_ready, 1)

                def values_out(u):
                    act.wait_ge(vp_ready, u + 1)
                    act.activation(v[:].rearrange("p t d -> p (t d)"), c.slots[0][:].rearrange("p a n -> p (a n)"),
                                   ACT.Copy).then_inc(v_ready, 1)

                def tick(u, n):
                    if n < JOBS:
                        i, h = n // 2, n % 2
                        act.wait_ge(max_ready, JOBS * u + n + 1)
                        act.activation(e[n % RING][:, 0:(i + 1) * P],
                                       c.slots[h][:].rearrange("p a n -> p (a n)")[:, 0:(i + 1) * P], ACT.Exp,
                                       bias=nmax[:, n:n + 1], accum_out=total[:, n:n + 1]).then_inc(e_ready, 1)
                    if 0 <= n - 1 < JOBS and n % 2 == 0:
                        act.wait_ge(inv_ready, JOBS * u + n)
                        part = e[(n - 1) % RING][:, 0:((n - 1) // 2 + 1) * P]
                        act.activation(part, part, ACT.Copy, scale=inv[:, n - 1:n]).then_inc(scaled_act, 1)
                    m = n - T_LAG
                    if 0 <= m < JOBS and m % 2 == 1:
                        act.wait_ge(turned, JOBS * u + m + 1)
                        width = (m // 2 + 1) * P
                        act.activation(eT[m % RING][:, 0:width], turn[:].rearrange("p a n -> p (a n)")[:, 0:width],
                                       ACT.Copy).then_inc(eT_act, 1)

                act.sem_inc(e_ready, JOBS)
                act.sem_inc(eT_act, 1)
                act.preload_act_table(ACT.Exp)
                for i in range(4):
                    high_part(0, i)
                values_out(0)
                with act.Fori(0, UNITS) as u:
                    for n in range(JOBS):
                        tick(u, n)
                    for i in range(4):
                        tick(u, JOBS + i)
                        high_part(u + 1, i)
                    values_out(u + 1)

            @block.gpsimd
            def _(pool):
                wide = bias[:].rearrange("p (t d) -> p t d", t=1).broadcast_to([P, NT, P])
                pool.tensor_tensor(c.X[:], c.X[:], wide, ALU.add).then_inc(x_ready, 1)
                pool.tensor_copy(xv[:], xT[:, 0:S]).then_inc(xv_ready, 1)
                with pool.Fori(0, UNITS) as u:
                    pool.wait_ge(vp_ready, u + 1)
                    pool.tensor_copy(xv[:], xT[:, bass.ds((((u + 1) % UNITS) // PAIRS) * S, S)]).then_inc(xv_ready, 1)
        clear()


def host_constants():
    eye = np.eye(P, dtype=np.float32)
    future = np.triu(np.full((P, P), BIG, np.float32), 1)
    sel = np.zeros((4, P, 2, 4, 32), np.float32)
    for head in range(16):
        sel[head // 4, head * 8:head * 8 + 8, head // 2 % 2, :, 16 + head % 2] = 1
    masks = np.zeros((4, 32, 8), np.float32)
    for j in range(2):
        masks[:, 8 * j:8 * j + 8, 2 * j] = 1
        masks[0:2, 16 + j, 2 * j + 1] = -1
    masks[:, :, 6] = 1
    masks[:, 16:18, 6] = np.float32(1) / np.sqrt(np.float32(8))
    D, WIN = 64, 64
    half = np.arange(0, D, 2, dtype=np.float32)
    inv_freq = np.float32(1) / np.float32(10000) ** (half / np.float32(D))
    t = np.arange(S, dtype=np.float32)
    freqs = (t[:, None] * inv_freq[None, :]).astype(np.float64)
    growth = ((half + 0.4 * D) / (1.4 * D)).astype(np.float64)[None, :] ** ((t - S // 2) / (WIN // 2)).astype(np.float64)[:, None]
    both = [np.stack([8 * f * growth, f / growth], axis=1) for f in (np.cos(freqs), np.sin(freqs))]
    angles = np.stack([np.concatenate([both[0], both[0]], axis=2), np.concatenate([-both[1], both[1]], axis=2)], axis=1)
    angles = angles.astype(np.float32).reshape(TPB, P, 2, 2, D).transpose(1, 0, 2, 3, 4)
    r, k = np.arange(P)[:, None] % WIN, np.arange(2 * WIN)[None, :]
    inside = (k >= r) & (k <= r + WIN)
    first = inside & ((np.arange(P)[:, None] >= WIN) | (k >= WIN))
    band = np.stack([np.tile(np.where(m, np.float32(0), np.float32(BIG)), (1, 4)) for m in (first, inside)], axis=1)
    flags = np.tile(np.array([[0, 1]], np.float32), (P, 1))
    centre = eye - np.float32(1) / np.float32(P)
    block_mask = np.kron(np.eye(16, dtype=np.float32), np.ones((8, 8), np.float32))
    return {"ident": eye, "sel": sel.reshape(4, P, 2, P), "masks": masks.reshape(P, 8), "block_mask": block_mask,
            "angles": np.ascontiguousarray(angles), "band": band.astype(np.float32), "flags": flags,
            "centre": centre, "causal": future}


def load_x(nc, c, x_d):
    with ExitStack() as st:
        future = st.enter_context(nc.sbuf_tensor(c.fresh("future"), [P, P], F32))
        sem, clear = semaphores(nc, st)
        loaded = sem("loaded")
        constants_ready = sem("constants_ready")
        with nc.Block() as block:
            @block.sync
            def _(sp):
                sp.dma_start(c.X[:], x_d.rearrange("(t p) d -> p t d", p=P)).then_inc(loaded, 16)
                sp.dma_start(c.ident[:], c.const["ident"]).then_inc(loaded, 16)
                sp.dma_start(future[:], c.const["causal"]).then_inc(loaded, 16)

            @block.vector
            def _(dve):
                dve.memset(c.eps[:], EPS).then_inc(constants_ready, 1)
                dve.wait_ge(loaded, 48)
                dve.tensor_copy(c.ident_bf[:], c.ident[:]).then_inc(constants_ready, 1)
                dve.tensor_copy(c.causal[:], future[:]).then_inc(constants_ready, 1)
        clear()


def store_x(nc, c, out_d):
    with ExitStack() as st:
        sem, clear = semaphores(nc, st)
        stored = sem("stored")
        with nc.Block() as block:
            @block.sync
            def _(sp):
                sp.dma_start(out_d.rearrange("(t p) d -> p t d", p=P), c.X[:]).then_inc(stored, 16)
                sp.wait_ge(stored, 16)


def open_ctx(nc, st, const):
    c = Ctx()
    c.const = const
    c.count = [0]
    c.X = st.enter_context(nc.sbuf_tensor("X", [P, NT, P], F32))
    c.ident = st.enter_context(nc.sbuf_tensor("ident", [P, P], F32))
    c.ident_bf = st.enter_context(nc.sbuf_tensor("ident_bf", [P, P], BF16))
    c.causal = st.enter_context(nc.sbuf_tensor("causal", [P, P], BF16))
    c.stats = st.enter_context(nc.sbuf_tensor("stats", [P, NT, 6], F32))
    c.moments = st.enter_context(nc.sbuf_tensor("moments", [P, NT, 2], F32))
    c.deviation = st.enter_context(nc.sbuf_tensor("deviation", [P, NT], F32))
    c.second = st.enter_context(nc.sbuf_tensor("second", [P, NT], F32))
    c.rstd = st.enter_context(nc.sbuf_tensor("rstd", [P, NT], F32))
    c.eps = st.enter_context(nc.sbuf_tensor("eps", [P, 1], F32))
    c.slots = [st.enter_context(nc.psum_tensor(f"slot{k}", [P, 2, 512], F32)) for k in range(4)]

    def fresh(name):
        c.count[0] += 1
        return f"{name}_{c.count[0]}"
    c.fresh = fresh
    return c


def causal_layout(w_qkv, w_out):
    q, k, v = (w_qkv[i * 1024:(i + 1) * 1024].reshape(8, 2, 64, P) for i in range(3))
    twice = [np.concatenate([m[:, h], m[:, h]], axis=1) for m in (q, k) for h in range(2)]
    w = np.stack(twice + [v.reshape(8, P, P)], axis=1)
    return np.ascontiguousarray(w.transpose(0, 3, 1, 2)), np.ascontiguousarray(w_out.T.reshape(8, P, P))


def distance_layout(W_k):
    wT = W_k.T.reshape(P, 4, 2, 16)
    rep = np.zeros((4, P, 2, 4, 32), W_k.dtype)
    rep[:, :, :, :, 0:16] = wT.transpose(1, 0, 2, 3)[:, :, :, None, :]
    return rep.reshape(4, P, 2, P)


def local_layout(wqkv, q_scale, k_scale, wo, ln_g, ln_b, w1, b1, w2, b2):
    n, hid, chunks = wqkv.shape[0], w2.shape[1], 3
    half = np.zeros((n, P, 2, chunks * P), w1.dtype)
    half[:, :, 0, :hid], half[:, :, 1, :hid] = w1[:, :, :hid], w1[:, :, hid:]
    bias = np.zeros((n, 2, chunks * P), b1.dtype)
    bias[:, 0, :hid], bias[:, 1, :hid] = b1[:, :hid], b1[:, hid:]
    down = np.zeros((n, chunks * P, P), w2.dtype)
    down[:, :hid] = w2
    small = np.concatenate([ln_g[:, None], ln_b[:, None], bias.reshape(n, 2 * chunks, P)], axis=1).transpose(0, 2, 1)
    qk = np.stack([q_scale, k_scale], axis=1)
    scales = np.stack([qk, np.concatenate([qk[:, :, 32:], qk[:, :, :32]], axis=2)], axis=1)
    return {
        "w_qk": np.ascontiguousarray(wqkv[:, :, :1024]),
        "w_v": np.ascontiguousarray(wqkv[:, :, 1024:]),
        "w_o": np.ascontiguousarray(wo.reshape(n, 4, P, P).transpose(0, 2, 1, 3)),
        "w1": half.reshape(n, P, 2, chunks, P),
        "w2": np.ascontiguousarray(down.reshape(n, chunks, P, P).transpose(0, 2, 1, 3)),
        "small": np.ascontiguousarray(small),
        "b2": np.ascontiguousarray(np.broadcast_to(b2[:, None, :], (n, P, P))),
        "scales": np.ascontiguousarray(np.broadcast_to(scales[:, None], (n, P, 2, 2, 64))),
    }


def macaron(nc, d, out_d):
    with ExitStack() as st:
        c = open_ctx(nc, st, {k[6:]: d[k] for k in d if k.startswith("const_")})
        local = {k[6:]: d[k] for k in d if k.startswith("local_")}
        load_x(nc, c, d["x"])
        gelu_ffn(nc, c, d["ffn_w1"], d["ffn_b1"], d["ffn_w2"], d["ffn_b2"])
        distance_attention(nc, c, d["dist_wk"], d["dist_wv"], d["dist_wo"], d["dist_rep"], c.const["sel"], c.const["masks"])
        gelu_ffn(nc, c, d["ffn_w1"], d["ffn_b1"], d["ffn_w2"], d["ffn_b2"])
        local_layers(nc, c, local)
        causal_attention(nc, c, d["causal_gain"], d["causal_shift"], d["causal_w"], d["causal_wo"], d["causal_bias"])
        local_layers(nc, c, local)
        store_x(nc, c, out_d)


def kernel(**inputs):
    import concourse.bacc as bacc
    from concourse.bass_utils import run_bass_kernel_spmd

    a = {k: np.asarray(v) for k, v in inputs.items()}
    flipped = lambda m: np.ascontiguousarray(m.T)
    rows = lambda r: np.ascontiguousarray(np.broadcast_to(r, (P, r.shape[0])))
    causal_w, causal_wo = causal_layout(a["L1_attn_w_qkv"], a["L1_attn_w_out"])
    names = ["wqkv", "q_scale", "k_scale", "wo", "ln_g", "ln_b", "w1", "b1", "w2", "b2"]
    data = {
        "x": a["L0_attn_x"].reshape(NT * P, P),
        "ffn_w1": a["L0_ffn_w1"], "ffn_b1": flipped(a["L0_ffn_b1"].reshape(-1, P)),
        "ffn_w2": a["L0_ffn_w2"], "ffn_b2": rows(a["L0_ffn_b2"]),
        "dist_wk": flipped(a["L0_attn_W_k"]), "dist_wv": flipped(a["L0_attn_W_v"]),
        "dist_wo": flipped(a["L0_attn_W_o"]), "dist_rep": distance_layout(a["L0_attn_W_k"]),
        "causal_gain": a["L1_attn_ln_gamma"].reshape(P, 1), "causal_shift": a["L1_attn_ln_beta"].reshape(P, 1),
        "causal_w": causal_w, "causal_wo": causal_wo, "causal_bias": rows(a["L1_attn_b_out"]),
    }
    data.update({"local_" + k: v for k, v in local_layout(*[a["L1_ffn_" + n] for n in names]).items()})
    data.update({"const_" + k: v for k, v in host_constants().items()})

    nc = bacc.Bacc("TRN2", target_bir_lowering=False, num_devices=1)
    arrays = {f"in_{k}_dram": np.ascontiguousarray(v) for k, v in data.items()}
    d = {k: nc.dram_tensor(f"in_{k}_dram", v.shape, mybir.dt.from_np(v.dtype), kind="ExternalInput").ap()
         for k, v in data.items()}
    out_d = nc.dram_tensor("out_0_dram", (NT * P, P), F32, kind="ExternalOutput").ap()
    macaron(nc, d, out_d)
    result = run_bass_kernel_spmd(nc, [arrays], core_ids=[0])
    return result.results[0]["out_0_dram"].reshape(B, S, P)
```

```python
from contextlib import ExitStack

import concourse.bass as bass
from concourse import mybir
import numpy as np

F32 = mybir.dt.float32
F32R = mybir.dt.float32r
BF16 = mybir.dt.bfloat16
ALU = mybir.AluOpType
ACT = mybir.ActivationFunctionType
AX = mybir.AxisListType

P = 128
B, S = 4, 1024
TPB = S // P
NT = B * TPB
EPS = 1e-5
BIG = -1e30


class Ctx:
    pass


def semaphores(nc, stack, first=100):
    made = []

    def sem(name):
        made.append(stack.enter_context(nc.semaphore(name, num=first + len(made))))
        return made[-1]

    def clear():
        nc.all_engine_barrier(sems_to_clear=range(first, first + len(made)))
    return sem, clear


def row_statistics(nc, c, twice=False):
    with ExitStack() as st:
        sem, clear = semaphores(nc, st, first=200)
        stats_ready = sem("stats_ready")
        moments_ready = sem("moments_ready")
        deviation_ready = sem("deviation_ready")
        rstd_ready = sem("rstd_ready")
        with nc.Block() as block:
            @block.vector
            def _(dve):
                for t in range(NT):
                    dve.bn_stats(c.stats[:, t, :], c.X[:, t, :]).then_inc(stats_ready, 1)
                for t in range(NT):
                    dve.wait_ge(stats_ready, t + 1)
                    dve.bn_aggr(c.moments[:, t, :], c.stats[:, t, :]).then_inc(moments_ready, 1)
                dve.wait_ge(deviation_ready, 1)
                dve.reciprocal(c.rstd[:], c.deviation[:]).then_inc(rstd_ready, 1)
                if twice:
                    dve.wait_ge(rstd_ready, 1)
                    dve.tensor_tensor(c.second[:], c.moments[:, :, 1], c.rstd[:], ALU.mult).then_inc(rstd_ready, 1)
                    dve.wait_ge(rstd_ready, 2)
                    dve.tensor_tensor(c.second[:], c.second[:], c.rstd[:], ALU.mult).then_inc(rstd_ready, 1)
                    dve.wait_ge(deviation_ready, 2)
                    dve.reciprocal(c.second[:], c.deviation[:]).then_inc(rstd_ready, 1)
                    dve.wait_ge(rstd_ready, 4)
                    dve.tensor_tensor(c.rstd[:], c.rstd[:], c.second[:], ALU.mult).then_inc(rstd_ready, 1)

            @block.scalar
            def _(act):
                act.preload_act_table(ACT.Sqrt)
                act.wait_ge(moments_ready, NT)
                act.activation(c.deviation[:], c.moments[:, :, 1], ACT.Sqrt, bias=c.eps[:]).then_inc(deviation_ready, 1)
                if twice:
                    act.wait_ge(rstd_ready, 3)
                    act.activation(c.deviation[:], c.second[:], ACT.Sqrt, bias=c.eps[:]).then_inc(deviation_ready, 1)
        clear()


def normalise(dve, c, t, dst):
    return dve.tensor_scalar(dst, c.X[:, t, :], c.moments[:, t, 0:1], c.rstd[:, bass.ds(t, 1)], ALU.subtract, ALU.mult)


def gelu_ffn(nc, c, w1_d, b1_d, w2_d, b2_d):
    HID = 512
    CH = HID // P
    G = 4
    W = G * P
    STEPS = NT // G
    with ExitStack() as st:
        def sb(name, shape, dt=F32):
            return st.enter_context(nc.sbuf_tensor(c.fresh(name), shape, dt))

        w1 = sb("w1", [P, HID])
        b1 = sb("b1", [P, CH])
        w2 = sb("w2", [P, CH, P])
        half_b2 = sb("half_b2", [P, P])
        xn = sb("xn", [P, G, P])
        xnT = sb("xnT", [P, W])
        hid = sb("hid", [P, CH, W])
        x_b2 = sb("x_b2", [P, G, P])
        tr, up0, up1, down = c.slots
        sem, clear = semaphores(nc, st)
        weights = sem("weights")
        half_b2_ready = sem("half_b2_ready")
        xn_ready = sem("xn_ready")
        tr_ready = sem("tr_ready")
        xnT_ready = sem("xnT_ready")
        up_ready = sem("up_ready")
        hid_ready = sem("hid_ready")
        down_ready = sem("down_ready")
        x_b2_ready = sem("x_b2_ready")
        x_ready = sem("x_ready")

        row_statistics(nc, c)
        with nc.Block() as block:
            @block.sync
            def _(sp):
                sp.dma_start(w1[:], w1_d).then_inc(weights, 16)
                sp.dma_start(b1[:], b1_d).then_inc(weights, 16)
                sp.dma_start(w2[:], w2_d.rearrange("(c p) e -> p c e", p=P)).then_inc(weights, 16)
                sp.dma_start(half_b2[:], b2_d).then_inc(weights, 16)

            @block.gpsimd
            def _(pool):
                pool.wait_ge(weights, 64)
                pool.tensor_scalar(half_b2[:], half_b2[:], 0.5, None, ALU.mult).then_inc(half_b2_ready, 1)
                pool.wait_ge(half_b2_ready, 1)
                bias = half_b2[:].rearrange("p (g e) -> p g e", g=1).broadcast_to([P, G, P])
                with pool.Fori(0, STEPS) as i:
                    pool.wait_ge(x_ready, i + 1)
                    pool.tensor_tensor(x_b2[:], c.X[:, bass.ds(i * G, G), :], bias, ALU.add).then_inc(x_b2_ready, 1)

            @block.vector
            def _(dve):
                def norm(i):
                    for j in range(G):
                        normalise(dve, c, i * G + j, xn[:, j, :]).then_inc(xn_ready, 1)

                def step(i, more):
                    dve.wait_ge(tr_ready, i + 1)
                    dve.tensor_copy(xnT[:], tr[:, 0, :]).then_inc(xnT_ready, 1)
                    if more:
                        norm(i + 1)
                    dve.wait_ge(down_ready, i + 1)
                    dve.wait_ge(x_b2_ready, i + 1)
                    dve.scalar_tensor_tensor(c.X[:, bass.ds(i * G, G), :].rearrange("p g e -> p (g e)"), down[:, 0, :], 0.5,
                                             x_b2[:].rearrange("p g e -> p (g e)"),
                                             ALU.mult, ALU.add).then_inc(x_ready, 1)

                dve.sem_inc(x_ready, 1)
                norm(0)
                with dve.Fori(0, STEPS - 1) as i:
                    step(i, True)
                step(STEPS - 1, False)

            @block.tensor
            def _(pe):
                pe.wait_ge(weights, 64)
                with pe.Fori(0, STEPS) as i:
                    pe.wait_ge(xn_ready, i * G + G)
                    for j in range(G):
                        m = pe.transpose(tr[:, 0, j * P:(j + 1) * P], xn[:, j, :], c.ident[:])
                    m.then_inc(tr_ready, 1)
                    pe.wait_ge(xnT_ready, i + 1)
                    for k in range(CH):
                        up = (up0, up1)[k // 2]
                        pe.wait_ge(hid_ready, i * CH + k + 1)
                        pe.matmul(up[:, k % 2, :], w1[:, k * P:(k + 1) * P], xnT[:],
                                  start=True, stop=True).then_inc(up_ready, 1)
                    pe.wait_ge(x_ready, i + 1)
                    for j in range(G):
                        for k in range(CH):
                            if j == 0:
                                pe.wait_ge(hid_ready, i * CH + CH + k + 1)
                            m = pe.matmul(down[:, 0, j * P:(j + 1) * P], hid[:, k, j * P:(j + 1) * P],
                                          w2[:, k, :], start=(k == 0), stop=(k == CH - 1))
                    m.then_inc(down_ready, 1)

            @block.scalar
            def _(act):
                act.wait_ge(weights, 64)
                act.sem_inc(hid_ready, CH)
                act.preload_act_table(ACT.Gelu)
                with act.Fori(0, STEPS) as i:
                    for k in range(CH):
                        up = (up0, up1)[k // 2]
                        act.wait_ge(up_ready, i * CH + k + 1)
                        act.activation(hid[:, k, :], up[:, k % 2, :], ACT.Gelu,
                                       bias=b1[:, k:k + 1]).then_inc(hid_ready, 1)
        clear()


def distance_attention(nc, c, wk_d, wv_d, wo_d, rep_d, sel_d, masks_d):
    HEADS, D = 16, 8
    SCALE = float(np.float32(1) / np.sqrt(np.float32(D)))
    GROUP = 4
    UNITS = B * HEADS // GROUP
    JOBS = TPB * GROUP
    AHEAD = 6
    VALUES = {GROUP * t + 5 + 2 * half + (t + half == 0): (t, half) for t in range(TPB) for half in range(2)}
    SIDES = {10: (0, 0), 12: (0, 1), 20: (1, 0), 22: (1, 1)}
    with ExitStack() as st:
        def sb(name, shape, dt=F32):
            return st.enter_context(nc.sbuf_tensor(c.fresh(name), shape, dt))

        wk = sb("wk", [P, P])
        wo_eff = sb("w_eff", [P, P])
        xT = sb("xT", [P, NT * P])
        sqT = sb("sqT", [P, NT * P])
        q_all = sb("q_all", [P, NT, HEADS, D])
        bias_all = sb("bias_all", [P, NT, HEADS])
        rep = [sb(f"rep{k}", [P, 2, P]) for k in range(2)]
        sel = [sb(f"sel{k}", [P, 2, P]) for k in range(2)]
        masks = sb("masks", [P, 8])
        key_parts = sb("key_parts", [P, S], F32R)
        query = [[sb(f"query{k}{p}", [P, S], F32R) for p in range(2)] for k in range(2)]
        keys = [[sb(f"keys{k}{j}", [P, S], F32R) for j in range(GROUP)] for k in range(2)]
        v = [sb(f"v{k}", [P, TPB, GROUP, 32]) for k in range(2)]
        bias = [sb(f"bias{k}", [P, TPB, GROUP]) for k in range(2)]
        e = [sb(f"e{r}", [P, S]) for r in range(2 * GROUP)]
        oT = sb("oT", [P, S])
        inv = sb("inv", [P, TPB, GROUP])
        ctx_all = sb("ctx_all", [P, NT, P])
        flat = "p a n -> p (a n)"

        normalised_columns(nc, c, xT)

        with ExitStack() as st2:
            sem, clear = semaphores(nc, st2)
            loaded = sem("loaded")
            q_ready = sem("q_ready")
            q_out = sem("q_out")
            qT_ready = sem("qT_ready")
            sqT_ready = sem("sqT_ready")
            sq_ready = sem("sq_ready")
            norm_ready = sem("norm_ready")
            bias_ready = sem("bias_ready")
            cross_ready = sem("cross_ready")
            merged_ready = sem("merged_ready")
            eff_ready = sem("eff_ready")
            eff_out = sem("eff_out")
            v_clear = sem("v_clear")
            wv = st2.enter_context(nc.sbuf_tensor(c.fresh("wv"), [P, P], F32))
            wo = st2.enter_context(nc.sbuf_tensor(c.fresh("wo"), [P, P], F32))
            block_mask = st2.enter_context(nc.sbuf_tensor(c.fresh("block_mask"), [P, P], F32))
            merged = st2.enter_context(nc.sbuf_tensor(c.fresh("merged"), [P, P], F32))
            sq = e[0]
            with nc.Block() as block:
                @block.sync
                def _(sp):
                    sp.dma_start(wk[:], wk_d).then_inc(loaded, 16)
                    sp.dma_start(wv[:], wv_d).then_inc(loaded, 16)
                    sp.dma_start(wo[:], wo_d).then_inc(loaded, 16)
                    sp.dma_start(block_mask[:], c.const["block_mask"]).then_inc(loaded, 16)
                    sp.dma_start(masks[:], masks_d).then_inc(loaded, 16)
                    sp.wait_ge(loaded, 80)

                @block.gpsimd
                def _(pool):
                    for k in range(2):
                        pool.memset(v[k][:], 0.0).then_inc(v_clear, 1)
                    pool.wait_ge(v_clear, 2)
                    for k in range(2):
                        pool.memset(v[k][:, :, :, D:D + 1], 1.0).then_inc(v_clear, 1)

                @block.tensor
                def _(pe):
                    pe.wait_ge(loaded, 80)
                    pe.matmul(c.slots[2][:, 0, 0:P], wv[:], wk[:], start=True, stop=True).then_inc(cross_ready, 1)
                    for b in range(B):
                        if b:
                            pe.wait_ge(q_out, b)
                        for t in range(TPB):
                            m = pe.matmul(c.slots[0][:, t // 4, (t % 4) * P:(t % 4 + 1) * P],
                                          xT[:, (b * TPB + t) * P:(b * TPB + t + 1) * P], wk[:], start=True, stop=True)
                        m.then_inc(q_ready, 1)
                        if b:
                            pe.wait_ge(sqT_ready, b)
                        for half in range(2):
                            m = pe.matmul(c.slots[1][:, half, :], wk[:], xT[:, b * S + half * 512:b * S + half * 512 + 512],
                                          start=True, stop=True)
                        m.then_inc(qT_ready, 1)
                        if b == 0:
                            pe.wait_ge(merged_ready, 1)
                            pe.matmul(c.slots[3][:, 0, 0:P], merged[:], wo[:], start=True, stop=True).then_inc(eff_ready, 1)

                @block.scalar
                def _(act):
                    for b in range(B):
                        act.wait_ge(q_ready, b + 1)
                        act.activation(q_all[:, b * TPB:(b + 1) * TPB, :, :].rearrange("p t h d -> p (t h d)"),
                                       c.slots[0][:].rearrange(flat), ACT.Copy).then_inc(q_out, 1)
                        act.wait_ge(qT_ready, b + 1)
                        act.activation(sqT[:, b * S:(b + 1) * S], c.slots[1][:].rearrange(flat), ACT.Square).then_inc(sqT_ready, 1)

                @block.vector
                def _(dve):
                    dve.wait_ge(cross_ready, 1)
                    dve.wait_ge(loaded, 80)
                    dve.scalar_tensor_tensor(merged[:], c.slots[2][:, 0, 0:P], SCALE, block_mask[:], ALU.mult, ALU.mult)\
                       .then_inc(merged_ready, 1)
                    dve.wait_ge(eff_ready, 1)
                    dve.tensor_copy(wo_eff[:], c.slots[3][:, 0, 0:P]).then_inc(eff_out, 1)
                    for b in range(B):
                        tiles = slice(b * TPB, (b + 1) * TPB)
                        rows = q_all[:, tiles, :, :].rearrange("p t h d -> p (t h d)")
                        dve.wait_ge(q_out, b + 1)
                        if b:
                            dve.wait_ge(norm_ready, b)
                        dve.tensor_tensor(sq[:], rows, rows, ALU.mult).then_inc(sq_ready, 1)
                        dve.wait_ge(sq_ready, b + 1)
                        dve.tensor_reduce(bias_all[:, tiles, :].rearrange("p t h -> p (t h)"),
                                          sq[:].rearrange("p (g d) -> p g d", d=D), AX.X, ALU.add).then_inc(norm_ready, 1)
                    dve.wait_ge(norm_ready, B)
                    dve.tensor_scalar(bias_all[:], bias_all[:], -SCALE, None, ALU.mult).then_inc(bias_ready, 1)
            clear()

        with ExitStack() as st2:
            sem, clear = semaphores(nc, st2)
            w_loaded = sem("w_loaded")
            p_ready = sem("p_ready")
            step_dve = sem("step_dve")
            p_out = sem("p_out")
            sides_ready = sem("sides_ready")
            v_ready = sem("v_ready")
            s_ready = sem("s_ready")
            e_ready = sem("e_ready")
            o_ready = sem("o_ready")
            o_out = sem("o_out")
            oT_ready = sem("oT_ready")
            inv_ready = sem("inv_ready")
            ctx_ready = sem("ctx_ready")

            with nc.Block() as block:
                @block.sync
                def _(sp):
                    def load(u, k):
                        sp.dma_start(rep[k][:], rep_d[bass.ds(u % 4, 1)].rearrange("a p c m -> (a p) c m")).then_inc(w_loaded, 16)
                        sp.dma_start(sel[k][:], sel_d[bass.ds(u % 4, 1)].rearrange("a p c m -> (a p) c m")).then_inc(w_loaded, 16)

                    load(0, 0)
                    with sp.Fori(0, UNITS // 2) as i:
                        for k in range(2):
                            sp.wait_ge(p_ready, 4 * i + 2 * k + 2)
                            load(2 * i + k + 1, 1 - k)

                @block.gpsimd
                def _(pool):
                    def rows(u, k):
                        tiles = bass.ds((u // 4 % B) * TPB, TPB)
                        pool.tensor_copy(v[k][:, :, :, 0:D], q_all[:, tiles, bass.ds(u % 4 * GROUP, GROUP), :]).then_inc(v_ready, 1)
                        pool.tensor_copy(bias[k][:], bias_all[:, tiles, bass.ds(u % 4 * GROUP, GROUP)]).then_inc(v_ready, 1)

                    rows(0, 0)
                    with pool.Fori(0, UNITS // 2) as i:
                        for k in range(2):
                            pool.wait_ge(o_ready, 2 * i + k + 1)
                            rows(2 * i + k + 1, 1 - k)

                @block.tensor
                def _(pe):
                    def sides(u, k, p, half):
                        if p == 0 and half == 0:
                            pe.wait_ge(w_loaded, 32 * u + 32)
                        pe.wait_ge(p_out, 2 * u + p + 1)
                        cols = (u // 4 % B) * S
                        pe.matmul(c.slots[2][:, half, :], rep[k][:, p, :], xT[:, bass.ds(cols + half * 512, 512)],
                                  start=True, stop=False)
                        m = pe.matmul(c.slots[2][:, half, :], sel[k][:, p, :], sqT[:, bass.ds(cols + half * 512, 512)],
                                      start=False, stop=True)
                        if half == 1:
                            m.then_inc(p_ready, 1)

                    def scores(u, k, n):
                        t, j = n % JOBS // GROUP, n % GROUP
                        if n % JOBS in (0, 2):
                            pe.wait_ge(sides_ready, 2 * (u + n // JOBS) + n % JOBS // 2 + 2)
                        pe.wait_ge(e_ready, JOBS * u + n + 1)
                        for half in range(2):
                            m = pe.matmul(c.slots[n % 2][:, half, :], keys[k][j][:, t * P:(t + 1) * P],
                                          query[k][j // 2][:, half * 512:half * 512 + 512], start=True, stop=True)
                        m.then_inc(s_ready, 1)

                    def values(u, k, t, half):
                        pe.wait_ge(e_ready, JOBS * u + 2 + GROUP * t + GROUP)
                        if t == 0 and half == 0:
                            pe.wait_ge(v_ready, 2 * u + 2)
                            pe.wait_ge(ctx_ready, u + 1)
                        for j in range(GROUP):
                            m = pe.matmul(c.slots[3][32 * j:32 * j + 32, half, :], v[k][:, t, j, :],
                                          e[GROUP * (t % 2) + j][:, half * 512:half * 512 + 512],
                                          start=(t == 0), stop=(t == TPB - 1), skip_group_check=True)
                        if t == TPB - 1 and half == 1:
                            m.then_inc(o_ready, 1)

                    def turn(u):
                        pe.wait_ge(o_out, u + 1)
                        for t in range(TPB):
                            m = pe.transpose(c.slots[3][:, t // 4, (t % 4) * P:(t % 4 + 1) * P], oT[:, t * P:(t + 1) * P], c.ident[:])
                        m.then_inc(oT_ready, 1)

                    pe.sem_inc(o_ready, 1)
                    for p in range(2):
                        for half in range(2):
                            sides(0, 0, p, half)
                    for n in range(AHEAD):
                        scores(0, 0, n)
                    with pe.Fori(0, UNITS // 2) as i:
                        for k in range(2):
                            u = 2 * i + k
                            for n in range(AHEAD, JOBS + AHEAD):
                                scores(u, k if n < JOBS else 1 - k, n)
                                if n in VALUES:
                                    values(u, k, *VALUES[n])
                                if n in SIDES:
                                    sides(u + 1, 1 - k, *SIDES[n])
                            turn(u)

                @block.scalar
                def _(act):
                    act.sem_inc(e_ready, 2)
                    act.preload_act_table(ACT.Exp)

                    def exp(u, k, n):
                        t, j = n % JOBS // GROUP, n % GROUP
                        if n % JOBS == 0:
                            act.wait_ge(v_ready, 2 * (u + n // JOBS) + 2)
                        act.wait_ge(s_ready, JOBS * u + n + 1)
                        act.activation(e[n % (2 * GROUP)][:], c.slots[n % 2][:].rearrange(flat), ACT.Exp,
                                       bias=bias[k][:, t, j:j + 1]).then_inc(e_ready, 1)

                    for n in range(AHEAD):
                        exp(0, 0, n)
                    with act.Fori(0, UNITS // 2) as i:
                        for k in range(2):
                            for n in range(AHEAD, JOBS + AHEAD):
                                exp(2 * i + k, k if n < JOBS else 1 - k, n)

                @block.vector
                def _(dve):
                    OWN = 5

                    def sides(u, k, p):
                        slot = c.slots[2][:].rearrange(flat)
                        quarter = query[k][p]
                        own = OWN * (2 * u + p)
                        dve.wait_ge(p_ready, 2 * u + p + 1)
                        dve.wait_ge(sides_ready, 2 * u + p + 1)
                        dve.tensor_scalar(key_parts[:], slot, 2 * SCALE, None, ALU.mult).then_inc(step_dve, 1)
                        dve.tensor_scalar(quarter[:], slot, masks[:, 6:7], None, ALU.mult).then_inc(step_dve, 1)
                        dve.wait_ge(step_dve, own + 1)
                        dve.scalar_tensor_tensor(key_parts[64:P, :], slot[64:P, :], 2 * SCALE, key_parts[64:P, :].bitcast(F32),
                                                 ALU.mult, ALU.subtract).then_inc(step_dve, 1)
                        dve.wait_ge(step_dve, own + 2)
                        for r in (32, 96):
                            dve.scalar_tensor_tensor(quarter[r:r + 32, :], slot[r:r + 32, :], masks[r:r + 32, 6:7],
                                                     quarter[r:r + 32, :].bitcast(F32), ALU.mult, ALU.subtract)\
                               .then_inc(step_dve if r == 32 else p_out, 1)
                        dve.wait_ge(step_dve, own + 3)
                        for j in range(2):
                            m = dve.tensor_scalar(keys[k][2 * p + j][:], key_parts[:].bitcast(F32), masks[:, 2 * j:2 * j + 1],
                                                  masks[:, 2 * j + 1:2 * j + 2], ALU.mult, ALU.add)
                            m.then_inc(step_dve if j == 0 else sides_ready, 1)

                    dve.sem_inc(p_out, 1)
                    dve.sem_inc(ctx_ready, 1)
                    dve.sem_inc(sides_ready, 1)
                    sides(0, 0, 0)
                    sides(0, 0, 1)
                    with dve.Fori(0, UNITS // 2) as i:
                        for k in range(2):
                            u = 2 * i + k
                            sides(u + 1, 1 - k, 0)
                            sides(u + 1, 1 - k, 1)
                            dve.wait_ge(o_ready, u + 2)
                            dve.tensor_copy(oT[:], c.slots[3][:].rearrange(flat)).then_inc(o_out, 1)
                            dve.wait_ge(oT_ready, u + 1)
                            rows = c.slots[3][:].rearrange("p a (t j d) -> p (a t) j d", j=GROUP, d=32)
                            dve.reciprocal(inv[:], rows[:, :, :, D]).then_inc(inv_ready, 1)
                            dve.wait_ge(inv_ready, u + 1)
                            dst = ctx_all[:, bass.ds((u // 4) * TPB, TPB), bass.ds(u % 4 * 32, 32)]
                            dve.tensor_tensor(dst.rearrange("p t (j d) -> p t j d", d=D), rows[:, :, :, 0:D],
                                              inv[:].unsqueeze(3).broadcast_to([P, TPB, GROUP, D]), ALU.mult).then_inc(ctx_ready, 1)
            clear()

        with ExitStack() as st2:
            sem, clear = semaphores(nc, st2)
            turned = sem("turned")
            cT_ready = sem("cT_ready")
            y_ready = sem("y_ready")
            x_ready = sem("x_ready")
            cT = [oT[:, 512 * k:512 * k + 512] for k in range(2)]
            G = 4
            with nc.Block() as block:
                @block.tensor
                def _(pe):
                    for i in range(NT // G + 1):
                        if i < NT // G:
                            if i >= 2:
                                pe.wait_ge(cT_ready, i - 1)
                            for j in range(G):
                                m = pe.transpose(c.slots[i % 2][:, 0, j * P:(j + 1) * P], ctx_all[:, i * G + j, :], c.ident[:])
                            m.then_inc(turned, 1)
                        if i >= 1:
                            pe.wait_ge(cT_ready, i)
                            if i >= 3:
                                pe.wait_ge(x_ready, i - 2)
                            for j in range(G):
                                m = pe.matmul(c.slots[2 + (i - 1) % 2][:, 0, j * P:(j + 1) * P],
                                              cT[(i - 1) % 2][:, j * P:(j + 1) * P], wo_eff[:], start=True, stop=True)
                            m.then_inc(y_ready, 1)

                @block.scalar
                def _(act):
                    for i in range(NT // G):
                        act.wait_ge(turned, i + 1)
                        if i >= 2:
                            act.wait_ge(y_ready, i - 1)
                        act.activation(cT[i % 2], c.slots[i % 2][:, 0, :], ACT.Copy).then_inc(cT_ready, 1)

                @block.vector
                def _(dve):
                    for i in range(NT // G):
                        xs = c.X[:, i * G:(i + 1) * G, :].rearrange("p t d -> p (t d)")
                        dve.wait_ge(y_ready, i + 1)
                        dve.tensor_tensor(xs, c.slots[2 + i % 2][:, 0, :], xs, ALU.add).then_inc(x_ready, 1)
            clear()


def local_layers(nc, c, d):
    HEADS, D, WIN = 8, 64, 64
    PAIRS = HEADS // 2
    G = 4
    STEPS = NT // G
    W = G * P
    CH = 3
    JOBS = ["tq0", "tq1", "tq2", "tq3", "s0", "s1", "s2", "s3", "pt0", "pt1", "pt2", "pt3", "o0", "o1", "o2", "o3",
            "t1", "qk0", "v0", "t2", "qk1", "v1", "hc", "qk2", "v2", "t3", "qk3", "v3", "up0", "up1", "up2", "down"]
    flat = "p a n -> p (a n)"
    FIRST = 0

    def slot(job):
        return c.slots[JOBS.index(job) % 4]

    with ExitStack() as st:
        def sb(name, shape, dt=F32):
            return st.enter_context(nc.sbuf_tensor(c.fresh(name), shape, dt))

        H = sb("H", [P, NT, P])
        w_qk = sb("w_qk", [P, 2 * HEADS * D])
        w_v = sb("w_v", [P, HEADS * D])
        w_o = sb("w_o", [P, PAIRS, P])
        w1 = sb("w1", [P, 2, CH, P])
        w2 = sb("w2", [P, CH, P])
        small = sb("small", [P, 8])
        b2 = sb("b2", [P, P])
        scales = sb("scales", [P, 2, 2, D])
        angles = sb("angles", [P, TPB, 2, 2, D])
        tables = sb("tables", [P, TPB, 2, 2, D])
        centre = sb("centre", [P, P])
        flags = sb("flags", [P, 2])
        band = sb("band", [P, 2, 512], BF16)
        hs = sb("hs", [P, G, P])
        hT = sb("hT", [P, WIN + W + 1])
        sq = [sb(f"sq{k}", [P, 1024]) for k in range(2)]
        cosine = sb("cosine", [P, 1024])
        sine = sb("sine", [P, 1024])
        rot = sb("rot", [P, G, 2 * HEADS, D])
        norm2 = sb("norm2", [P, G, 2 * HEADS])
        norm = sb("norm", [P, G, 2 * HEADS])
        inv_norm = sb("inv_norm", [P, G, 2 * HEADS])
        v = sb("v", [P, G, 2, HEADS * D])
        qT = sb("qT", [P, G, PAIRS, P])
        kz = sb("kz", [P, PAIRS, 2, WIN + W])
        top = sb("top", [P, G, HEADS])
        prob = sb("prob", [P, G, HEADS, P])
        total = sb("total", [P, G, HEADS])
        inv_total = sb("inv_total", [P, G, HEADS])
        probT = sb("probT", [P, G, HEADS, P])
        attn = sb("attn", [P, G, HEADS * D])
        attnT = sb("attnT", [P, G, PAIRS, P])
        h1 = sb("h1", [P, G, P])
        h1_b2 = sb("h1_b2", [P, G, P])
        h1T = sb("h1T", [P, W + 1])
        dev2 = sb("dev2", [P, G])
        dev = sb("dev", [P, G])
        inv_dev = sb("inv_dev", [P, G])
        scrap = sb("scrap", [P, G, P])
        z = sb("z", [P, G, P])
        zT = sb("zT", [P, W])
        gate = [prob[:, k // 2, k % 2 * 4:k % 2 * 4 + 4, :].rearrange("p h k -> p (h k)") for k in range(CH)]
        hid = [prob[:, 2 + k // 2, k % 2 * 4:k % 2 * 4 + 4, :].rearrange("p h k -> p (h k)") for k in range(CH)]

        row_statistics(nc, c)
        with ExitStack() as st2:
            sem, clear = semaphores(nc, st2)
            h_ready = sem("h_ready")
            loaded = sem("loaded")
            zeroed = sem("zeroed")
            band_ready = sem("band_ready")
            with nc.Block() as block:
                @block.sync
                def _(sp):
                    sp.dma_start(angles[:], c.const["angles"]).then_inc(loaded, 16)
                    sp.dma_start(centre[:], c.const["centre"]).then_inc(loaded, 16)
                    sp.dma_start(flags[:], c.const["flags"]).then_inc(loaded, 16)
                    sp.dma_start(sq[0][:], c.const["band"].rearrange(flat)).then_inc(loaded, 16)

                @block.vector
                def _(dve):
                    dve.wait_ge(loaded, 64)
                    dve.tensor_copy(band[:].rearrange(flat), sq[0][:]).then_inc(band_ready, 1)
                    for t in range(NT):
                        normalise(dve, c, t, H[:, t, :]).then_inc(h_ready, 1)

                @block.gpsimd
                def _(pool):
                    pool.memset(hT[:], 0.0).then_inc(zeroed, 1)
                    pool.memset(kz[:], 0.0).then_inc(zeroed, 1)
                    pool.memset(h1T[:], 0.0).then_inc(zeroed, 1)
            clear()

        sem, clear = semaphores(nc, st)
        w_loaded = sem("w_loaded")
        tables_ready = sem("tables_ready")
        hs_ready = sem("hs_ready")
        hT_carried = sem("hT_carried")
        hT_edge = sem("hT_edge")
        t1_ready = sem("t1_ready")
        hT_low = sem("hT_low")
        hT_high = sem("hT_high")
        qk_ready = sem("qk_ready")
        sq_ready = sem("sq_ready")
        norm2_ready = sem("norm2_ready")
        turn_ready = sem("turn_ready")
        rot_ready = sem("rot_ready")
        v_ready = sem("v_ready")
        v_out = sem("v_out")
        norm_ready = sem("norm_ready")
        inv_step = sem("inv_step")
        unit_ready = sem("unit_ready")
        kz_carried = sem("kz_carried")
        tq_ready = sem("tq_ready")
        tq_act = sem("tq_act")
        tq_dve = sem("tq_dve")
        s_ready = sem("s_ready")
        top_ready = sem("top_ready")
        less_top = sem("less_top")
        exp_ready = sem("exp_ready")
        total_ready = sem("total_ready")
        inv_total_ready = sem("inv_total_ready")
        pt_ready = sem("pt_ready")
        probT_ready = sem("probT_ready")
        o_ready = sem("o_ready")
        attn_ready = sem("attn_ready")
        ot_ready = sem("ot_ready")
        attnT_ready = sem("attnT_ready")
        y_ready = sem("y_ready")
        h1_ready = sem("h1_ready")
        h1_b2_ready = sem("h1_b2_ready")
        t2_ready = sem("t2_ready")
        h1T_edge = sem("h1T_edge")
        h1T_low = sem("h1T_low")
        h1T_high = sem("h1T_high")
        hc_ready = sem("hc_ready")
        dev2_ready = sem("dev2_ready")
        dev_ready = sem("dev_ready")
        inv_dev_ready = sem("inv_dev_ready")
        z_ready = sem("z_ready")
        t3_ready = sem("t3_ready")
        zT_ready = sem("zT_ready")
        up_ready = sem("up_ready")
        gate_ready = sem("gate_ready")
        hid_ready = sem("hid_ready")
        down_ready = sem("down_ready")
        layer_out = sem("layer_out")

        def layer(depth):
            with nc.Block() as block:
                @block.sync
                def _(sp):
                    at = bass.ds(depth, 1)
                    sp.dma_start(w_qk[:], d["w_qk"][at].rearrange("a p n -> (a p) n")).then_inc(w_loaded, 16)
                    sp.dma_start(w_v[:], d["w_v"][at].rearrange("a p n -> (a p) n")).then_inc(w_loaded, 16)
                    sp.dma_start(scales[:], d["scales"][at].rearrange("a p x y n -> (a p) x y n")).then_inc(w_loaded, 16)
                    sp.dma_start(w_o[:], d["w_o"][at].rearrange("a p c n -> (a p) c n")).then_inc(w_loaded, 16)
                    sp.dma_start(w1[:], d["w1"][at].rearrange("a p g c n -> (a p) g c n")).then_inc(w_loaded, 16)
                    sp.dma_start(w2[:], d["w2"][at].rearrange("a p c n -> (a p) c n")).then_inc(w_loaded, 16)
                    sp.dma_start(small[:], d["small"][at].rearrange("a p n -> (a p) n")).then_inc(w_loaded, 16)
                    sp.dma_start(b2[:], d["b2"][at].rearrange("a p n -> (a p) n")).then_inc(w_loaded, 16)

                @block.gpsimd
                def _(pool):
                    def before_projections(u):
                        if u is not FIRST:
                            pool.wait_ge(t1_ready, u)
                        pool.tensor_copy(hs[:], H[:, bass.ds(u % STEPS * G, G), :]).then_inc(hs_ready, 1)
                        if u is not FIRST:
                            pool.wait_ge(v_ready, G * u)
                        pool.tensor_tensor(hT[:, WIN:WIN + 1], hT[:, WIN + W:WIN + W + 1],
                                           flags[:, bass.ds(u % 2, 1)], ALU.mult).then_inc(hT_edge, 1)

                    before_projections(FIRST)
                    pool.wait_ge(w_loaded, 128)
                    with pool.Fori(0, STEPS) as i:
                        before_projections(i + 1)
                        pool.wait_ge(h1_ready, G * i + G)
                        pool.wait_ge(layer_out, i + 1)
                        pool.tensor_tensor(h1_b2[:], h1[:], b2[:].unsqueeze(1).broadcast_to([P, G, P]),
                                           ALU.add).then_inc(h1_b2_ready, 1)

                @block.tensor
                def _(pe):
                    def t1(u):
                        pe.wait_ge(hs_ready, u + 1)
                        if u is not FIRST:
                            pe.wait_ge(h1_ready, G * u - 3)
                        for j in range(G):
                            m = pe.transpose(slot("t1")[:, 0, j * P:(j + 1) * P], hs[:, j, :], c.ident[:])
                        m.then_inc(t1_ready, 1)

                    def qkv(u, j):
                        job = f"qk{j}"
                        if j == 0:
                            pe.wait_ge(hT_low, u + 1)
                            pe.wait_ge(hT_high, u + 1)
                            if u is not FIRST:
                                pe.wait_ge(h1_ready, G * u - 2)
                        if j == 3 and u is FIRST:
                            pe.wait_ge(v_out, 1)
                        own = hT[:, WIN + j * P:WIN + (j + 1) * P]
                        for half in range(2):
                            m = pe.matmul(slot(job)[:, half, :], own, w_qk[:, half * 512:half * 512 + 512], start=True, stop=True)
                        m.then_inc(qk_ready, 1)
                        job = f"v{j}"
                        if j == 0 and u is not FIRST:
                            pe.wait_ge(h1_ready, G * u - 1)
                        if j > 0:
                            pe.wait_ge(turn_ready, 3 * (G * u + j))
                        pe.matmul(slot(job)[:, 0, :], hT[:, j * P:j * P + P], w_v[:], start=True, stop=True)
                        pe.matmul(slot(job)[:, 1, :], own, w_v[:], start=True, stop=True).then_inc(v_ready, 1)

                    def attention(i):
                        for j in range(G):
                            job = f"tq{j}"
                            pe.wait_ge(unit_ready, G * i + j + 1)
                            if j == 0:
                                pe.wait_ge(v_out, G * i + G)
                            if j < CH:
                                pe.wait_ge(hid_ready, CH * i + j + 1)
                            else:
                                pe.wait_ge(layer_out, i + 1)
                            for s in range(2 * PAIRS):
                                m = pe.transpose(slot(job)[:, s // PAIRS, (s % PAIRS) * P:(s % PAIRS + 1) * P],
                                                 rot[:, j, 2 * s:2 * s + 2, :].rearrange("p h d -> p (h d)"), c.ident[:])
                            m.then_inc(tq_ready, 1)
                        for j in range(G):
                            job = f"s{j}"
                            pe.wait_ge(tq_act, 2 * (G * i + j) + 2)
                            pe.wait_ge(tq_dve, G * i + j + 1)
                            for bank in range(2):
                                mask = band[:, 1, :] if j else band[:, bass.ds(i % 2, 1), :].rearrange("p a n -> p (a n)")
                                pe.matmul(slot(job)[:, bank, :], c.ident_bf[:], mask, start=True, stop=False,
                                          skip_group_check=True)
                                for p in range(2 * bank, 2 * bank + 2):
                                    for a in range(2):
                                        at = (2 * j + a) * WIN
                                        m = pe.matmul(slot(job)[64 * a:64 * a + 64, bank, (p % 2) * 256:(p % 2) * 256 + 256],
                                                      qT[:, j, p, 64 * a:64 * a + 64], kz[:, p, :, at:at + 2 * WIN],
                                                      start=False, stop=True, skip_group_check=True)
                            m.then_inc(s_ready, 1)
                        for j in range(G):
                            job = f"pt{j}"
                            pe.wait_ge(exp_ready, G * i + j + 1)
                            for h in range(HEADS):
                                m = pe.transpose(slot(job)[:, h // 4, (h % 4) * P:(h % 4 + 1) * P], prob[:, j, h, :], c.ident[:])
                            m.then_inc(pt_ready, 1)
                        for j in range(G):
                            job = f"o{j}"
                            pe.wait_ge(probT_ready, G * i + j + 1)
                            for h in range(HEADS):
                                for a in range(2):
                                    m = pe.matmul(slot(job)[64 * a:64 * a + 64, 0, h * D:(h + 1) * D],
                                                  probT[:, j, h, 64 * a:64 * a + 64], v[:, j, a, h * D:(h + 1) * D],
                                                  start=True, stop=True, skip_group_check=True)
                            m.then_inc(o_ready, 1)
                        for j in range(G):
                            pe.wait_ge(attn_ready, G * i + j + 1)
                            for s in range(PAIRS):
                                m = pe.transpose(slot(f"o{j}")[:, 1, s * P:(s + 1) * P], attn[:, j, s * P:(s + 1) * P], c.ident[:])
                            m.then_inc(ot_ready, 1)
                        for j in range(G):
                            pe.wait_ge(attnT_ready, G * i + j + 1)
                            for s in range(PAIRS):
                                m = pe.matmul(slot(f"o{j}")[:, 0, 0:P], attnT[:, j, s, :], w_o[:, s, :],
                                              start=(s == 0), stop=(s == PAIRS - 1))
                            m.then_inc(y_ready, 1)

                    def t2(i):
                        pe.wait_ge(h1_ready, G * i + G)
                        for j in range(G):
                            m = pe.transpose(slot("t2")[:, 0, j * P:(j + 1) * P], h1[:, j, :], c.ident[:])
                        m.then_inc(t2_ready, 1)

                    def centred(i):
                        pe.wait_ge(h1T_low, i + 1)
                        pe.wait_ge(h1T_high, i + 1)
                        pe.wait_ge(v_out, G * (i + 1) + 1)
                        for j in range(G):
                            m = pe.matmul(slot("hc")[:, 0, j * P:(j + 1) * P], h1T[:, j * P:(j + 1) * P], centre[:],
                                          start=True, stop=True)
                        m.then_inc(hc_ready, 1)

                    def t3(i):
                        pe.wait_ge(z_ready, G * i + G)
                        pe.wait_ge(v_out, G * (i + 1) + 2)
                        for j in range(G):
                            m = pe.transpose(slot("t3")[:, 0, j * P:(j + 1) * P], z[:, j, :], c.ident[:])
                        m.then_inc(t3_ready, 1)

                    def up_down(i):
                        for k in range(CH):
                            job = f"up{k}"
                            if k == 0:
                                pe.wait_ge(zT_ready, i + 1)
                                pe.wait_ge(v_out, G * (i + 1) + 3)
                            if k == 2:
                                pe.wait_ge(turn_ready, 3 * G * (i + 2))
                            for g in (1, 0):
                                m = pe.matmul(slot(job)[:, g, :], w1[:, g, k, :], zT[:], start=True, stop=True)
                            m.then_inc(up_ready, 1)
                        pe.wait_ge(v_out, G * (i + 1) + 4)
                        pe.wait_ge(hid_ready, CH * i + 2 * CH)
                        for j in range(G):
                            for k in range(CH):
                                m = pe.matmul(slot("down")[:, 0, j * P:(j + 1) * P], hid[k][:, j * P:(j + 1) * P], w2[:, k, :],
                                              start=(k == 0), stop=(k == CH - 1))
                        m.then_inc(down_ready, 1)

                    pe.sem_inc(s_ready, 1)
                    pe.wait_ge(w_loaded, 128)
                    t1(FIRST)
                    for j in range(G):
                        qkv(FIRST, j)
                    with pe.Fori(0, STEPS) as i:
                        attention(i)
                        t1(i + 1)
                        qkv(i + 1, 0)
                        t2(i)
                        qkv(i + 1, 1)
                        centred(i)
                        qkv(i + 1, 2)
                        t3(i)
                        qkv(i + 1, 3)
                        up_down(i)

                @block.scalar
                def _(act):
                    def t1(u):
                        if u is not FIRST:
                            act.wait_ge(v_ready, G * u)
                        act.activation(hT[:, 0:WIN], hT[:, W:W + WIN], ACT.Copy).then_inc(hT_carried, 1)
                        act.wait_ge(t1_ready, u + 1)
                        act.wait_ge(hT_carried, u + 1)
                        act.wait_ge(hT_edge, u + 1)
                        act.activation(hT[0:64, WIN:WIN + W], slot("t1")[0:64, 0, :], ACT.Copy).then_inc(hT_low, 1)

                    def qkv(u, j):
                        act.wait_ge(qk_ready, G * u + j + 1)
                        act.wait_ge(norm2_ready, G * u + j + 1)
                        act.activation(sq[j % 2][:], slot(f"qk{j}")[:].rearrange(flat), ACT.Square).then_inc(sq_ready, 1)
                        act.wait_ge(v_ready, G * u + j + 1)
                        act.activation(v[:, j, :, :].rearrange(flat), slot(f"v{j}")[:].rearrange(flat), ACT.Copy).then_inc(v_out, 1)

                    def norms(u):
                        act.wait_ge(norm2_ready, G * u + G + 2)
                        act.activation(norm[:], norm2[:], ACT.Sqrt).then_inc(norm_ready, 1)

                    def attention(i):
                        act.wait_ge(s_ready, G * i + 1)
                        act.activation(kz[:, :, :, 0:WIN], kz[:, :, :, W:W + WIN], ACT.Copy).then_inc(kz_carried, 1)
                        for j in range(G):
                            act.wait_ge(tq_ready, G * i + j + 1)
                            if j == 0:
                                act.wait_ge(kz_carried, i + 1)
                            at = WIN + j * P
                            act.activation(qT[:, j, :, :].rearrange(flat), slot(f"tq{j}")[:, 0, :], ACT.Copy).then_inc(tq_act, 1)
                            act.activation(kz[0:64, :, 0, at:at + P], slot(f"tq{j}")[0:64, 1, :].rearrange("p (s t) -> p s t", t=P),
                                           ACT.Copy).then_inc(tq_act, 1)
                        for j in range(G):
                            act.wait_ge(less_top, G * i + j + 1)
                            rows = prob[:, j, :, :].rearrange(flat)
                            act.activation(rows, rows, ACT.Exp).then_inc(exp_ready, 1)
                        for j in range(G):
                            act.wait_ge(pt_ready, G * i + j + 1)
                            act.activation(probT[:, j, :, :].rearrange(flat), slot(f"pt{j}")[:].rearrange(flat),
                                           ACT.Copy).then_inc(probT_ready, 1)
                        for j in range(G):
                            act.wait_ge(ot_ready, G * i + j + 1)
                            act.activation(attnT[:, j, :, :].rearrange(flat), slot(f"o{j}")[:, 1, :], ACT.Copy).then_inc(attnT_ready, 1)

                    def t2(i):
                        act.wait_ge(t2_ready, i + 1)
                        act.activation(h1T[0:64, 0:W], slot("t2")[0:64, 0, :], ACT.Copy).then_inc(h1T_low, 1)

                    def deviation(i):
                        act.wait_ge(hc_ready, i + 1)
                        act.wait_ge(inv_dev_ready, i + 1)
                        for j in range(G):
                            act.activation(scrap[:, j, :], slot("hc")[:, 0, j * P:(j + 1) * P], ACT.Square,
                                           accum_out=dev2[:, j:j + 1]).then_inc(dev2_ready, 1)
                        act.wait_ge(dev2_ready, G * i + G)
                        act.activation(dev[:], dev2[:], ACT.Sqrt, scale=1.0 / P, bias=c.eps[:]).then_inc(dev_ready, 1)

                    def t3(i):
                        act.wait_ge(t3_ready, i + 1)
                        act.activation(zT[:], slot("t3")[:, 0, :], ACT.Identity, bias=small[:, 1:2], scale=small[:, 0:1])\
                           .then_inc(zT_ready, 1)

                    def gates(i):
                        for k in range(CH):
                            act.wait_ge(up_ready, CH * i + k + 1)
                            act.activation(gate[k], slot(f"up{k}")[:, 1, :], ACT.Gelu,
                                           bias=small[:, 5 + k:6 + k]).then_inc(gate_ready, 1)

                    act.wait_ge(w_loaded, 128)
                    t1(0)
                    for j in range(G):
                        qkv(0, j)
                    norms(0)
                    with act.Fori(0, STEPS) as i:
                        attention(i)
                        t1(i + 1)
                        qkv(i + 1, 0)
                        t2(i)
                        qkv(i + 1, 1)
                        deviation(i)
                        qkv(i + 1, 2)
                        t3(i)
                        qkv(i + 1, 3)
                        gates(i)
                        norms(i + 1)

                @block.vector
                def _(dve):
                    def t1(u):
                        dve.wait_ge(t1_ready, u + 1)
                        dve.wait_ge(hT_carried, u + 1)
                        dve.wait_ge(hT_edge, u + 1)
                        dve.tensor_copy(hT[64:P, WIN + 1:WIN + W + 1], slot("t1")[64:P, 0, :]).then_inc(hT_high, 1)

                    def rotate(u, j):
                        qk = slot(f"qk{j}")[:].rearrange("p a (h d) -> p a h d", d=D)
                        place = bass.ds(u % 2 * G + j, 1)

                        def table(kind, lo, hi):
                            t = tables[:, place, kind, :, lo:hi].rearrange("p x y d -> p (x y) d")
                            return t.unsqueeze(2).broadcast_to([P, 2, HEADS, hi - lo])
                        cos4 = cosine[:].rearrange("p (a h d) -> p a h d", a=2, d=D)
                        sin4 = sine[:].rearrange("p (a h d) -> p a h d", a=2, d=D)
                        dve.wait_ge(sq_ready, G * u + j + 1)
                        dve.wait_ge(rot_ready, G * u + j + 1)
                        dve.tensor_tensor(cos4, qk, table(0, 0, D), ALU.mult).then_inc(turn_ready, 1)
                        dve.tensor_tensor(sin4[:, :, :, 0:32], qk[:, :, :, 32:64], table(1, 0, 32), ALU.mult).then_inc(turn_ready, 1)
                        dve.tensor_tensor(sin4[:, :, :, 32:64], qk[:, :, :, 0:32], table(1, 32, 64), ALU.mult).then_inc(turn_ready, 1)
                        dve.tensor_reduce(norm2[:, j, :], sq[j % 2][:].rearrange("p (h d) -> p h d", d=D), AX.X, ALU.add)\
                           .then_inc(norm2_ready, 1)
                        dve.wait_ge(turn_ready, 3 * (G * u + j) + 3)
                        dve.tensor_tensor(rot[:, j, :, :].rearrange(flat), cosine[:], sine[:], ALU.add).then_inc(rot_ready, 1)

                    def attention(i):
                        dve.wait_ge(norm_ready, i + 1)
                        dve.tensor_scalar(norm[:], norm[:], 1e-12, None, ALU.max).then_inc(inv_step, 1)
                        dve.wait_ge(inv_step, 2 * i + 1)
                        dve.reciprocal(inv_norm[:], norm[:]).then_inc(inv_step, 1)
                        dve.wait_ge(inv_step, 2 * i + 2)
                        for j in range(G):
                            dve.wait_ge(rot_ready, G * i + j + 2)
                            dve.tensor_tensor(rot[:, j, :, :], rot[:, j, :, :], inv_norm[:, j, :].unsqueeze(2).broadcast_to(
                                [P, 2 * HEADS, D]), ALU.mult).then_inc(unit_ready, 1)
                        for j in range(G):
                            dve.wait_ge(tq_ready, G * i + j + 1)
                            if j == 0:
                                dve.wait_ge(kz_carried, i + 1)
                            at = WIN + j * P
                            dve.tensor_copy(kz[64:P, :, 1, at:at + P], slot(f"tq{j}")[64:P, 1, :].rearrange("p (s t) -> p s t", t=P))\
                               .then_inc(tq_dve, 1)
                        for j in range(G):
                            scores = slot(f"s{j}")[:].rearrange("p a (h k) -> p (a h) k", k=P)
                            dve.wait_ge(s_ready, G * i + j + 2)
                            dve.tensor_reduce(top[:, j, :], scores, AX.X, ALU.max).then_inc(top_ready, 1)
                            dve.wait_ge(top_ready, G * i + j + 1)
                            dve.tensor_tensor(prob[:, j, :, :], scores, top[:, j, :].unsqueeze(2).broadcast_to([P, HEADS, P]),
                                              ALU.subtract).then_inc(less_top, 1)
                        for j in range(G):
                            dve.wait_ge(exp_ready, G * i + j + 1)
                            dve.tensor_reduce(total[:, j, :], prob[:, j, :, :], AX.X, ALU.add).then_inc(total_ready, 1)
                            dve.wait_ge(total_ready, G * i + j + 1)
                            dve.reciprocal(inv_total[:, j, :], total[:, j, :]).then_inc(inv_total_ready, 1)
                        for j in range(G):
                            dve.wait_ge(o_ready, G * i + j + 1)
                            dve.wait_ge(inv_total_ready, G * i + j + 1)
                            dve.tensor_tensor(attn[:, j, :].rearrange("p (h d) -> p h d", d=D),
                                              slot(f"o{j}")[:, 0, :].rearrange("p (h d) -> p h d", d=D),
                                              inv_total[:, j, :].unsqueeze(2).broadcast_to([P, HEADS, D]), ALU.mult)\
                               .then_inc(attn_ready, 1)
                        for j in range(G):
                            dve.wait_ge(y_ready, G * i + j + 1)
                            dve.tensor_tensor(h1[:, j, :], slot(f"o{j}")[:, 0, 0:P],
                                              H[:, bass.ds(i * G + j, 1), :].rearrange(flat), ALU.add).then_inc(h1_ready, 1)

                    def t2(i):
                        dve.tensor_tensor(h1T[64:P, 0:1], h1T[64:P, W:W + 1], flags[64:P, bass.ds(i % 2, 1)], ALU.mult)\
                           .then_inc(h1T_edge, 1)
                        dve.wait_ge(h1T_edge, i + 1)
                        dve.wait_ge(t2_ready, i + 1)
                        dve.wait_ge(h1T_low, i + 1)
                        dve.tensor_copy(h1T[64:P, 1:W + 1], slot("t2")[64:P, 0, :]).then_inc(h1T_high, 1)

                    def normalised(i):
                        dve.wait_ge(dev_ready, i + 1)
                        dve.reciprocal(inv_dev[:], dev[:]).then_inc(inv_dev_ready, 1)
                        dve.wait_ge(inv_dev_ready, i + 2)
                        for j in range(G):
                            dve.tensor_scalar(z[:, j, :], slot("hc")[:, 0, j * P:(j + 1) * P], inv_dev[:, j:j + 1], None, ALU.mult)\
                               .then_inc(z_ready, 1)

                    def out(i):
                        for k in range(CH):
                            dve.wait_ge(gate_ready, CH * i + k + 1)
                            dve.scalar_tensor_tensor(hid[k], slot(f"up{k}")[:, 0, :], small[:, 2 + k:3 + k], gate[k],
                                                     ALU.add, ALU.mult).then_inc(hid_ready, 1)
                        dve.wait_ge(down_ready, i + 1)
                        dve.wait_ge(h1_b2_ready, i + 1)
                        dve.tensor_tensor(H[:, bass.ds(i * G, G), :].rearrange(flat), slot("down")[:, 0, :],
                                          h1_b2[:].rearrange(flat), ALU.add).then_inc(layer_out, 1)

                    for s, n in ((norm2_ready, 2), (rot_ready, 1), (inv_dev_ready, 1), (layer_out, 1), (hid_ready, CH)):
                        dve.sem_inc(s, n)
                    dve.wait_ge(w_loaded, 128)
                    dve.tensor_tensor(tables[:].rearrange("p t x y d -> p t (x y d)"), angles[:].rearrange("p t x y d -> p t (x y d)"),
                                      scales[:].rearrange("p x y d -> p (x y d)").unsqueeze(1).broadcast_to([P, TPB, 4 * D]),
                                      ALU.mult).then_inc(tables_ready, 1)
                    dve.wait_ge(tables_ready, 1)
                    t1(0)
                    for j in range(G):
                        rotate(0, j)
                    with dve.Fori(0, STEPS) as i:
                        attention(i)
                        t1(i + 1)
                        rotate(i + 1, 0)
                        t2(i)
                        rotate(i + 1, 1)
                        normalised(i)
                        rotate(i + 1, 2)
                        rotate(i + 1, 3)
                        out(i)
            clear()

        with nc.Fori(0, 2) as depth:
            layer(depth)

        with ExitStack() as st2:
            sem, clear = semaphores(nc, st2, first=200)
            x_ready = sem("x_ready")
            with nc.Block() as block:
                @block.vector
                def _(dve):
                    for b in range(B):
                        tiles = slice(b * TPB, (b + 1) * TPB)
                        xs = c.X[:, tiles, :].rearrange(flat)
                        dve.scalar_tensor_tensor(xs, H[:, tiles, :].rearrange(flat), 0.5, xs, ALU.mult, ALU.add).then_inc(x_ready, 1)
            clear()


def normalised_columns(nc, c, dst, gain=None, shift=None, twice=False):
    G = 4
    STEPS = NT // G
    row_statistics(nc, c, twice)
    with ExitStack() as st:
        xn = st.enter_context(nc.sbuf_tensor(c.fresh("xn"), [P, 2, G, P], F32))
        sem, clear = semaphores(nc, st)
        xn_ready = sem("xn_ready")
        turned = sem("turned")
        columns_ready = sem("columns_ready")
        with nc.Block() as block:
            @block.vector
            def _(dve):
                for i in range(STEPS):
                    if i >= 2:
                        dve.wait_ge(turned, i - 1)
                    for j in range(G):
                        normalise(dve, c, i * G + j, xn[:, i % 2, j, :]).then_inc(xn_ready, 1)

            @block.tensor
            def _(pe):
                for i in range(STEPS):
                    pe.wait_ge(xn_ready, G * (i + 1))
                    if i >= 2:
                        pe.wait_ge(columns_ready, i - 1)
                    for j in range(G):
                        m = pe.transpose(c.slots[i % 2][:, 0, j * P:(j + 1) * P], xn[:, i % 2, j, :], c.ident[:])
                    m.then_inc(turned, 1)

            @block.scalar
            def _(act):
                for i in range(STEPS):
                    act.wait_ge(turned, i + 1)
                    out = dst[:, i * G * P:(i + 1) * G * P]
                    if gain is None:
                        act.activation(out, c.slots[i % 2][:, 0, :], ACT.Copy).then_inc(columns_ready, 1)
                    else:
                        act.activation(out, c.slots[i % 2][:, 0, :], ACT.Identity, bias=shift,
                                       scale=gain).then_inc(columns_ready, 1)
        clear()


def causal_attention(nc, c, gain_d, shift_d, w_d, wo_d, bias_d):
    HEADS, D = 16, 64
    PAIRS = HEADS // 2
    UNITS = B * PAIRS
    JOBS = 2 * TPB
    WIDE = JOBS // 2
    USES = JOBS - WIDE // 2
    RING = 4
    T_LAG, PV_LAG = 3, 5
    AHEAD = PV_LAG + 1
    PROJECT = {8: (0,), 9: (1,), 10: (2,), 11: (3,), 12: (4,), 13: (5, 6), 14: (7, 8), 15: (9,)}
    HALF = S // 2
    flat = "p a n -> p (a n)"

    def tile_of(n):
        return TPB - 1 - n % JOBS // 2

    def bank_uses(n):
        unit, n = n // JOBS, n % JOBS
        return unit * USES + (n if n < WIDE else WIDE + (n - WIDE) // 2)

    with ExitStack() as st:
        def sb(name, shape, dt=F32):
            return st.enter_context(nc.sbuf_tensor(c.fresh(name), shape, dt))

        gain = sb("gain", [P, 1])
        shift = sb("shift", [P, 1])
        bias = sb("bias", [P, P])
        xT = sb("xT", [P, NT * P])
        w = sb("w_qkv", [P, 5, P])
        wo = sb("w_out", [P, P])
        q = [[sb(f"q{k}{h}", [P, S], F32R) for h in range(2)] for k in range(2)]
        k_hi = [[sb(f"k_hi{k}{h}", [P, S], F32R) for h in range(2)] for k in range(2)]
        k_lo = [[sb(f"k_lo{k}{h}", [P, S], F32R) for h in range(2)] for k in range(2)]
        v = [sb(f"v{k}", [P, TPB, P]) for k in range(2)]
        xv = sb("x_batch", [P, S])
        e = [sb(f"e{r}", [P, S]) for r in range(RING)]
        eT = [sb(f"eT{r}", [P, S]) for r in range(RING)]
        nmax = sb("nmax", [P, JOBS])
        total = sb("total", [P, JOBS])
        inv = sb("inv", [P, JOBS])
        oT = sb("oT", [P, S])
        turn = c.slots[2]
        o = c.slots[3]

        with ExitStack() as st2:
            sem2, clear2 = semaphores(nc, st2)
            loaded = sem2("loaded")
            with nc.Block() as block:
                @block.sync
                def _(sp):
                    sp.dma_start(gain[:], gain_d).then_inc(loaded, 16)
                    sp.dma_start(shift[:], shift_d).then_inc(loaded, 16)
                    sp.dma_start(bias[:], bias_d).then_inc(loaded, 16)
                    sp.wait_ge(loaded, 48)
            clear2()
        normalised_columns(nc, c, xT, gain[:], shift[:], twice=True)

        sem, clear = semaphores(nc, st)
        w_loaded = sem("w_loaded")
        wo_loaded = sem("wo_loaded")
        x_ready = sem("x_ready")
        p_ready = sem("p_ready")
        hi_ready = sem("hi_ready")
        lo_ready = sem("lo_ready")
        xv_ready = sem("xv_ready")
        v_ready = sem("v_ready")
        s_ready = sem("s_ready")
        max_ready = sem("max_ready")
        e_ready = sem("e_ready")
        inv_ready = sem("inv_ready")
        scaled_dve = sem("scaled_dve")
        scaled_act = sem("scaled_act")
        turned = [sem("turned_bank0"), sem("turned_bank1")]
        eT_out = [sem("eT_bank0_dve"), sem("eT_bank1_act")]
        o_ready = sem("o_ready")
        oT_ready = sem("oT_ready")
        y_ready = sem("y_ready")

        def pieces(n):
            tiles = tile_of(n) + 1
            return [(0, 0, 4), (1, 4, tiles - 4)] if n % JOBS < WIDE else [(n % 2, 0, tiles)]

        with nc.Block() as block:
            @block.sync
            def _(sp):
                sp.dma_start(w[:], w_d[0]).then_inc(w_loaded, 16)
                with sp.Fori(0, UNITS) as u:
                    sp.wait_ge(y_ready, u + 1)
                    sp.dma_start(wo[:], wo_d[bass.ds(u % PAIRS, 1)].rearrange("a p e -> (a p) e")).then_inc(wo_loaded, 16)
                    sp.wait_ge(p_ready, 10 * u + 10)
                    sp.dma_start(w[:], w_d[bass.ds((u + 1) % PAIRS, 1)].rearrange("a p c e -> (a p) c e")).then_inc(w_loaded, 16)

            @block.tensor
            def _(pe):
                def project(u, m, first=False):
                    if m == 0:
                        pe.wait_ge(w_loaded, 16 * u + 16)
                        pe.wait_ge(xv_ready, u + 1)
                    if m >= 2:
                        pe.wait_ge(lo_ready, 8 * u + m - 1)
                    elif not first:
                        pe.wait_ge(e_ready, JOBS * u - WIDE - 1 + m)
                    out = c.slots[m % 2][:, 1, :]
                    if m < 8:
                        j = pe.matmul(out, w[:, (0, 2, 1, 3)[m // 2], :], xv[:, m % 2 * HALF:(m % 2 + 1) * HALF],
                                      start=True, stop=True)
                    else:
                        for t in range(4):
                            at = (4 * (m - 8) + t) * P
                            j = pe.matmul(out[:, t * P:(t + 1) * P], xv[:, at:at + P], w[:, 4, :], start=True, stop=True)
                    j.then_inc(p_ready, 1)

                def scores(u, n, k, first=False):
                    i, h = tile_of(n), n % 2
                    if n % JOBS < 2:
                        unit = u + n // JOBS
                        pe.wait_ge(lo_ready, 8 * unit + 4 * h + 4)
                        pe.wait_ge(v_ready, 2 * unit + h + 1)
                    if not (first and n < 2):
                        pe.wait_ge(e_ready, JOBS * u + n - 1)
                    qi = q[k][h][:, i * P:(i + 1) * P]
                    for bank in range(i // 4 + 1):
                        lo, hi = bank * 512, min((i + 1) * P, bank * 512 + 512)
                        out = c.slots[h][:, bank, 0:hi - lo]
                        pe.matmul(out, qi, k_hi[k][h][:, lo:hi], start=True, stop=False)
                        if bank == i // 4:
                            pe.matmul(c.slots[h][:, bank, hi - lo - P:hi - lo], c.ident_bf[:], c.causal[:],
                                      start=False, stop=False, skip_group_check=True)
                        m = pe.matmul(out, qi, k_lo[k][h][:, lo:hi], start=False, stop=True)
                    m.then_inc(s_ready, 1)

                def transpose(u, n, first=False):
                    r = n % RING
                    pe.wait_ge((scaled_dve, scaled_act)[n % 2], TPB * u + n // 2 + 1)
                    for bank, at, tiles in pieces(n):
                        if not (first and bank_uses(n) == 0):
                            pe.wait_ge(eT_out[bank], USES * u + bank_uses(n))
                        for t in range(tiles):
                            m = pe.transpose(turn[:, bank, t * P:(t + 1) * P], e[r][:, (at + t) * P:(at + t + 1) * P], c.ident[:])
                        m.then_inc(turned[bank], 1)

                def values(u, n, k):
                    i = tile_of(n)
                    if n == 1:
                        pe.wait_ge(x_ready, u + 1)
                    for bank in range(2):
                        pe.wait_ge(eT_out[bank], USES * u + bank_uses(n) + 1)
                    for t in range(i + 1):
                        for h in range(2):
                            m = pe.matmul(o[64 * h:64 * h + 64, i // 4, (i % 4) * P:(i % 4 + 1) * P],
                                          v[k][:, t, 64 * h:64 * h + 64], eT[(n - 1 + h) % RING][:, t * P:(t + 1) * P],
                                          start=(t == 0), stop=(t == i), skip_group_check=True)
                    if i == 0:
                        m.then_inc(o_ready, 1)

                def output(u):
                    pe.wait_ge(wo_loaded, 16 * u + 16)
                    pe.wait_ge(oT_ready, u + 1)
                    for t in range(TPB):
                        m = pe.matmul(o[:, t // 4, (t % 4) * P:(t % 4 + 1) * P], oT[:, t * P:(t + 1) * P],
                                      wo[:], start=True, stop=True)
                    m.then_inc(y_ready, 1)

                def tick(u, n, k, first=False):
                    scores(u, n, k if n < JOBS else 1 - k, first)
                    if n >= T_LAG:
                        transpose(u, n - T_LAG, first)
                    if n > PV_LAG and (n - PV_LAG) % 2 == 1 and n - PV_LAG < JOBS:
                        values(u, n - PV_LAG, k)
                    for m in PROJECT.get(n, ()):
                        project(u + 1, m)

                pe.sem_inc(y_ready, 1)
                for m in range(10):
                    project(0, m, first=True)
                for n in range(AHEAD):
                    tick(0, n, 0, first=True)
                with pe.Fori(0, UNITS // 2) as pair:
                    for k in range(2):
                        u = 2 * pair + k
                        for n in range(AHEAD, JOBS + AHEAD):
                            tick(u, n, k)
                        output(u)

            @block.vector
            def _(dve):
                def low_part(u, m, k):
                    slot, h = c.slots[m % 2][:, 1, :], m // 4
                    cols = slice(m % 2 * HALF, (m % 2 + 1) * HALF)
                    dve.wait_ge(hi_ready, 8 * u + m + 1)
                    if m // 2 % 2 == 0:
                        dve.scalar_tensor_tensor(q[k][h][64:P, cols], slot[64:P, :], D ** -0.5,
                                                 q[k][h][64:P, cols].bitcast(F32), ALU.mult, ALU.subtract).then_inc(lo_ready, 1)
                    else:
                        dve.tensor_tensor(k_lo[k][h][:, cols], slot, k_hi[k][h][:, cols].bitcast(F32),
                                          ALU.subtract).then_inc(lo_ready, 1)

                def tick(u, n, k):
                    i, h, col = tile_of(n), n % 2, n % JOBS
                    dve.wait_ge(s_ready, JOBS * u + n + 1)
                    dve.tensor_reduce(nmax[:, col:col + 1], c.slots[h][:].rearrange(flat)[:, 0:(i + 1) * P],
                                      AX.X, ALU.max, negate=True).then_inc(max_ready, 1)
                    if n >= T_LAG:
                        evacuate(u, n - T_LAG)
                    last = n - 1
                    for m in PROJECT.get(last, ()):
                        if m < 8:
                            low_part(u + 1, m, 1 - k)
                    if last >= 0:
                        col = last % JOBS
                        dve.wait_ge(e_ready, JOBS * u + last + 1)
                        dve.reciprocal(inv[:, col:col + 1], total[:, col:col + 1]).then_inc(inv_ready, 1)
                        if last % 2 == 0:
                            dve.wait_ge(inv_ready, JOBS * u + last + 1)
                            part = e[last % RING][:, 0:(tile_of(last) + 1) * P]
                            dve.tensor_scalar(part, part, inv[:, col:col + 1], None, ALU.mult).then_inc(scaled_dve, 1)

                def evacuate(u, n):
                    for bank, at, tiles in pieces(n):
                        if bank == 0:
                            dve.wait_ge(turned[0], USES * u + bank_uses(n) + 1)
                            dve.tensor_copy(eT[n % RING][:, at * P:(at + tiles) * P], turn[:, 0, 0:tiles * P]).then_inc(eT_out[0], 1)

                for m in range(8):
                    low_part(0, m, 0)
                for n in range(AHEAD):
                    tick(0, n, 0)
                with dve.Fori(0, UNITS // 2) as pair:
                    for k in range(2):
                        u = 2 * pair + k
                        for n in range(AHEAD, JOBS + AHEAD):
                            tick(u, n, k)
                            if n == JOBS + PV_LAG - 1:
                                dve.wait_ge(o_ready, u + 1)
                                dve.tensor_copy(oT[:], o[:].rearrange(flat)).then_inc(oT_ready, 1)
                        dve.wait_ge(y_ready, u + 2)
                        dve.wait_ge(x_ready, u + 1)
                        xs = c.X[:, bass.ds((u // PAIRS) * TPB, TPB), :].rearrange("p t d -> p (t d)")
                        dve.tensor_tensor(xs, o[:].rearrange(flat), xs, ALU.add).then_inc(x_ready, 1)

            @block.scalar
            def _(act):
                def project_out(u, m, k):
                    slot = c.slots[m % 2][:, 1, :]
                    act.wait_ge(p_ready, 10 * u + m + 1)
                    if m < 8:
                        dst, scale = (q[k][m // 4], D ** -0.5) if m // 2 % 2 == 0 else (k_hi[k][m // 4], 1.0)
                        act.activation(dst[:, m % 2 * HALF:(m % 2 + 1) * HALF], slot, ACT.Copy, scale=scale).then_inc(hi_ready, 1)
                    else:
                        act.activation(v[k][:, 4 * (m - 8):4 * (m - 7), :].rearrange("p t d -> p (t d)"), slot,
                                       ACT.Copy).then_inc(v_ready, 1)

                def tick(u, n, k):
                    i, h, col = tile_of(n), n % 2, n % JOBS
                    last = n - 1
                    for m in PROJECT.get(last, ()):
                        project_out(u + 1, m, 1 - k)
                    if n >= T_LAG:
                        evacuate(u, n - T_LAG)
                    act.wait_ge(max_ready, JOBS * u + n + 1)
                    act.activation(e[n % RING][:, 0:(i + 1) * P], c.slots[h][:].rearrange(flat)[:, 0:(i + 1) * P], ACT.Exp,
                                   bias=nmax[:, col:col + 1], accum_out=total[:, col:col + 1]).then_inc(e_ready, 1)
                    if last > 0 and last % 2 == 1:
                        col = last % JOBS
                        act.wait_ge(inv_ready, JOBS * u + last + 1)
                        part = e[last % RING][:, 0:(tile_of(last) + 1) * P]
                        act.activation(part, part, ACT.Copy, scale=inv[:, col:col + 1]).then_inc(scaled_act, 1)

                def evacuate(u, n):
                    for bank, at, tiles in pieces(n):
                        if bank == 1:
                            act.wait_ge(turned[1], USES * u + bank_uses(n) + 1)
                            act.activation(eT[n % RING][:, at * P:(at + tiles) * P], turn[:, 1, 0:tiles * P],
                                           ACT.Copy).then_inc(eT_out[1], 1)

                act.preload_act_table(ACT.Exp)
                for m in range(10):
                    project_out(0, m, 0)
                for n in range(AHEAD):
                    tick(0, n, 0)
                with act.Fori(0, UNITS // 2) as pair:
                    for k in range(2):
                        for n in range(AHEAD, JOBS + AHEAD):
                            tick(2 * pair + k, n, k)

            @block.gpsimd
            def _(pool):
                wide = bias[:].rearrange("p (t d) -> p t d", t=1).broadcast_to([P, NT, P])
                pool.tensor_tensor(c.X[:], c.X[:], wide, ALU.add).then_inc(x_ready, 1)
                pool.tensor_copy(xv[:], xT[:, 0:S]).then_inc(xv_ready, 1)
                with pool.Fori(0, UNITS) as u:
                    pool.wait_ge(p_ready, 10 * u + 10)
                    pool.tensor_copy(xv[:], xT[:, bass.ds((((u + 1) % UNITS) // PAIRS) * S, S)]).then_inc(xv_ready, 1)
        clear()


def host_constants():
    eye = np.eye(P, dtype=np.float32)
    future = np.triu(np.full((P, P), BIG, np.float32), 1)
    sel = np.zeros((4, P, 2, 4, 32), np.float32)
    for head in range(16):
        sel[head // 4, head * 8:head * 8 + 8, head // 2 % 2, :, 16 + head % 2] = 1
    masks = np.zeros((4, 32, 8), np.float32)
    for j in range(2):
        masks[:, 8 * j:8 * j + 8, 2 * j] = 1
        masks[0:2, 16 + j, 2 * j + 1] = -1
    masks[:, :, 6] = 1
    masks[:, 16:18, 6] = np.float32(1) / np.sqrt(np.float32(8))
    D, WIN = 64, 64
    half = np.arange(0, D, 2, dtype=np.float32)
    inv_freq = np.float32(1) / np.float32(10000) ** (half / np.float32(D))
    t = np.arange(S, dtype=np.float32)
    freqs = (t[:, None] * inv_freq[None, :]).astype(np.float64)
    growth = ((half + 0.4 * D) / (1.4 * D)).astype(np.float64)[None, :] ** ((t - S // 2) / (WIN // 2)).astype(np.float64)[:, None]
    both = [np.stack([8 * f * growth, f / growth], axis=1) for f in (np.cos(freqs), np.sin(freqs))]
    angles = np.stack([np.concatenate([both[0], both[0]], axis=2), np.concatenate([-both[1], both[1]], axis=2)], axis=1)
    angles = angles.astype(np.float32).reshape(TPB, P, 2, 2, D).transpose(1, 0, 2, 3, 4)
    r, k = np.arange(P)[:, None] % WIN, np.arange(2 * WIN)[None, :]
    inside = (k >= r) & (k <= r + WIN)
    first = inside & ((np.arange(P)[:, None] >= WIN) | (k >= WIN))
    band = np.stack([np.tile(np.where(m, np.float32(0), np.float32(BIG)), (1, 4)) for m in (first, inside)], axis=1)
    flags = np.tile(np.array([[0, 1]], np.float32), (P, 1))
    centre = eye - np.float32(1) / np.float32(P)
    block_mask = np.kron(np.eye(16, dtype=np.float32), np.ones((8, 8), np.float32))
    return {"ident": eye, "sel": sel.reshape(4, P, 2, P), "masks": masks.reshape(P, 8), "block_mask": block_mask,
            "angles": np.ascontiguousarray(angles), "band": band.astype(np.float32), "flags": flags,
            "centre": centre, "causal": future}


def load_x(nc, c, x_d):
    with ExitStack() as st:
        future = st.enter_context(nc.sbuf_tensor(c.fresh("future"), [P, P], F32))
        sem, clear = semaphores(nc, st)
        loaded = sem("loaded")
        constants_ready = sem("constants_ready")
        with nc.Block() as block:
            @block.sync
            def _(sp):
                sp.dma_start(c.X[:], x_d.rearrange("(t p) d -> p t d", p=P)).then_inc(loaded, 16)
                sp.dma_start(c.ident[:], c.const["ident"]).then_inc(loaded, 16)
                sp.dma_start(future[:], c.const["causal"]).then_inc(loaded, 16)

            @block.vector
            def _(dve):
                dve.memset(c.eps[:], EPS).then_inc(constants_ready, 1)
                dve.wait_ge(loaded, 48)
                dve.tensor_copy(c.ident_bf[:], c.ident[:]).then_inc(constants_ready, 1)
                dve.tensor_copy(c.causal[:], future[:]).then_inc(constants_ready, 1)
        clear()


def store_x(nc, c, out_d):
    with ExitStack() as st:
        sem, clear = semaphores(nc, st)
        stored = sem("stored")
        with nc.Block() as block:
            @block.sync
            def _(sp):
                sp.dma_start(out_d.rearrange("(t p) d -> p t d", p=P), c.X[:]).then_inc(stored, 16)
                sp.wait_ge(stored, 16)


def open_ctx(nc, st, const):
    c = Ctx()
    c.const = const
    c.count = [0]
    c.X = st.enter_context(nc.sbuf_tensor("X", [P, NT, P], F32))
    c.ident = st.enter_context(nc.sbuf_tensor("ident", [P, P], F32))
    c.ident_bf = st.enter_context(nc.sbuf_tensor("ident_bf", [P, P], BF16))
    c.causal = st.enter_context(nc.sbuf_tensor("causal", [P, P], BF16))
    c.stats = st.enter_context(nc.sbuf_tensor("stats", [P, NT, 6], F32))
    c.moments = st.enter_context(nc.sbuf_tensor("moments", [P, NT, 2], F32))
    c.deviation = st.enter_context(nc.sbuf_tensor("deviation", [P, NT], F32))
    c.second = st.enter_context(nc.sbuf_tensor("second", [P, NT], F32))
    c.rstd = st.enter_context(nc.sbuf_tensor("rstd", [P, NT], F32))
    c.eps = st.enter_context(nc.sbuf_tensor("eps", [P, 1], F32))
    c.slots = [st.enter_context(nc.psum_tensor(f"slot{k}", [P, 2, 512], F32)) for k in range(4)]

    def fresh(name):
        c.count[0] += 1
        return f"{name}_{c.count[0]}"
    c.fresh = fresh
    return c


def causal_layout(w_qkv, w_out):
    q, k, v = (w_qkv[i * 1024:(i + 1) * 1024].reshape(8, 2, 64, P) for i in range(3))
    twice = [np.concatenate([m[:, h], m[:, h]], axis=1) for m in (q, k) for h in range(2)]
    w = np.stack(twice + [v.reshape(8, P, P)], axis=1)
    return np.ascontiguousarray(w.transpose(0, 3, 1, 2)), np.ascontiguousarray(w_out.T.reshape(8, P, P))


def distance_layout(W_k):
    wT = W_k.T.reshape(P, 4, 2, 16)
    rep = np.zeros((4, P, 2, 4, 32), W_k.dtype)
    rep[:, :, :, :, 0:16] = wT.transpose(1, 0, 2, 3)[:, :, :, None, :]
    return rep.reshape(4, P, 2, P)


def local_layout(wqkv, q_scale, k_scale, wo, ln_g, ln_b, w1, b1, w2, b2):
    n, hid, chunks = wqkv.shape[0], w2.shape[1], 3
    half = np.zeros((n, P, 2, chunks * P), w1.dtype)
    half[:, :, 0, :hid], half[:, :, 1, :hid] = w1[:, :, :hid], w1[:, :, hid:]
    bias = np.zeros((n, 2, chunks * P), b1.dtype)
    bias[:, 0, :hid], bias[:, 1, :hid] = b1[:, :hid], b1[:, hid:]
    down = np.zeros((n, chunks * P, P), w2.dtype)
    down[:, :hid] = w2
    small = np.concatenate([ln_g[:, None], ln_b[:, None], bias.reshape(n, 2 * chunks, P)], axis=1).transpose(0, 2, 1)
    qk = np.stack([q_scale, k_scale], axis=1)
    scales = np.stack([qk, np.concatenate([qk[:, :, 32:], qk[:, :, :32]], axis=2)], axis=1)
    return {
        "w_qk": np.ascontiguousarray(wqkv[:, :, :1024]),
        "w_v": np.ascontiguousarray(wqkv[:, :, 1024:]),
        "w_o": np.ascontiguousarray(wo.reshape(n, 4, P, P).transpose(0, 2, 1, 3)),
        "w1": half.reshape(n, P, 2, chunks, P),
        "w2": np.ascontiguousarray(down.reshape(n, chunks, P, P).transpose(0, 2, 1, 3)),
        "small": np.ascontiguousarray(small),
        "b2": np.ascontiguousarray(np.broadcast_to(b2[:, None, :], (n, P, P))),
        "scales": np.ascontiguousarray(np.broadcast_to(scales[:, None], (n, P, 2, 2, 64))),
    }


def macaron(nc, d, out_d):
    with ExitStack() as st:
        c = open_ctx(nc, st, {k[6:]: d[k] for k in d if k.startswith("const_")})
        local = {k[6:]: d[k] for k in d if k.startswith("local_")}
        load_x(nc, c, d["x"])
        gelu_ffn(nc, c, d["ffn_w1"], d["ffn_b1"], d["ffn_w2"], d["ffn_b2"])
        distance_attention(nc, c, d["dist_wk"], d["dist_wv"], d["dist_wo"], d["dist_rep"], c.const["sel"], c.const["masks"])
        gelu_ffn(nc, c, d["ffn_w1"], d["ffn_b1"], d["ffn_w2"], d["ffn_b2"])
        local_layers(nc, c, local)
        causal_attention(nc, c, d["causal_gain"], d["causal_shift"], d["causal_w"], d["causal_wo"], d["causal_bias"])
        local_layers(nc, c, local)
        store_x(nc, c, out_d)


def kernel(**inputs):
    import concourse.bacc as bacc
    from concourse.bass_utils import run_bass_kernel_spmd

    a = {k: np.asarray(v) for k, v in inputs.items()}
    flipped = lambda m: np.ascontiguousarray(m.T)
    rows = lambda r: np.ascontiguousarray(np.broadcast_to(r, (P, r.shape[0])))
    causal_w, causal_wo = causal_layout(a["L1_attn_w_qkv"], a["L1_attn_w_out"])
    names = ["wqkv", "q_scale", "k_scale", "wo", "ln_g", "ln_b", "w1", "b1", "w2", "b2"]
    data = {
        "x": a["L0_attn_x"].reshape(NT * P, P),
        "ffn_w1": a["L0_ffn_w1"], "ffn_b1": flipped(a["L0_ffn_b1"].reshape(-1, P)),
        "ffn_w2": a["L0_ffn_w2"], "ffn_b2": rows(a["L0_ffn_b2"]),
        "dist_wk": flipped(a["L0_attn_W_k"]), "dist_wv": flipped(a["L0_attn_W_v"]),
        "dist_wo": flipped(a["L0_attn_W_o"]), "dist_rep": distance_layout(a["L0_attn_W_k"]),
        "causal_gain": a["L1_attn_ln_gamma"].reshape(P, 1), "causal_shift": a["L1_attn_ln_beta"].reshape(P, 1),
        "causal_w": causal_w, "causal_wo": causal_wo, "causal_bias": rows(a["L1_attn_b_out"]),
    }
    data.update({"local_" + k: v for k, v in local_layout(*[a["L1_ffn_" + n] for n in names]).items()})
    data.update({"const_" + k: v for k, v in host_constants().items()})

    nc = bacc.Bacc("TRN2", target_bir_lowering=False, num_devices=1)
    arrays = {f"in_{k}_dram": np.ascontiguousarray(v) for k, v in data.items()}
    d = {k: nc.dram_tensor(f"in_{k}_dram", v.shape, mybir.dt.from_np(v.dtype), kind="ExternalInput").ap()
         for k, v in data.items()}
    out_d = nc.dram_tensor("out_0_dram", (NT * P, P), F32, kind="ExternalOutput").ap()
    macaron(nc, d, out_d)
    result = run_bass_kernel_spmd(nc, [arrays], core_ids=[0])
    return result.results[0]["out_0_dram"].reshape(B, S, P)
```

```python
from contextlib import ExitStack

import concourse.bass as bass
from concourse import mybir
import numpy as np

F32 = mybir.dt.float32
F32R = mybir.dt.float32r
BF16 = mybir.dt.bfloat16
ALU = mybir.AluOpType
ACT = mybir.ActivationFunctionType
AX = mybir.AxisListType

P = 128
B, S = 4, 1024
TPB = S // P
NT = B * TPB
EPS = 1e-5
BIG = -1e30


class Ctx:
    pass


def semaphores(nc, stack, first=100):
    made = []

    def sem(name):
        made.append(stack.enter_context(nc.semaphore(name, num=first + len(made))))
        return made[-1]

    def clear():
        nc.all_engine_barrier(sems_to_clear=range(first, first + len(made)))
    return sem, clear


def row_statistics(nc, c, twice=False):
    with ExitStack() as st:
        sem, clear = semaphores(nc, st, first=200)
        stats_ready = sem("stats_ready")
        moments_ready = sem("moments_ready")
        deviation_ready = sem("deviation_ready")
        rstd_ready = sem("rstd_ready")
        with nc.Block() as block:
            @block.vector
            def _(dve):
                for t in range(NT):
                    dve.bn_stats(c.stats[:, t, :], c.X[:, t, :]).then_inc(stats_ready, 1)
                for t in range(NT):
                    dve.wait_ge(stats_ready, t + 1)
                    dve.bn_aggr(c.moments[:, t, :], c.stats[:, t, :]).then_inc(moments_ready, 1)
                dve.wait_ge(deviation_ready, 1)
                dve.reciprocal(c.rstd[:], c.deviation[:]).then_inc(rstd_ready, 1)
                if twice:
                    dve.wait_ge(rstd_ready, 1)
                    dve.tensor_tensor(c.second[:], c.moments[:, :, 1], c.rstd[:], ALU.mult).then_inc(rstd_ready, 1)
                    dve.wait_ge(rstd_ready, 2)
                    dve.tensor_tensor(c.second[:], c.second[:], c.rstd[:], ALU.mult).then_inc(rstd_ready, 1)
                    dve.wait_ge(deviation_ready, 2)
                    dve.reciprocal(c.second[:], c.deviation[:]).then_inc(rstd_ready, 1)
                    dve.wait_ge(rstd_ready, 4)
                    dve.tensor_tensor(c.rstd[:], c.rstd[:], c.second[:], ALU.mult).then_inc(rstd_ready, 1)

            @block.scalar
            def _(act):
                act.preload_act_table(ACT.Sqrt)
                act.wait_ge(moments_ready, NT)
                act.activation(c.deviation[:], c.moments[:, :, 1], ACT.Sqrt, bias=c.eps[:]).then_inc(deviation_ready, 1)
                if twice:
                    act.wait_ge(rstd_ready, 3)
                    act.activation(c.deviation[:], c.second[:], ACT.Sqrt, bias=c.eps[:]).then_inc(deviation_ready, 1)
        clear()


def normalise(dve, c, t, dst):
    return dve.tensor_scalar(dst, c.X[:, t, :], c.moments[:, t, 0:1], c.rstd[:, bass.ds(t, 1)], ALU.subtract, ALU.mult)


def gelu_ffn(nc, c, w1_d, b1_d, w2_d, b2_d):
    HID = 512
    CH = HID // P
    G = 4
    W = G * P
    STEPS = NT // G
    with ExitStack() as st:
        def sb(name, shape, dt=F32):
            return st.enter_context(nc.sbuf_tensor(c.fresh(name), shape, dt))

        w1 = sb("w1", [P, HID])
        b1 = sb("b1", [P, CH])
        w2 = sb("w2", [P, CH, P])
        half_b2 = sb("half_b2", [P, P])
        xn = sb("xn", [P, G, P])
        xnT = sb("xnT", [P, W])
        hid = sb("hid", [P, CH, W])
        x_b2 = sb("x_b2", [P, G, P])
        tr, up0, up1, down = c.slots
        sem, clear = semaphores(nc, st)
        weights = sem("weights")
        half_b2_ready = sem("half_b2_ready")
        xn_ready = sem("xn_ready")
        tr_ready = sem("tr_ready")
        xnT_ready = sem("xnT_ready")
        up_ready = sem("up_ready")
        hid_ready = sem("hid_ready")
        down_ready = sem("down_ready")
        x_b2_ready = sem("x_b2_ready")
        x_ready = sem("x_ready")

        with nc.Block() as block:
            @block.sync
            def _(sp):
                sp.dma_start(w1[:], w1_d).then_inc(weights, 16)
                sp.dma_start(b1[:], b1_d).then_inc(weights, 16)
                sp.dma_start(w2[:], w2_d.rearrange("(c p) e -> p c e", p=P)).then_inc(weights, 16)
                sp.dma_start(half_b2[:], b2_d).then_inc(weights, 16)
        row_statistics(nc, c)
        with nc.Block() as block:
            @block.gpsimd
            def _(pool):
                pool.wait_ge(weights, 64)
                pool.tensor_scalar(half_b2[:], half_b2[:], 0.5, None, ALU.mult).then_inc(half_b2_ready, 1)
                pool.wait_ge(half_b2_ready, 1)
                bias = half_b2[:].rearrange("p (g e) -> p g e", g=1).broadcast_to([P, G, P])
                with pool.Fori(0, STEPS) as i:
                    pool.wait_ge(x_ready, i + 1)
                    pool.tensor_tensor(x_b2[:], c.X[:, bass.ds(i * G, G), :], bias, ALU.add).then_inc(x_b2_ready, 1)

            @block.vector
            def _(dve):
                def norm(i):
                    for j in range(G):
                        normalise(dve, c, i * G + j, xn[:, j, :]).then_inc(xn_ready, 1)

                def columns(i):
                    dve.wait_ge(tr_ready, i + 1)
                    dve.tensor_copy(xnT[:], tr[:, 0, :]).then_inc(xnT_ready, 1)

                def sums(i):
                    dve.wait_ge(down_ready, i + 1)
                    dve.wait_ge(x_b2_ready, i + 1)
                    dve.scalar_tensor_tensor(c.X[:, bass.ds(i * G, G), :].rearrange("p g e -> p (g e)"), down[:, 0, :], 0.5,
                                             x_b2[:].rearrange("p g e -> p (g e)"),
                                             ALU.mult, ALU.add).then_inc(x_ready, 1)

                dve.sem_inc(x_ready, 1)
                norm(0)
                columns(0)
                norm(1)
                with dve.Fori(0, STEPS - 2) as i:
                    columns(i + 1)
                    norm(i + 2)
                    sums(i)
                columns(STEPS - 1)
                sums(STEPS - 2)
                sums(STEPS - 1)

            @block.tensor
            def _(pe):
                pe.wait_ge(weights, 64)

                def turn(i):
                    pe.wait_ge(xn_ready, i * G + G)
                    for j in range(G):
                        m = pe.transpose(tr[:, 0, j * P:(j + 1) * P], xn[:, j, :], c.ident[:])
                    m.then_inc(tr_ready, 1)

                def products(i, more):
                    pe.wait_ge(xnT_ready, i + 1)
                    for k in range(CH):
                        up = (up0, up1)[k // 2]
                        pe.wait_ge(hid_ready, i * CH + k + 1)
                        pe.matmul(up[:, k % 2, :], w1[:, k * P:(k + 1) * P], xnT[:],
                                  start=True, stop=True).then_inc(up_ready, 1)
                    if more:
                        turn(i + 1)
                    pe.wait_ge(x_ready, i + 1)
                    for j in range(G):
                        for k in range(CH):
                            if j == 0:
                                pe.wait_ge(hid_ready, i * CH + CH + k + 1)
                            m = pe.matmul(down[:, 0, j * P:(j + 1) * P], hid[:, k, j * P:(j + 1) * P],
                                          w2[:, k, :], start=(k == 0), stop=(k == CH - 1))
                    m.then_inc(down_ready, 1)

                turn(0)
                with pe.Fori(0, STEPS - 1) as i:
                    products(i, True)
                products(STEPS - 1, False)

            @block.scalar
            def _(act):
                act.wait_ge(weights, 64)
                act.sem_inc(hid_ready, CH)
                act.preload_act_table(ACT.Gelu)
                with act.Fori(0, STEPS) as i:
                    for k in range(CH):
                        up = (up0, up1)[k // 2]
                        act.wait_ge(up_ready, i * CH + k + 1)
                        act.activation(hid[:, k, :], up[:, k % 2, :], ACT.Gelu,
                                       bias=b1[:, k:k + 1]).then_inc(hid_ready, 1)
        clear()


def distance_attention(nc, c, wk_d, wv_d, wo_d, rep_d, sel_d, masks_d):
    HEADS, D = 16, 8
    SCALE = float(np.float32(1) / np.sqrt(np.float32(D)))
    GROUP = 4
    UNITS = B * HEADS // GROUP
    JOBS = TPB * GROUP
    AHEAD = 6
    VALUES = {GROUP * t + 5 + 2 * half + (t + half == 0): (t, half) for t in range(TPB) for half in range(2)}
    SIDES = {8: (0, 0), 12: (0, 1), 20: (1, 0), 24: (1, 1)}
    with ExitStack() as st:
        def sb(name, shape, dt=F32):
            return st.enter_context(nc.sbuf_tensor(c.fresh(name), shape, dt))

        wk = sb("wk", [P, P])
        wo_eff = sb("w_eff", [P, P])
        xT = sb("xT", [P, NT * P])
        sqT = sb("sqT", [P, NT * P])
        q_all = sb("q_all", [P, NT, HEADS, D])
        bias_all = sb("bias_all", [P, NT, HEADS])
        rep = [sb(f"rep{k}", [P, 2, P]) for k in range(2)]
        sel = [sb(f"sel{k}", [P, 2, P]) for k in range(2)]
        masks = sb("masks", [P, 8])
        key_parts = sb("key_parts", [P, S], F32R)
        query = [[sb(f"query{k}{p}", [P, S], F32R) for p in range(2)] for k in range(2)]
        keys = [[sb(f"keys{k}{j}", [P, S], F32R) for j in range(GROUP)] for k in range(2)]
        v = [sb(f"v{k}", [P, TPB, GROUP, 32]) for k in range(2)]
        bias = [sb(f"bias{k}", [P, TPB, GROUP]) for k in range(2)]
        e = [sb(f"e{r}", [P, S]) for r in range(2 * GROUP)]
        oT = sb("oT", [P, S])
        inv = sb("inv", [P, TPB, GROUP])
        ctx_all = sb("ctx_all", [P, NT, P])
        flat = "p a n -> p (a n)"

        with ExitStack() as st2:
            sem, clear = semaphores(nc, st2, first=150)
            loaded = sem("loaded")
            q_ready = sem("q_ready")
            q_out = sem("q_out")
            qT_ready = sem("qT_ready")
            sqT_ready = sem("sqT_ready")
            sq_ready = sem("sq_ready")
            norm_ready = sem("norm_ready")
            bias_ready = sem("bias_ready")
            cross_ready = sem("cross_ready")
            merged_ready = sem("merged_ready")
            eff_ready = sem("eff_ready")
            eff_out = sem("eff_out")
            v_clear = sem("v_clear")
            wv = st2.enter_context(nc.sbuf_tensor(c.fresh("wv"), [P, P], F32))
            wo = st2.enter_context(nc.sbuf_tensor(c.fresh("wo"), [P, P], F32))
            block_mask = st2.enter_context(nc.sbuf_tensor(c.fresh("block_mask"), [P, P], F32))
            merged = st2.enter_context(nc.sbuf_tensor(c.fresh("merged"), [P, P], F32))
            sq = e[0]
            with nc.Block() as block:
                @block.sync
                def _(sp):
                    sp.dma_start(wk[:], wk_d).then_inc(loaded, 16)
                    sp.dma_start(wv[:], wv_d).then_inc(loaded, 16)
                    sp.dma_start(wo[:], wo_d).then_inc(loaded, 16)
                    sp.dma_start(block_mask[:], c.const["block_mask"]).then_inc(loaded, 16)
                    sp.dma_start(masks[:], masks_d).then_inc(loaded, 16)
            normalised_columns(nc, c, xT)
            with nc.Block() as block:
                @block.gpsimd
                def _(pool):
                    for k in range(2):
                        pool.memset(v[k][:], 0.0).then_inc(v_clear, 1)
                    pool.wait_ge(v_clear, 2)
                    for k in range(2):
                        pool.memset(v[k][:, :, :, D:D + 1], 1.0).then_inc(v_clear, 1)

                @block.tensor
                def _(pe):
                    pe.wait_ge(loaded, 80)
                    pe.matmul(c.slots[2][:, 0, 0:P], wv[:], wk[:], start=True, stop=True).then_inc(cross_ready, 1)
                    for b in range(B):
                        if b:
                            pe.wait_ge(q_out, b)
                        for t in range(TPB):
                            m = pe.matmul(c.slots[0][:, t // 4, (t % 4) * P:(t % 4 + 1) * P],
                                          xT[:, (b * TPB + t) * P:(b * TPB + t + 1) * P], wk[:], start=True, stop=True)
                        m.then_inc(q_ready, 1)
                        if b:
                            pe.wait_ge(sqT_ready, b)
                        for half in range(2):
                            m = pe.matmul(c.slots[1][:, half, :], wk[:], xT[:, b * S + half * 512:b * S + half * 512 + 512],
                                          start=True, stop=True)
                        m.then_inc(qT_ready, 1)
                        if b == 0:
                            pe.wait_ge(merged_ready, 1)
                            pe.matmul(c.slots[3][:, 0, 0:P], merged[:], wo[:], start=True, stop=True).then_inc(eff_ready, 1)

                @block.scalar
                def _(act):
                    for b in range(B):
                        act.wait_ge(q_ready, b + 1)
                        act.activation(q_all[:, b * TPB:(b + 1) * TPB, :, :].rearrange("p t h d -> p (t h d)"),
                                       c.slots[0][:].rearrange(flat), ACT.Copy).then_inc(q_out, 1)
                        act.wait_ge(qT_ready, b + 1)
                        act.activation(sqT[:, b * S:(b + 1) * S], c.slots[1][:].rearrange(flat), ACT.Square).then_inc(sqT_ready, 1)

                @block.vector
                def _(dve):
                    dve.wait_ge(cross_ready, 1)
                    dve.wait_ge(loaded, 80)
                    dve.scalar_tensor_tensor(merged[:], c.slots[2][:, 0, 0:P], SCALE, block_mask[:], ALU.mult, ALU.mult)\
                       .then_inc(merged_ready, 1)
                    dve.wait_ge(eff_ready, 1)
                    dve.tensor_copy(wo_eff[:], c.slots[3][:, 0, 0:P]).then_inc(eff_out, 1)
                    for b in range(B):
                        tiles = slice(b * TPB, (b + 1) * TPB)
                        rows = q_all[:, tiles, :, :].rearrange("p t h d -> p (t h d)")
                        dve.wait_ge(q_out, b + 1)
                        if b:
                            dve.wait_ge(norm_ready, b)
                        dve.tensor_tensor(sq[:], rows, rows, ALU.mult).then_inc(sq_ready, 1)
                        dve.wait_ge(sq_ready, b + 1)
                        dve.tensor_reduce(bias_all[:, tiles, :].rearrange("p t h -> p (t h)"),
                                          sq[:].rearrange("p (g d) -> p g d", d=D), AX.X, ALU.add).then_inc(norm_ready, 1)
                    dve.wait_ge(norm_ready, B)
                    dve.tensor_scalar(bias_all[:], bias_all[:], -SCALE, None, ALU.mult).then_inc(bias_ready, 1)
            clear()

        with ExitStack() as st2:
            sem, clear = semaphores(nc, st2)
            w_loaded = sem("w_loaded")
            p_ready = sem("p_ready")
            step_dve = sem("step_dve")
            p_out = sem("p_out")
            sides_ready = sem("sides_ready")
            v_ready = sem("v_ready")
            s_ready = sem("s_ready")
            e_ready = sem("e_ready")
            o_ready = sem("o_ready")
            o_out = sem("o_out")
            oT_ready = sem("oT_ready")
            inv_ready = sem("inv_ready")
            ctx_ready = sem("ctx_ready")

            with nc.Block() as block:
                @block.sync
                def _(sp):
                    def load(u, k):
                        sp.dma_start(rep[k][:], rep_d[bass.ds(u % 4, 1)].rearrange("a p c m -> (a p) c m")).then_inc(w_loaded, 16)
                        sp.dma_start(sel[k][:], sel_d[bass.ds(u % 4, 1)].rearrange("a p c m -> (a p) c m")).then_inc(w_loaded, 16)

                    load(0, 0)
                    with sp.Fori(0, UNITS // 2) as i:
                        for k in range(2):
                            sp.wait_ge(p_ready, 4 * i + 2 * k + 2)
                            load(2 * i + k + 1, 1 - k)

                @block.gpsimd
                def _(pool):
                    def rows(u, k):
                        tiles = bass.ds((u // 4 % B) * TPB, TPB)
                        pool.tensor_copy(v[k][:, :, :, 0:D], q_all[:, tiles, bass.ds(u % 4 * GROUP, GROUP), :]).then_inc(v_ready, 1)
                        pool.tensor_copy(bias[k][:], bias_all[:, tiles, bass.ds(u % 4 * GROUP, GROUP)]).then_inc(v_ready, 1)

                    rows(0, 0)
                    with pool.Fori(0, UNITS // 2) as i:
                        for k in range(2):
                            pool.wait_ge(o_ready, 2 * i + k + 1)
                            rows(2 * i + k + 1, 1 - k)

                @block.tensor
                def _(pe):
                    def sides(u, k, p, half):
                        if p == 0 and half == 0:
                            pe.wait_ge(w_loaded, 32 * u + 32)
                        pe.wait_ge(p_out, 2 * u + p + 1)
                        cols = (u // 4 % B) * S
                        pe.matmul(c.slots[2][:, half, :], rep[k][:, p, :], xT[:, bass.ds(cols + half * 512, 512)],
                                  start=True, stop=False)
                        m = pe.matmul(c.slots[2][:, half, :], sel[k][:, p, :], sqT[:, bass.ds(cols + half * 512, 512)],
                                      start=False, stop=True)
                        if half == 1:
                            m.then_inc(p_ready, 1)

                    def scores(u, k, n):
                        t, j = n % JOBS // GROUP, n % GROUP
                        if n % JOBS in (0, 2):
                            pe.wait_ge(sides_ready, 2 * (u + n // JOBS) + n % JOBS // 2 + 2)
                        pe.wait_ge(e_ready, JOBS * u + n + 1)
                        for half in range(2):
                            m = pe.matmul(c.slots[n % 2][:, half, :], keys[k][j][:, t * P:(t + 1) * P],
                                          query[k][j // 2][:, half * 512:half * 512 + 512], start=True, stop=True)
                        m.then_inc(s_ready, 1)

                    def values(u, k, t, half):
                        pe.wait_ge(e_ready, JOBS * u + 2 + GROUP * t + GROUP)
                        if t == 0 and half == 0:
                            pe.wait_ge(v_ready, 2 * u + 2)
                            pe.wait_ge(ctx_ready, u + 1)
                        for j in range(GROUP):
                            m = pe.matmul(c.slots[3][32 * j:32 * j + 32, half, :], v[k][:, t, j, :],
                                          e[GROUP * (t % 2) + j][:, half * 512:half * 512 + 512],
                                          start=(t == 0), stop=(t == TPB - 1), skip_group_check=True)
                        if t == TPB - 1 and half == 1:
                            m.then_inc(o_ready, 1)

                    def turn(u):
                        pe.wait_ge(o_out, u + 1)
                        for t in range(TPB):
                            m = pe.transpose(c.slots[3][:, t // 4, (t % 4) * P:(t % 4 + 1) * P], oT[:, t * P:(t + 1) * P], c.ident[:])
                        m.then_inc(oT_ready, 1)

                    pe.sem_inc(o_ready, 1)
                    for p in range(2):
                        for half in range(2):
                            sides(0, 0, p, half)
                    for n in range(AHEAD):
                        scores(0, 0, n)
                    with pe.Fori(0, UNITS // 2) as i:
                        for k in range(2):
                            u = 2 * i + k
                            for n in range(AHEAD, JOBS + AHEAD):
                                scores(u, k if n < JOBS else 1 - k, n)
                                if n in VALUES:
                                    values(u, k, *VALUES[n])
                                if n in SIDES:
                                    sides(u + 1, 1 - k, *SIDES[n])
                            turn(u)

                @block.scalar
                def _(act):
                    act.sem_inc(e_ready, 2)
                    act.preload_act_table(ACT.Exp)

                    def exp(u, k, n):
                        t, j = n % JOBS // GROUP, n % GROUP
                        if n % JOBS == 0:
                            act.wait_ge(v_ready, 2 * (u + n // JOBS) + 2)
                        act.wait_ge(s_ready, JOBS * u + n + 1)
                        act.activation(e[n % (2 * GROUP)][:], c.slots[n % 2][:].rearrange(flat), ACT.Exp,
                                       bias=bias[k][:, t, j:j + 1]).then_inc(e_ready, 1)

                    for n in range(AHEAD):
                        exp(0, 0, n)
                    with act.Fori(0, UNITS // 2) as i:
                        for k in range(2):
                            for n in range(AHEAD, JOBS + AHEAD):
                                exp(2 * i + k, k if n < JOBS else 1 - k, n)

                @block.vector
                def _(dve):
                    OWN = 5

                    def sides(u, k, p):
                        slot = c.slots[2][:].rearrange(flat)
                        quarter = query[k][p]
                        own = OWN * (2 * u + p)
                        dve.wait_ge(p_ready, 2 * u + p + 1)
                        dve.wait_ge(sides_ready, 2 * u + p + 1)
                        dve.tensor_scalar(key_parts[:], slot, 2 * SCALE, None, ALU.mult).then_inc(step_dve, 1)
                        dve.tensor_scalar(quarter[:], slot, masks[:, 6:7], None, ALU.mult).then_inc(step_dve, 1)
                        dve.wait_ge(step_dve, own + 1)
                        dve.scalar_tensor_tensor(key_parts[64:P, :], slot[64:P, :], 2 * SCALE, key_parts[64:P, :].bitcast(F32),
                                                 ALU.mult, ALU.subtract).then_inc(step_dve, 1)
                        dve.wait_ge(step_dve, own + 2)
                        for r in (32, 96):
                            dve.scalar_tensor_tensor(quarter[r:r + 32, :], slot[r:r + 32, :], masks[r:r + 32, 6:7],
                                                     quarter[r:r + 32, :].bitcast(F32), ALU.mult, ALU.subtract)\
                               .then_inc(step_dve if r == 32 else p_out, 1)
                        dve.wait_ge(step_dve, own + 3)
                        for j in range(2):
                            m = dve.tensor_scalar(keys[k][2 * p + j][:], key_parts[:].bitcast(F32), masks[:, 2 * j:2 * j + 1],
                                                  masks[:, 2 * j + 1:2 * j + 2], ALU.mult, ALU.add)
                            m.then_inc(step_dve if j == 0 else sides_ready, 1)

                    dve.sem_inc(p_out, 1)
                    dve.sem_inc(ctx_ready, 1)
                    dve.sem_inc(sides_ready, 1)
                    sides(0, 0, 0)
                    sides(0, 0, 1)
                    with dve.Fori(0, UNITS // 2) as i:
                        for k in range(2):
                            u = 2 * i + k
                            sides(u + 1, 1 - k, 0)
                            sides(u + 1, 1 - k, 1)
                            dve.wait_ge(o_ready, u + 2)
                            dve.tensor_copy(oT[:], c.slots[3][:].rearrange(flat)).then_inc(o_out, 1)
                            dve.wait_ge(oT_ready, u + 1)
                            rows = c.slots[3][:].rearrange("p a (t j d) -> p (a t) j d", j=GROUP, d=32)
                            dve.reciprocal(inv[:], rows[:, :, :, D]).then_inc(inv_ready, 1)
                            dve.wait_ge(inv_ready, u + 1)
                            dst = ctx_all[:, bass.ds((u // 4) * TPB, TPB), bass.ds(u % 4 * 32, 32)]
                            dve.tensor_tensor(dst.rearrange("p t (j d) -> p t j d", d=D), rows[:, :, :, 0:D],
                                              inv[:].unsqueeze(3).broadcast_to([P, TPB, GROUP, D]), ALU.mult).then_inc(ctx_ready, 1)
            clear()

        with ExitStack() as st2:
            sem, clear = semaphores(nc, st2)
            turned = sem("turned")
            cT_ready = sem("cT_ready")
            y_ready = sem("y_ready")
            x_ready = sem("x_ready")
            cT = [oT[:, 512 * k:512 * k + 512] for k in range(2)]
            G = 4
            with nc.Block() as block:
                @block.tensor
                def _(pe):
                    for i in range(NT // G + 1):
                        if i < NT // G:
                            if i >= 2:
                                pe.wait_ge(cT_ready, i - 1)
                            for j in range(G):
                                m = pe.transpose(c.slots[i % 2][:, 0, j * P:(j + 1) * P], ctx_all[:, i * G + j, :], c.ident[:])
                            m.then_inc(turned, 1)
                        if i >= 1:
                            pe.wait_ge(cT_ready, i)
                            if i >= 3:
                                pe.wait_ge(x_ready, i - 2)
                            for j in range(G):
                                m = pe.matmul(c.slots[2 + (i - 1) % 2][:, 0, j * P:(j + 1) * P],
                                              cT[(i - 1) % 2][:, j * P:(j + 1) * P], wo_eff[:], start=True, stop=True)
                            m.then_inc(y_ready, 1)

                @block.scalar
                def _(act):
                    for i in range(NT // G):
                        act.wait_ge(turned, i + 1)
                        if i >= 2:
                            act.wait_ge(y_ready, i - 1)
                        act.activation(cT[i % 2], c.slots[i % 2][:, 0, :], ACT.Copy).then_inc(cT_ready, 1)

                @block.vector
                def _(dve):
                    for i in range(NT // G):
                        xs = c.X[:, i * G:(i + 1) * G, :].rearrange("p t d -> p (t d)")
                        dve.wait_ge(y_ready, i + 1)
                        dve.tensor_tensor(xs, c.slots[2 + i % 2][:, 0, :], xs, ALU.add).then_inc(x_ready, 1)
            clear()


def local_layers(nc, c, d):
    HEADS, D, WIN = 8, 64, 64
    PAIRS = HEADS // 2
    LONE = 4
    EXPS = LONE + 1
    G = 4
    STEPS = NT // G
    W = G * P
    CH = 3
    JOBS = ["next t1", "tq0", "tq1", "tq2", "tq3", "s0", "s1", "s2", "s3", "next qk0", "pt0", "pt1", "pt2", "pt3",
            "o0", "o1", "o2", "o3", "t2", "next v0", "next qk1", "hc", "next v1", "next qk2", "t3", "next v2",
            "next qk3", "up0", "next v3", "up1", "up2", "down"]
    flat = "p a n -> p (a n)"
    FIRST = 0
    START = [(0, 0), (0, 1), (1, 0), (1, 1), (0, 2), (0, 3), (1, 2), (1, 3)]

    def slot(job):
        return c.slots[JOBS.index(job if job in JOBS else "next " + job) % 4]

    with ExitStack() as st:
        def sb(name, shape, dt=F32):
            return st.enter_context(nc.sbuf_tensor(c.fresh(name), shape, dt))

        H = sb("H", [P, NT, P])
        w_qk = sb("w_qk", [P, 2 * HEADS * D])
        w_v = sb("w_v", [P, HEADS * D])
        w_o = sb("w_o", [P, PAIRS, P])
        w1 = sb("w1", [P, 2, CH, P])
        w2 = sb("w2", [P, CH, P])
        small = sb("small", [P, 8])
        b2 = sb("b2", [P, P])
        scales = sb("scales", [P, 2, 2, D])
        tables = sb("tables", [P, TPB, 2, 2, D])
        centre = sb("centre", [P, P])
        flags = sb("flags", [P, 2])
        band = sb("band", [P, 2, 512], BF16)
        hs = sb("hs", [P, G, P])
        hT = sb("hT", [P, W + 1])
        sq = [sb(f"sq{k}", [P, 1024]) for k in range(2)]
        cosine = [sb(f"cosine{k}", [P, 1024]) for k in range(2)]
        sine = [sb(f"sine{k}", [P, 1024]) for k in range(2)]
        rot = sb("rot", [P, G, 2 * HEADS, D])
        norm2 = sb("norm2", [P, G, 2 * HEADS])
        norm = sb("norm", [P, G, 2 * HEADS])
        inv_norm = sb("inv_norm", [P, G, 2 * HEADS])
        v = sb("v", [P, G, HEADS * D])
        v_mix = sb("v_mix", [P, G + 1, HEADS * D])
        qT = sb("qT", [P, G, PAIRS, P])
        kz = sb("kz", [P, PAIRS, 2, WIN + W])
        top = sb("top", [P, G, HEADS])
        less_top = sb("less_top", [P, G, HEADS])
        prob = sb("prob", [P, G, HEADS, P])
        total = sb("total", [P, G, HEADS])
        inv_total = sb("inv_total", [P, G, HEADS])
        probT = sb("probT", [P, G, HEADS, P])
        attn = sb("attn", [P, G, HEADS * D])
        attnT = sb("attnT", [P, G, PAIRS, P])
        h1 = sb("h1", [P, G, P])
        h1_b2 = sb("h1_b2", [P, G, P])
        h1T = sb("h1T", [P, W + 1])
        dev2 = sb("dev2", [P, G])
        dev = sb("dev", [P, G])
        inv_dev = sb("inv_dev", [P, G])
        zT = sb("zT", [P, W])
        scrap, z = prob[:, 1, 4:8, :], prob[:, 3, 4:8, :]
        gate = [prob[:, k // 2, k % 2 * 4:k % 2 * 4 + 4, :].rearrange("p h k -> p (h k)") for k in range(CH)]
        hid = [prob[:, 2 + k // 2, k % 2 * 4:k % 2 * 4 + 4, :].rearrange("p h k -> p (h k)") for k in range(CH)]

        row_statistics(nc, c)
        with ExitStack() as st2:
            sem, clear = semaphores(nc, st2)
            h_ready = sem("h_ready")
            loaded = sem("loaded")
            zeroed = sem("zeroed")
            band_ready = sem("band_ready")
            with nc.Block() as block:
                @block.sync
                def _(sp):
                    sp.dma_start(centre[:], c.const["centre"]).then_inc(loaded, 16)
                    sp.dma_start(flags[:], c.const["flags"]).then_inc(loaded, 16)
                    sp.dma_start(sq[0][:], c.const["band"].rearrange(flat)).then_inc(loaded, 16)

                @block.vector
                def _(dve):
                    dve.memset(kz[:, 2:PAIRS], 0.0).then_inc(zeroed, 1)
                    for t in range(NT):
                        normalise(dve, c, t, H[:, t, :]).then_inc(h_ready, 1)
                    dve.wait_ge(loaded, 48)
                    dve.tensor_copy(band[:].rearrange(flat), sq[0][:]).then_inc(band_ready, 1)

                @block.gpsimd
                def _(pool):
                    pool.memset(hT[:], 0.0).then_inc(zeroed, 1)
                    pool.memset(kz[:, 0:2], 0.0).then_inc(zeroed, 1)
                    pool.memset(h1T[:], 0.0).then_inc(zeroed, 1)
                    pool.memset(v_mix[:], 0.0).then_inc(zeroed, 1)
            clear()

        sem, clear = semaphores(nc, st)
        w_qk_loaded = sem("w_qk_loaded")
        w_loaded = sem("w_loaded")
        tables_loaded = sem("tables_loaded")
        tables_ready = sem("tables_ready")
        hs_ready = sem("hs_ready")
        hT_edge = sem("hT_edge")
        t1_ready = sem("t1_ready")
        hT_low = sem("hT_low")
        hT_high = sem("hT_high")
        qk_ready = sem("qk_ready")
        sq_ready = sem("sq_ready")
        norm2_ready = sem("norm2_ready")
        turn_ready = sem("turn_ready")
        rot_ready = sem("rot_ready")
        v_ready = sem("v_ready")
        v_out = sem("v_out")
        v_carried = sem("v_carried")
        norm_ready = sem("norm_ready")
        inv_step = sem("inv_step")
        unit_ready = sem("unit_ready")
        kz_carried = sem("kz_carried")
        tq_ready = sem("tq_ready")
        tq_act = sem("tq_act")
        tq_dve = sem("tq_dve")
        s_ready = sem("s_ready")
        top_ready = sem("top_ready")
        less_top_ready = sem("less_top_ready")
        others_ready = sem("others_ready")
        exp_ready = sem("exp_ready")
        total_ready = sem("total_ready")
        inv_total_ready = sem("inv_total_ready")
        pt_ready = sem("pt_ready")
        probT_ready = sem("probT_ready")
        o_ready = sem("o_ready")
        attn_ready = sem("attn_ready")
        ot_ready = sem("ot_ready")
        attnT_ready = sem("attnT_ready")
        y_ready = sem("y_ready")
        h1_ready = sem("h1_ready")
        h1_b2_ready = sem("h1_b2_ready")
        t2_ready = sem("t2_ready")
        h1T_edge = sem("h1T_edge")
        h1T_low = sem("h1T_low")
        h1T_high = sem("h1T_high")
        hc_ready = sem("hc_ready")
        dev2_ready = sem("dev2_ready")
        dev_ready = sem("dev_ready")
        inv_dev_ready = sem("inv_dev_ready")
        z_ready = sem("z_ready")
        t3_ready = sem("t3_ready")
        zT_ready = sem("zT_ready")
        up_ready = sem("up_ready")
        gate_ready = sem("gate_ready")
        hid_ready = sem("hid_ready")
        down_ready = sem("down_ready")
        layer_out = sem("layer_out")

        def layer(depth):
            with nc.Block() as block:
                @block.sync
                def _(sp):
                    at = bass.ds(depth, 1)
                    sp.dma_start(w_qk[:], d["w_qk"][at].rearrange("a p n -> (a p) n")).then_inc(w_qk_loaded, 16)
                    sp.dma_start(w_v[:], d["w_v"][at].rearrange("a p n -> (a p) n")).then_inc(w_loaded, 16)
                    sp.dma_start(w_o[:], d["w_o"][at].rearrange("a p c n -> (a p) c n")).then_inc(w_loaded, 16)
                    sp.dma_start(w1[:], d["w1"][at].rearrange("a p g c n -> (a p) g c n")).then_inc(w_loaded, 16)
                    sp.dma_start(w2[:], d["w2"][at].rearrange("a p c n -> (a p) c n")).then_inc(w_loaded, 16)
                    sp.dma_start(small[:], d["small"][at].rearrange("a p n -> (a p) n")).then_inc(w_loaded, 16)
                    sp.dma_start(b2[:], d["b2"][at].rearrange("a p n -> (a p) n")).then_inc(w_loaded, 16)

                @block.gpsimd
                def _(pool):
                    def before_projections(u):
                        if u is not FIRST:
                            pool.wait_ge(t1_ready, u)
                        pool.tensor_copy(hs[:], H[:, bass.ds(u % STEPS * G, G), :]).then_inc(hs_ready, 1)
                        if u is not FIRST:
                            pool.wait_ge(v_ready, G * u)
                        pool.tensor_tensor(hT[:, 0:1], hT[:, W:W + 1], flags[:, bass.ds(u % 2, 1)], ALU.mult)\
                            .then_inc(hT_edge, 1)

                    def rotated(u, j):
                        pool.wait_ge(turn_ready, 3 * (G * u + j) + 3)
                        pool.tensor_tensor(rot[:, j, :, :].rearrange(flat), cosine[j % 2][:], sine[j % 2][:], ALU.add)\
                            .then_inc(rot_ready, 1)

                    before_projections(FIRST)
                    for j in range(G):
                        rotated(FIRST, j)
                    pool.wait_ge(w_loaded, 96)
                    with pool.Fori(0, STEPS) as i:
                        before_projections(i + 1)
                        for j in range(G):
                            rotated(i + 1, j)
                        pool.wait_ge(layer_out, i + 1)
                        pool.wait_ge(h1_ready, G * i + G)
                        pool.tensor_tensor(h1_b2[:], h1[:], b2[:].unsqueeze(1).broadcast_to([P, G, P]),
                                           ALU.add).then_inc(h1_b2_ready, 1)

                @block.tensor
                def _(pe):
                    def t1(u):
                        pe.wait_ge(hs_ready, u + 1)
                        if u is not FIRST:
                            pe.wait_ge(v_out, 3 * G * u)
                        for j in range(G):
                            m = pe.transpose(slot("t1")[:, 0, j * P:(j + 1) * P], hs[:, j, :], c.ident[:])
                        m.then_inc(t1_ready, 1)

                    def evacuated(i, j):
                        pe.wait_ge(tq_act, 2 * (G * i + j) + 2)
                        pe.wait_ge(tq_dve, G * i + j + 1)

                    def qk(u, j):
                        if j == 0:
                            pe.wait_ge(hT_low, u + 1)
                            pe.wait_ge(hT_high, u + 1)
                        if j == 0 and u is not FIRST:
                            pe.wait_ge(exp_ready, EXPS * (G * (u - 1) + 1))
                        if j >= 2:
                            pe.wait_ge(v_out, 3 * (G * u + j - 1))
                        for half in range(2):
                            m = pe.matmul(slot(f"qk{j}")[:, half, :], hT[:, j * P:(j + 1) * P],
                                          w_qk[:, half * 512:half * 512 + 512], start=True, stop=True)
                        m.then_inc(qk_ready, 1)

                    def values(u, j):
                        if u is FIRST and j >= 2:
                            pe.wait_ge(turn_ready, 3 * (j - 2) + 3)
                        pe.matmul(slot(f"v{j}")[:, 0, :], hT[:, j * P:(j + 1) * P], w_v[:], start=True, stop=True)\
                            .then_inc(v_ready, 1)

                    def attention(i):
                        for j in range(G):
                            job = f"tq{j}"
                            pe.wait_ge(unit_ready, G * i + j + 1)
                            if j < 2:
                                pe.wait_ge(hid_ready, CH * i + j + 2)
                            elif j == 2:
                                pe.wait_ge(layer_out, i + 1)
                            else:
                                pe.wait_ge(hT_low, i + 2)
                                pe.wait_ge(hT_high, i + 2)
                            for s in range(2 * PAIRS):
                                m = pe.transpose(slot(job)[:, s // PAIRS, (s % PAIRS) * P:(s % PAIRS + 1) * P],
                                                 rot[:, j, 2 * s:2 * s + 2, :].rearrange("p h d -> p (h d)"), c.ident[:])
                            m.then_inc(tq_ready, 1)
                        for j in range(G):
                            job = f"s{j}"
                            evacuated(i, j)
                            for bank in range(2):
                                mask = band[:, 1, :] if j else band[:, bass.ds(i % 2, 1), :].rearrange("p a n -> p (a n)")
                                pe.matmul(slot(job)[:, bank, :], c.ident_bf[:], mask, start=True, stop=False,
                                          skip_group_check=True)
                                for p in range(2 * bank, 2 * bank + 2):
                                    heads = slot(job)[:, bank, (p % 2) * 256:(p % 2) * 256 + 256].rearrange("q (h k) -> q h k", k=P)
                                    at = 2 * j * WIN
                                    for lo, key in ((0, at + WIN), (WIN, at)):
                                        pe.matmul(heads[0:64, :, lo:lo + WIN], qT[:, j, p, 0:64], kz[:, p, :, key:key + WIN],
                                                  start=False, stop=True, skip_group_check=True)
                                    m = pe.matmul(heads[64:P, :, :], qT[:, j, p, 64:P], kz[:, p, :, at + WIN:at + 3 * WIN],
                                                  start=False, stop=True, skip_group_check=True)
                            m.then_inc(s_ready, 1)
                        qk(i + 1, 0)
                        for j in range(G):
                            job = f"pt{j}"
                            pe.wait_ge(exp_ready, EXPS * (G * i + min(j + 2, G)))
                            if j == 3:
                                pe.wait_ge(turn_ready, 3 * G * (i + 1) + 3)
                            for h in range(HEADS):
                                m = pe.transpose(slot(job)[:, h // 4, (h % 4) * P:(h % 4 + 1) * P], prob[:, j, h, :], c.ident[:])
                            m.then_inc(pt_ready, 1)
                        for j in range(G):
                            job = f"o{j}"
                            pe.wait_ge(probT_ready, G * i + j + 1)
                            for a in range(2):
                                for h in range(HEADS):
                                    m = pe.matmul(slot(job)[64 * a:64 * a + 64, 0, h * D:(h + 1) * D],
                                                  probT[:, j, h, 64 * a:64 * a + 64], (v_mix, v)[a][:, j, h * D:(h + 1) * D],
                                                  start=True, stop=True, skip_group_check=True)
                            m.then_inc(o_ready, 1)
                        for j in range(G):
                            pe.wait_ge(attn_ready, G * i + j + 1)
                            for s in range(PAIRS):
                                m = pe.transpose(slot(f"o{j}")[:, 1, s * P:(s + 1) * P], attn[:, j, s * P:(s + 1) * P], c.ident[:])
                            m.then_inc(ot_ready, 1)
                        for j in range(G):
                            pe.wait_ge(attnT_ready, G * i + j + 1)
                            for s in range(PAIRS):
                                m = pe.matmul(slot(f"o{j}")[:, 0, 0:P], attnT[:, j, s, :], w_o[:, s, :],
                                              start=(s == 0), stop=(s == PAIRS - 1))
                            m.then_inc(y_ready, 1)

                    def t2(i):
                        pe.wait_ge(h1_ready, G * i + G)
                        for j in range(G):
                            m = pe.transpose(slot("t2")[:, 0, j * P:(j + 1) * P], h1[:, j, :], c.ident[:])
                        m.then_inc(t2_ready, 1)

                    def centred(i):
                        pe.wait_ge(h1T_low, i + 1)
                        pe.wait_ge(h1T_high, i + 1)
                        for j in range(G):
                            m = pe.matmul(slot("hc")[:, 0, j * P:(j + 1) * P], h1T[:, j * P:(j + 1) * P], centre[:],
                                          start=True, stop=True)
                        m.then_inc(hc_ready, 1)

                    def t3(i):
                        pe.wait_ge(z_ready, G * i + G)
                        pe.wait_ge(turn_ready, 3 * (G * (i + 1) + 1) + 3)
                        for j in range(G):
                            m = pe.transpose(slot("t3")[:, 0, j * P:(j + 1) * P], z[:, j, :], c.ident[:])
                        m.then_inc(t3_ready, 1)

                    def up(i, k):
                        if k == 0:
                            pe.wait_ge(zT_ready, i + 1)
                            pe.wait_ge(turn_ready, 3 * (G * (i + 1) + 2) + 3)
                        if k == 1:
                            pe.wait_ge(v_out, 3 * (G * (i + 1) + 3))
                        if k == 2:
                            pe.wait_ge(turn_ready, 3 * (G * (i + 1) + 3) + 3)
                        for g in (1, 0):
                            m = pe.matmul(slot(f"up{k}")[:, g, :], w1[:, g, k, :], zT[:], start=True, stop=True)
                        m.then_inc(up_ready, 1)

                    def down(i):
                        pe.wait_ge(hid_ready, CH * i + 2 * CH)
                        for j in range(G):
                            for k in range(CH):
                                m = pe.matmul(slot("down")[:, 0, j * P:(j + 1) * P], hid[k][:, j * P:(j + 1) * P], w2[:, k, :],
                                              start=(k == 0), stop=(k == CH - 1))
                        m.then_inc(down_ready, 1)

                    pe.sem_inc(s_ready, 1)
                    t1(FIRST)
                    pe.wait_ge(w_qk_loaded, 16)
                    for part, j in START:
                        if part == 1 and j == 0:
                            pe.wait_ge(w_loaded, 96)
                        (values if part else qk)(FIRST, j)
                    with pe.Fori(0, STEPS) as i:
                        t1(i + 1)
                        attention(i)
                        t2(i)
                        values(i + 1, 0)
                        qk(i + 1, 1)
                        centred(i)
                        values(i + 1, 1)
                        qk(i + 1, 2)
                        t3(i)
                        values(i + 1, 2)
                        qk(i + 1, 3)
                        up(i, 0)
                        values(i + 1, 3)
                        up(i, 1)
                        up(i, 2)
                        down(i)

                @block.scalar
                def _(act):
                    act.dma_start(tables[:], c.const["angles"]).then_inc(tables_loaded, 16)
                    act.dma_start(scales[:], d["scales"][bass.ds(depth, 1)].rearrange("a p x y n -> (a p) x y n"))\
                        .then_inc(tables_loaded, 16)

                    def t1(u):
                        act.wait_ge(t1_ready, u + 1)
                        act.wait_ge(hT_edge, u + 1)
                        act.activation(hT[0:64, 0:W], slot("t1")[0:64, 0, :], ACT.Copy).then_inc(hT_low, 1)

                    def squares(u, j):
                        act.wait_ge(qk_ready, G * u + j + 1)
                        act.wait_ge(norm2_ready, G * u + j + 1)
                        act.activation(sq[j % 2][:], slot(f"qk{j}")[:].rearrange(flat), ACT.Square).then_inc(sq_ready, 1)

                    def values(u, j):
                        if j == 0:
                            act.activation(v_mix[64:P, 0, :], v_mix[64:P, G, :], ACT.Copy).then_inc(v_carried, 1)
                        act.wait_ge(v_ready, G * u + j + 1)
                        own = slot(f"v{j}")[:, 0, :]
                        act.activation(v_mix[0:64, j, :], own[0:64, :], ACT.Copy).then_inc(v_out, 1)
                        if j == G - 1:
                            act.wait_ge(v_carried, u + 1)
                        act.activation(v_mix[64:P, j + 1, :], own[64:P, :], ACT.Copy).then_inc(v_out, 1)
                        act.activation(v[:, j, :], own, ACT.Copy).then_inc(v_out, 1)

                    def norms(u):
                        act.wait_ge(norm2_ready, G * u + G + 2)
                        act.activation(norm[:], norm2[:], ACT.Sqrt).then_inc(norm_ready, 1)

                    def attention(i):
                        act.wait_ge(s_ready, G * i + 1)
                        act.activation(kz[:, :, :, 0:WIN], kz[:, :, :, W:W + WIN], ACT.Copy).then_inc(kz_carried, 1)
                        for j in range(G):
                            act.wait_ge(tq_ready, G * i + j + 1)
                            if j == 0:
                                act.wait_ge(kz_carried, i + 1)
                            at = WIN + j * P
                            act.activation(qT[:, j, :, :].rearrange(flat), slot(f"tq{j}")[:, 0, :], ACT.Copy).then_inc(tq_act, 1)
                            act.activation(kz[0:64, :, 0, at:at + P], slot(f"tq{j}")[0:64, 1, :].rearrange("p (s t) -> p s t", t=P),
                                           ACT.Copy).then_inc(tq_act, 1)
                        for j in range(G):
                            if j == G - 1:
                                squares(i + 1, 0)
                            act.wait_ge(less_top_ready, G * i + j + 1)
                            for h in range(LONE):
                                act.activation(prob[:, j, h, :], slot(f"s{j}")[:, h // 4, (h % 4) * P:(h % 4 + 1) * P], ACT.Exp,
                                               bias=less_top[:, j, h:h + 1], scale=inv_norm[:, j, h:h + 1],
                                               accum_out=total[:, j, h:h + 1]).then_inc(exp_ready, 1)
                            act.wait_ge(others_ready, G * i + j + 1)
                            others = prob[:, j, LONE:HEADS, :].rearrange(flat)
                            act.activation(others, others, ACT.Exp).then_inc(exp_ready, 1)
                        for j in range(G):
                            act.wait_ge(pt_ready, G * i + j + 1)
                            act.activation(probT[:, j, :, :].rearrange(flat), slot(f"pt{j}")[:].rearrange(flat),
                                           ACT.Copy).then_inc(probT_ready, 1)
                        for j in range(G):
                            act.wait_ge(ot_ready, G * i + j + 1)
                            act.activation(attnT[:, j, :, :].rearrange(flat), slot(f"o{j}")[:, 1, :], ACT.Copy).then_inc(attnT_ready, 1)

                    def t2(i):
                        act.wait_ge(t2_ready, i + 1)
                        act.activation(h1T[0:64, 0:W], slot("t2")[0:64, 0, :], ACT.Copy).then_inc(h1T_low, 1)

                    def deviation(i):
                        act.wait_ge(hc_ready, i + 1)
                        act.wait_ge(inv_dev_ready, i + 1)
                        for j in range(G):
                            act.activation(scrap[:, j, :], slot("hc")[:, 0, j * P:(j + 1) * P], ACT.Square,
                                           accum_out=dev2[:, j:j + 1]).then_inc(dev2_ready, 1)
                        act.wait_ge(dev2_ready, G * i + G)
                        act.activation(dev[:], dev2[:], ACT.Sqrt, scale=1.0 / P, bias=c.eps[:]).then_inc(dev_ready, 1)

                    def t3(i):
                        act.wait_ge(t3_ready, i + 1)
                        act.activation(zT[:], slot("t3")[:, 0, :], ACT.Identity, bias=small[:, 1:2], scale=small[:, 0:1])\
                           .then_inc(zT_ready, 1)

                    def gates(i, k):
                        act.wait_ge(up_ready, CH * i + k + 1)
                        act.activation(gate[k], slot(f"up{k}")[:, 1, :], ACT.Gelu,
                                       bias=small[:, 5 + k:6 + k]).then_inc(gate_ready, 1)

                    t1(0)
                    for part, j in START:
                        (values if part else squares)(0, j)
                    norms(0)
                    act.wait_ge(w_loaded, 96)
                    with act.Fori(0, STEPS) as i:
                        t1(i + 1)
                        attention(i)
                        t2(i)
                        values(i + 1, 0)
                        squares(i + 1, 1)
                        deviation(i)
                        values(i + 1, 1)
                        squares(i + 1, 2)
                        t3(i)
                        values(i + 1, 2)
                        squares(i + 1, 3)
                        gates(i, 0)
                        values(i + 1, 3)
                        gates(i, 1)
                        gates(i, 2)
                        norms(i + 1)

                @block.vector
                def _(dve):
                    def t1(u):
                        dve.wait_ge(t1_ready, u + 1)
                        dve.wait_ge(hT_edge, u + 1)
                        dve.tensor_copy(hT[64:P, 1:W + 1], slot("t1")[64:P, 0, :]).then_inc(hT_high, 1)

                    def rotate(u, j):
                        qk = slot(f"qk{j}")[:].rearrange("p a (h d) -> p a h d", d=D)
                        place = bass.ds(u % 2 * G + j, 1)

                        def table(kind, lo, hi):
                            t = tables[:, place, kind, :, lo:hi].rearrange("p x y d -> p (x y) d")
                            return t.unsqueeze(2).broadcast_to([P, 2, HEADS, hi - lo])
                        cos4 = cosine[j % 2][:].rearrange("p (a h d) -> p a h d", a=2, d=D)
                        sin4 = sine[j % 2][:].rearrange("p (a h d) -> p a h d", a=2, d=D)
                        dve.wait_ge(sq_ready, G * u + j + 1)
                        dve.wait_ge(rot_ready, G * u + j + 1)
                        dve.tensor_tensor(cos4, qk, table(0, 0, D), ALU.mult).then_inc(turn_ready, 1)
                        dve.tensor_tensor(sin4[:, :, :, 0:32], qk[:, :, :, 32:64], table(1, 0, 32), ALU.mult).then_inc(turn_ready, 1)
                        dve.tensor_tensor(sin4[:, :, :, 32:64], qk[:, :, :, 0:32], table(1, 32, 64), ALU.mult).then_inc(turn_ready, 1)
                        dve.tensor_reduce(norm2[:, j, :], sq[j % 2][:].rearrange("p (h d) -> p h d", d=D), AX.X, ALU.add)\
                           .then_inc(norm2_ready, 1)

                    def inverse_norms(u):
                        dve.wait_ge(norm_ready, u + 1)
                        dve.tensor_scalar(norm[:], norm[:], 1e-12, None, ALU.max).then_inc(inv_step, 1)
                        dve.wait_ge(inv_step, 2 * u + 1)
                        dve.reciprocal(inv_norm[:], norm[:]).then_inc(inv_step, 1)
                        dve.wait_ge(inv_step, 2 * u + 2)

                    def unit_rows(u, j):
                        dve.wait_ge(rot_ready, G * u + j + 3)
                        rows = rot[:, j, LONE:2 * HEADS, :]
                        dve.tensor_tensor(rows, rows, inv_norm[:, j, LONE:2 * HEADS].unsqueeze(2).broadcast_to(
                            [P, 2 * HEADS - LONE, D]), ALU.mult).then_inc(unit_ready, 1)

                    def attention(i):
                        for j in range(G):
                            dve.wait_ge(tq_ready, G * i + j + 1)
                            if j == 0:
                                dve.wait_ge(kz_carried, i + 1)
                            at = WIN + j * P
                            dve.tensor_copy(kz[64:P, :, 1, at:at + P], slot(f"tq{j}")[64:P, 1, :].rearrange("p (s t) -> p s t", t=P))\
                               .then_inc(tq_dve, 1)
                        for j in range(G):
                            scores = slot(f"s{j}")[:].rearrange("p a (h k) -> p (a h) k", k=P)
                            dve.wait_ge(s_ready, G * i + j + 2)
                            dve.tensor_reduce(top[:, j, :], scores, AX.X, ALU.max).then_inc(top_ready, 1)
                            dve.wait_ge(top_ready, G * i + j + 1)
                            dve.scalar_tensor_tensor(less_top[:, j, :], top[:, j, :], -1.0, inv_norm[:, j, 0:HEADS],
                                                     ALU.mult, ALU.mult).then_inc(less_top_ready, 1)
                            dve.tensor_tensor(prob[:, j, LONE:HEADS, :], scores[:, LONE:HEADS, :], top[:, j, LONE:HEADS]
                                              .unsqueeze(2).broadcast_to([P, HEADS - LONE, P]), ALU.subtract).then_inc(others_ready, 1)
                        rotate(i + 1, 0)
                        for j in range(G):
                            dve.wait_ge(exp_ready, EXPS * (G * i + j + 1))
                            dve.tensor_reduce(total[:, j, LONE:HEADS], prob[:, j, LONE:HEADS, :], AX.X, ALU.add).then_inc(total_ready, 1)
                            dve.wait_ge(total_ready, G * i + j + 1)
                            dve.reciprocal(inv_total[:, j, :], total[:, j, :]).then_inc(inv_total_ready, 1)
                        for j in range(G):
                            dve.wait_ge(o_ready, G * i + j + 1)
                            dve.wait_ge(inv_total_ready, G * i + j + 1)
                            dve.tensor_tensor(attn[:, j, :].rearrange("p (h d) -> p h d", d=D),
                                              slot(f"o{j}")[:, 0, :].rearrange("p (h d) -> p h d", d=D),
                                              inv_total[:, j, :].unsqueeze(2).broadcast_to([P, HEADS, D]), ALU.mult)\
                               .then_inc(attn_ready, 1)
                        for j in range(G):
                            dve.wait_ge(y_ready, G * i + j + 1)
                            dve.tensor_tensor(h1[:, j, :], slot(f"o{j}")[:, 0, 0:P],
                                              H[:, bass.ds(i * G + j, 1), :].rearrange(flat), ALU.add).then_inc(h1_ready, 1)

                    def t2(i):
                        dve.tensor_tensor(h1T[64:P, 0:1], h1T[64:P, W:W + 1], flags[64:P, bass.ds(i % 2, 1)], ALU.mult)\
                           .then_inc(h1T_edge, 1)
                        dve.wait_ge(h1T_edge, i + 1)
                        dve.wait_ge(t2_ready, i + 1)
                        dve.wait_ge(h1T_low, i + 1)
                        dve.tensor_copy(h1T[64:P, 1:W + 1], slot("t2")[64:P, 0, :]).then_inc(h1T_high, 1)

                    def normalised(i):
                        dve.wait_ge(dev_ready, i + 1)
                        dve.reciprocal(inv_dev[:], dev[:]).then_inc(inv_dev_ready, 1)
                        dve.wait_ge(inv_dev_ready, i + 2)
                        for j in range(G):
                            dve.tensor_scalar(z[:, j, :], slot("hc")[:, 0, j * P:(j + 1) * P], inv_dev[:, j:j + 1], None, ALU.mult)\
                               .then_inc(z_ready, 1)

                    def hidden(i):
                        for k in range(CH):
                            dve.wait_ge(gate_ready, CH * i + k + 1)
                            dve.scalar_tensor_tensor(hid[k], slot(f"up{k}")[:, 0, :], small[:, 2 + k:3 + k], gate[k],
                                                     ALU.add, ALU.mult).then_inc(hid_ready, 1)

                    def out(i):
                        dve.wait_ge(down_ready, i + 1)
                        dve.wait_ge(h1_b2_ready, i + 1)
                        dve.tensor_tensor(H[:, bass.ds(i * G, G), :].rearrange(flat), slot("down")[:, 0, :],
                                          h1_b2[:].rearrange(flat), ALU.add).then_inc(layer_out, 1)

                    dve.sem_inc(norm2_ready, 2)
                    dve.sem_inc(rot_ready, 2)
                    dve.sem_inc(inv_dev_ready, 1)
                    dve.sem_inc(layer_out, 1)
                    dve.sem_inc(hid_ready, CH)
                    t1(0)
                    dve.wait_ge(tables_loaded, 32)
                    dve.tensor_tensor(tables[:].rearrange("p t x y d -> p t (x y d)"), tables[:].rearrange("p t x y d -> p t (x y d)"),
                                      scales[:].rearrange("p x y d -> p (x y d)").unsqueeze(1).broadcast_to([P, TPB, 4 * D]),
                                      ALU.mult).then_inc(tables_ready, 1)
                    dve.wait_ge(tables_ready, 1)
                    for j in range(G):
                        rotate(0, j)
                    inverse_norms(0)
                    for j in range(G):
                        unit_rows(0, j)
                    dve.wait_ge(w_loaded, 96)
                    with dve.Fori(0, STEPS) as i:
                        t1(i + 1)
                        attention(i)
                        t2(i)
                        rotate(i + 1, 1)
                        normalised(i)
                        rotate(i + 1, 2)
                        rotate(i + 1, 3)
                        hidden(i)
                        inverse_norms(i + 1)
                        unit_rows(i + 1, 0)
                        unit_rows(i + 1, 1)
                        out(i)
                        unit_rows(i + 1, 2)
                        unit_rows(i + 1, 3)
            clear()

        with nc.Fori(0, 2) as depth:
            layer(depth)

        with ExitStack() as st2:
            sem, clear = semaphores(nc, st2, first=200)
            x_ready = sem("x_ready")
            with nc.Block() as block:
                @block.vector
                def _(dve):
                    for b in range(B):
                        tiles = slice(b * TPB, (b + 1) * TPB)
                        xs = c.X[:, tiles, :].rearrange(flat)
                        dve.scalar_tensor_tensor(xs, H[:, tiles, :].rearrange(flat), 0.5, xs, ALU.mult, ALU.add).then_inc(x_ready, 1)
            clear()


def normalised_columns(nc, c, dst, gain=None, shift=None, twice=False, loaded=None):
    G = 4
    STEPS = NT // G
    row_statistics(nc, c, twice)
    with ExitStack() as st:
        xn = st.enter_context(nc.sbuf_tensor(c.fresh("xn"), [P, 2, G, P], F32))
        sem, clear = semaphores(nc, st)
        xn_ready = sem("xn_ready")
        turned = sem("turned")
        columns_ready = sem("columns_ready")
        with nc.Block() as block:
            @block.vector
            def _(dve):
                for i in range(STEPS):
                    if i >= 2:
                        dve.wait_ge(turned, i - 1)
                    for j in range(G):
                        normalise(dve, c, i * G + j, xn[:, i % 2, j, :]).then_inc(xn_ready, 1)

            @block.tensor
            def _(pe):
                for i in range(STEPS):
                    pe.wait_ge(xn_ready, G * (i + 1))
                    if i >= 2:
                        pe.wait_ge(columns_ready, i - 1)
                    for j in range(G):
                        m = pe.transpose(c.slots[i % 2][:, 0, j * P:(j + 1) * P], xn[:, i % 2, j, :], c.ident[:])
                    m.then_inc(turned, 1)

            @block.scalar
            def _(act):
                if loaded:
                    act.wait_ge(*loaded)
                for i in range(STEPS):
                    act.wait_ge(turned, i + 1)
                    out = dst[:, i * G * P:(i + 1) * G * P]
                    if gain is None:
                        act.activation(out, c.slots[i % 2][:, 0, :], ACT.Copy).then_inc(columns_ready, 1)
                    else:
                        act.activation(out, c.slots[i % 2][:, 0, :], ACT.Identity, bias=shift,
                                       scale=gain).then_inc(columns_ready, 1)
        clear()


def causal_attention(nc, c, gain_d, shift_d, w_d, wo_d, bias_d):
    HEADS, D = 16, 64
    PAIRS = HEADS // 2
    UNITS = B * PAIRS
    JOBS = 2 * TPB
    WIDE = JOBS // 2
    USES = JOBS - WIDE // 2
    RING = 8
    T_LAG, PV_LAG = 3, 7
    AHEAD = PV_LAG + 1
    PROJECT = {8: (0,), 9: (1,), 10: (2,), 11: (3,), 12: (4,), 13: (5,)}
    PARTS = (0, 2, 4, 8, 12)
    HALF = S // 2
    flat = "p a n -> p (a n)"

    def tile_of(n):
        return TPB - 1 - n % JOBS // 2

    def bank_uses(n):
        unit, n = n // JOBS, n % JOBS
        return unit * USES + (n if n < WIDE else WIDE + (n - WIDE) // 2)

    with ExitStack() as st:
        def sb(name, shape, dt=F32):
            return st.enter_context(nc.sbuf_tensor(c.fresh(name), shape, dt))

        gain = sb("gain", [P, 1])
        shift = sb("shift", [P, 1])
        bias = sb("bias", [P, P])
        xT = sb("xT", [P, NT * P])
        w = sb("w_qkv", [P, 3, P])
        wo = sb("w_out", [P, P])
        q = [[sb(f"q{k}{h}", [P, S], F32R) for h in range(2)] for k in range(2)]
        k_hi = [[sb(f"k_hi{k}{h}", [P, S], F32R) for h in range(2)] for k in range(2)]
        k_lo = [[sb(f"k_lo{k}{h}", [P, S], F32R) for h in range(2)] for k in range(2)]
        v = [sb(f"v{k}", [P, TPB, P]) for k in range(2)]
        xv = sb("x_batch", [P, S])
        e = [sb(f"e{r}", [P, S]) for r in range(RING)]
        eT = [sb(f"eT{r}", [P, S]) for r in range(RING)]
        nmax = sb("nmax", [P, JOBS])
        total = sb("total", [P, JOBS])
        inv = sb("inv", [P, JOBS])
        oT = sb("oT", [P, S])
        turn = c.slots[2]
        o = c.slots[3]

        with ExitStack() as st2:
            sem, clear = semaphores(nc, st2, first=150)
            loaded = sem("loaded")
            with nc.Block() as block:
                @block.sync
                def _(sp):
                    sp.dma_start(gain[:], gain_d).then_inc(loaded, 16)
                    sp.dma_start(shift[:], shift_d).then_inc(loaded, 16)
                    sp.dma_start(bias[:], bias_d).then_inc(loaded, 16)
            normalised_columns(nc, c, xT, gain[:], shift[:], twice=True, loaded=(loaded, 48))
            clear()

        sem, clear = semaphores(nc, st)
        w_loaded = sem("w_loaded")
        wo_loaded = sem("wo_loaded")
        x_ready = sem("x_ready")
        p_ready = sem("p_ready")
        hi_ready = sem("hi_ready")
        lo_ready = sem("lo_ready")
        xv_ready = sem("xv_ready")
        v_ready = sem("v_ready")
        s_ready = sem("s_ready")
        max_ready = sem("max_ready")
        e_ready = sem("e_ready")
        inv_ready = sem("inv_ready")
        scaled_dve = sem("scaled_dve")
        scaled_act = sem("scaled_act")
        turned = [sem("turned_bank0"), sem("turned_bank1")]
        eT_out = [sem("eT_bank0_dve"), sem("eT_bank1_act")]
        o_ready = sem("o_ready")
        oT_ready = sem("oT_ready")
        y_ready = sem("y_ready")

        def pieces(n):
            tiles = tile_of(n) + 1
            return [(0, 0, 4), (1, 4, tiles - 4)] if n % JOBS < WIDE else [(n % 2, 0, tiles)]

        with nc.Block() as block:
            @block.sync
            def _(sp):
                sp.dma_start(w[:], w_d[0]).then_inc(w_loaded, 16)
                with sp.Fori(0, UNITS) as u:
                    sp.wait_ge(y_ready, u + 1)
                    sp.dma_start(wo[:], wo_d[bass.ds(u % PAIRS, 1)].rearrange("a p e -> (a p) e")).then_inc(wo_loaded, 16)
                    sp.wait_ge(p_ready, 6 * u + 6)
                    sp.dma_start(w[:], w_d[bass.ds((u + 1) % PAIRS, 1)].rearrange("a p c e -> (a p) c e")).then_inc(w_loaded, 16)

            @block.tensor
            def _(pe):
                def project(u, m, first=False):
                    if m == 0:
                        pe.wait_ge(w_loaded, 16 * u + 16)
                        pe.wait_ge(xv_ready, u + 1)
                    if m >= 2:
                        pe.wait_ge(lo_ready, PARTS[4] * u + PARTS[m - 1])
                    elif not first:
                        pe.wait_ge(e_ready, JOBS * u - WIDE - 1 + m)
                    out = c.slots[m % 2][:, 1, :]
                    if m < 4:
                        j = pe.matmul(out, w[:, m // 2, :], xv[:, m % 2 * HALF:(m % 2 + 1) * HALF],
                                      start=True, stop=True)
                    else:
                        for t in range(4):
                            at = (4 * (m - 4) + t) * P
                            j = pe.matmul(out[:, t * P:(t + 1) * P], xv[:, at:at + P], w[:, 2, :], start=True, stop=True)
                    j.then_inc(p_ready, 1)

                def scores(u, n, k, first=False):
                    i, h = tile_of(n), n % 2
                    if n % JOBS < 2:
                        unit = u + n // JOBS
                        pe.wait_ge(lo_ready, PARTS[4] * (unit + 1))
                        pe.wait_ge(v_ready, 2 * unit + h + 1)
                    if not (first and n < 2):
                        pe.wait_ge(e_ready, JOBS * u + n - 1)
                    qi = q[k][h][:, i * P:(i + 1) * P]
                    for bank in range(i // 4 + 1):
                        lo, hi = bank * 512, min((i + 1) * P, bank * 512 + 512)
                        out = c.slots[h][:, bank, 0:hi - lo]
                        pe.matmul(out, qi, k_hi[k][h][:, lo:hi], start=True, stop=False)
                        if bank == i // 4:
                            pe.matmul(c.slots[h][:, bank, hi - lo - P:hi - lo], c.ident_bf[:], c.causal[:],
                                      start=False, stop=False, skip_group_check=True)
                        m = pe.matmul(out, qi, k_lo[k][h][:, lo:hi], start=False, stop=True)
                    m.then_inc(s_ready, 1)

                def transpose(u, n, first=False):
                    r = n % RING
                    pe.wait_ge((scaled_dve, scaled_act)[n % 2], TPB * u + n // 2 + 1)
                    for bank, at, tiles in pieces(n):
                        if not (first and bank_uses(n) == 0):
                            pe.wait_ge(eT_out[bank], USES * u + bank_uses(n))
                        for t in range(tiles):
                            m = pe.transpose(turn[:, bank, t * P:(t + 1) * P], e[r][:, (at + t) * P:(at + t + 1) * P], c.ident[:])
                        m.then_inc(turned[bank], 1)

                def values(u, n, k):
                    i = tile_of(n)
                    if n == 1:
                        pe.wait_ge(x_ready, u + 1)
                    for bank in range(2):
                        pe.wait_ge(eT_out[bank], USES * u + bank_uses(n) + 1)
                    for t in range(i + 1):
                        for h in range(2):
                            m = pe.matmul(o[64 * h:64 * h + 64, i // 4, (i % 4) * P:(i % 4 + 1) * P],
                                          v[k][:, t, 64 * h:64 * h + 64], eT[(n - 1 + h) % RING][:, t * P:(t + 1) * P],
                                          start=(t == 0), stop=(t == i), skip_group_check=True)
                    if i == 0:
                        m.then_inc(o_ready, 1)

                def output(u):
                    pe.wait_ge(wo_loaded, 16 * u + 16)
                    pe.wait_ge(oT_ready, u + 1)
                    for t in range(TPB):
                        m = pe.matmul(o[:, t // 4, (t % 4) * P:(t % 4 + 1) * P], oT[:, t * P:(t + 1) * P],
                                      wo[:], start=True, stop=True)
                    m.then_inc(y_ready, 1)

                def tick(u, n, k, first=False):
                    scores(u, n, k if n < JOBS else 1 - k, first)
                    if n >= T_LAG:
                        transpose(u, n - T_LAG, first)
                    if n > PV_LAG and (n - PV_LAG) % 2 == 1 and n - PV_LAG < JOBS:
                        values(u, n - PV_LAG, k)
                    for m in PROJECT.get(n, ()):
                        project(u + 1, m)

                pe.sem_inc(y_ready, 1)
                for m in range(6):
                    project(0, m, first=True)
                for n in range(AHEAD):
                    tick(0, n, 0, first=True)
                with pe.Fori(0, UNITS // 2) as pair:
                    for k in range(2):
                        u = 2 * pair + k
                        for n in range(AHEAD, JOBS + AHEAD):
                            tick(u, n, k)
                        output(u)

            @block.vector
            def _(dve):
                def low_part(u, m, k):
                    cols = slice(m % 2 * HALF, (m % 2 + 1) * HALF)
                    dve.wait_ge(hi_ready, PARTS[4] * u + PARTS[m + 1])
                    for h in range(2):
                        rows, others = slice(64 * h, 64 * h + 64), slice(64 - 64 * h, P - 64 * h)
                        slot = c.slots[m % 2][rows, 1, :]
                        if m < 2:
                            dve.scalar_tensor_tensor(q[k][h][others, cols], slot, D ** -0.5, q[k][h][rows, cols].bitcast(F32),
                                                     ALU.mult, ALU.subtract).then_inc(lo_ready, 1)
                        else:
                            for out in (rows, others):
                                dve.tensor_tensor(k_lo[k][h][out, cols], slot, k_hi[k][h][rows, cols].bitcast(F32),
                                                  ALU.subtract).then_inc(lo_ready, 1)

                def tick(u, n, k):
                    i, h, col = tile_of(n), n % 2, n % JOBS
                    dve.wait_ge(s_ready, JOBS * u + n + 1)
                    dve.tensor_reduce(nmax[:, col:col + 1], c.slots[h][:].rearrange(flat)[:, 0:(i + 1) * P],
                                      AX.X, ALU.max, negate=True).then_inc(max_ready, 1)
                    if n >= T_LAG:
                        evacuate(u, n - T_LAG)
                    last = n - 1
                    for m in PROJECT.get(last, ()):
                        if m < 4:
                            low_part(u + 1, m, 1 - k)
                    if last >= 0:
                        col = last % JOBS
                        dve.wait_ge(e_ready, JOBS * u + last + 1)
                        dve.reciprocal(inv[:, col:col + 1], total[:, col:col + 1]).then_inc(inv_ready, 1)
                        if last % 2 == 0:
                            dve.wait_ge(inv_ready, JOBS * u + last + 1)
                            part = e[last % RING][:, 0:(tile_of(last) + 1) * P]
                            dve.tensor_scalar(part, part, inv[:, col:col + 1], None, ALU.mult).then_inc(scaled_dve, 1)

                def evacuate(u, n):
                    for bank, at, tiles in pieces(n):
                        if bank == 0:
                            dve.wait_ge(turned[0], USES * u + bank_uses(n) + 1)
                            dve.tensor_copy(eT[n % RING][:, at * P:(at + tiles) * P], turn[:, 0, 0:tiles * P]).then_inc(eT_out[0], 1)

                dve.tensor_copy(xv[:], xT[:, 0:S]).then_inc(xv_ready, 1)
                for m in range(4):
                    low_part(0, m, 0)
                for n in range(AHEAD):
                    tick(0, n, 0)
                with dve.Fori(0, UNITS // 2) as pair:
                    for k in range(2):
                        u = 2 * pair + k
                        for n in range(AHEAD, JOBS + AHEAD):
                            tick(u, n, k)
                            if n == JOBS + PV_LAG - 1:
                                dve.wait_ge(o_ready, u + 1)
                                dve.tensor_copy(oT[:], o[:].rearrange(flat)).then_inc(oT_ready, 1)
                        dve.wait_ge(y_ready, u + 2)
                        dve.wait_ge(x_ready, u + 1)
                        xs = c.X[:, bass.ds((u // PAIRS) * TPB, TPB), :].rearrange("p t d -> p (t d)")
                        dve.tensor_tensor(xs, o[:].rearrange(flat), xs, ALU.add).then_inc(x_ready, 1)

            @block.scalar
            def _(act):
                def project_out(u, m, k):
                    cols = slice(m % 2 * HALF, (m % 2 + 1) * HALF)
                    act.wait_ge(p_ready, 6 * u + m + 1)
                    if m >= 4:
                        act.activation(v[k][:, 4 * (m - 4):4 * (m - 3), :].rearrange("p t d -> p (t d)"), c.slots[m % 2][:, 1, :],
                                       ACT.Copy).then_inc(v_ready, 1)
                        return
                    for h in range(2):
                        rows, others = slice(64 * h, 64 * h + 64), slice(64 - 64 * h, P - 64 * h)
                        slot = c.slots[m % 2][rows, 1, :]
                        if m < 2:
                            act.activation(q[k][h][rows, cols], slot, ACT.Copy, scale=D ** -0.5).then_inc(hi_ready, 1)
                        else:
                            for out in (rows, others):
                                act.activation(k_hi[k][h][out, cols], slot, ACT.Copy).then_inc(hi_ready, 1)

                def tick(u, n, k):
                    i, h, col = tile_of(n), n % 2, n % JOBS
                    last = n - 1
                    for m in PROJECT.get(last, ()):
                        project_out(u + 1, m, 1 - k)
                    if n >= T_LAG:
                        evacuate(u, n - T_LAG)
                    act.wait_ge(max_ready, JOBS * u + n + 1)
                    act.activation(e[n % RING][:, 0:(i + 1) * P], c.slots[h][:].rearrange(flat)[:, 0:(i + 1) * P], ACT.Exp,
                                   bias=nmax[:, col:col + 1], accum_out=total[:, col:col + 1]).then_inc(e_ready, 1)
                    if last > 0 and last % 2 == 1:
                        col = last % JOBS
                        act.wait_ge(inv_ready, JOBS * u + last + 1)
                        part = e[last % RING][:, 0:(tile_of(last) + 1) * P]
                        act.activation(part, part, ACT.Copy, scale=inv[:, col:col + 1]).then_inc(scaled_act, 1)

                def evacuate(u, n):
                    for bank, at, tiles in pieces(n):
                        if bank == 1:
                            act.wait_ge(turned[1], USES * u + bank_uses(n) + 1)
                            act.activation(eT[n % RING][:, at * P:(at + tiles) * P], turn[:, 1, 0:tiles * P],
                                           ACT.Copy).then_inc(eT_out[1], 1)

                act.preload_act_table(ACT.Exp)
                for m in range(6):
                    project_out(0, m, 0)
                for n in range(AHEAD):
                    tick(0, n, 0)
                with act.Fori(0, UNITS // 2) as pair:
                    for k in range(2):
                        for n in range(AHEAD, JOBS + AHEAD):
                            tick(2 * pair + k, n, k)

            @block.gpsimd
            def _(pool):
                wide = bias[:].rearrange("p (t d) -> p t d", t=1).broadcast_to([P, NT, P])
                pool.tensor_tensor(c.X[:], c.X[:], wide, ALU.add).then_inc(x_ready, 1)
                with pool.Fori(0, UNITS) as u:
                    pool.wait_ge(p_ready, 6 * u + 6)
                    pool.tensor_copy(xv[:], xT[:, bass.ds((((u + 1) % UNITS) // PAIRS) * S, S)]).then_inc(xv_ready, 1)
        clear()


def host_constants():
    eye = np.eye(P, dtype=np.float32)
    future = np.triu(np.full((P, P), BIG, np.float32), 1)
    sel = np.zeros((4, P, 2, 4, 32), np.float32)
    for head in range(16):
        sel[head // 4, head * 8:head * 8 + 8, head // 2 % 2, :, 16 + head % 2] = 1
    masks = np.zeros((4, 32, 8), np.float32)
    for j in range(2):
        masks[:, 8 * j:8 * j + 8, 2 * j] = 1
        masks[0:2, 16 + j, 2 * j + 1] = -1
    masks[:, :, 6] = 1
    masks[:, 16:18, 6] = np.float32(1) / np.sqrt(np.float32(8))
    D, WIN = 64, 64
    half = np.arange(0, D, 2, dtype=np.float32)
    inv_freq = np.float32(1) / np.float32(10000) ** (half / np.float32(D))
    t = np.arange(S, dtype=np.float32)
    freqs = (t[:, None] * inv_freq[None, :]).astype(np.float64)
    growth = ((half + 0.4 * D) / (1.4 * D)).astype(np.float64)[None, :] ** ((t - S // 2) / (WIN // 2)).astype(np.float64)[:, None]
    both = [np.stack([8 * f * growth, f / growth], axis=1) for f in (np.cos(freqs), np.sin(freqs))]
    angles = np.stack([np.concatenate([both[0], both[0]], axis=2), np.concatenate([-both[1], both[1]], axis=2)], axis=1)
    angles = angles.astype(np.float32).reshape(TPB, P, 2, 2, D).transpose(1, 0, 2, 3, 4)
    r, k = np.arange(P)[:, None] % WIN, np.arange(2 * WIN)[None, :]
    second = np.arange(P)[:, None] >= WIN
    place = np.where(second, k, (k + WIN) % (2 * WIN))
    inside = (place >= r) & (place <= r + WIN)
    first = inside & (second | (place >= WIN))
    band = np.stack([np.tile(np.where(m, np.float32(0), np.float32(BIG)), (1, 4)) for m in (first, inside)], axis=1)
    flags = np.tile(np.array([[0, 1]], np.float32), (P, 1))
    centre = eye - np.float32(1) / np.float32(P)
    block_mask = np.kron(np.eye(16, dtype=np.float32), np.ones((8, 8), np.float32))
    return {"ident": eye, "sel": sel.reshape(4, P, 2, P), "masks": masks.reshape(P, 8), "block_mask": block_mask,
            "angles": np.ascontiguousarray(angles), "band": band.astype(np.float32), "flags": flags,
            "centre": centre, "causal": future}


def load_x(nc, c, x_d):
    with ExitStack() as st:
        future = st.enter_context(nc.sbuf_tensor(c.fresh("future"), [P, P], F32))
        sem, clear = semaphores(nc, st)
        loaded = sem("loaded")
        constants_ready = sem("constants_ready")
        with nc.Block() as block:
            @block.sync
            def _(sp):
                sp.dma_start(c.X[:], x_d.rearrange("(t p) d -> p t d", p=P)).then_inc(loaded, 16)
                sp.dma_start(c.ident[:], c.const["ident"]).then_inc(loaded, 16)
                sp.dma_start(future[:], c.const["causal"]).then_inc(loaded, 16)

            @block.vector
            def _(dve):
                dve.memset(c.eps[:], EPS).then_inc(constants_ready, 1)
                dve.wait_ge(loaded, 48)
                dve.tensor_copy(c.ident_bf[:], c.ident[:]).then_inc(constants_ready, 1)
                dve.tensor_copy(c.causal[:], future[:]).then_inc(constants_ready, 1)
        clear()


def store_x(nc, c, out_d):
    with ExitStack() as st:
        sem, clear = semaphores(nc, st)
        stored = sem("stored")
        with nc.Block() as block:
            @block.sync
            def _(sp):
                sp.dma_start(out_d.rearrange("(t p) d -> p t d", p=P), c.X[:]).then_inc(stored, 16)
                sp.wait_ge(stored, 16)


def open_ctx(nc, st, const):
    c = Ctx()
    c.const = const
    c.count = [0]
    c.X = st.enter_context(nc.sbuf_tensor("X", [P, NT, P], F32))
    c.ident = st.enter_context(nc.sbuf_tensor("ident", [P, P], F32))
    c.ident_bf = st.enter_context(nc.sbuf_tensor("ident_bf", [P, P], BF16))
    c.causal = st.enter_context(nc.sbuf_tensor("causal", [P, P], BF16))
    c.stats = st.enter_context(nc.sbuf_tensor("stats", [P, NT, 6], F32))
    c.moments = st.enter_context(nc.sbuf_tensor("moments", [P, NT, 2], F32))
    c.deviation = st.enter_context(nc.sbuf_tensor("deviation", [P, NT], F32))
    c.second = st.enter_context(nc.sbuf_tensor("second", [P, NT], F32))
    c.rstd = st.enter_context(nc.sbuf_tensor("rstd", [P, NT], F32))
    c.eps = st.enter_context(nc.sbuf_tensor("eps", [P, 1], F32))
    c.slots = [st.enter_context(nc.psum_tensor(f"slot{k}", [P, 2, 512], F32)) for k in range(4)]

    def fresh(name):
        c.count[0] += 1
        return f"{name}_{c.count[0]}"
    c.fresh = fresh
    return c


def causal_layout(w_qkv, w_out):
    return np.ascontiguousarray(w_qkv.reshape(3, 8, P, P).transpose(1, 3, 0, 2)), np.ascontiguousarray(w_out.T.reshape(8, P, P))


def distance_layout(W_k):
    wT = W_k.T.reshape(P, 4, 2, 16)
    rep = np.zeros((4, P, 2, 4, 32), W_k.dtype)
    rep[:, :, :, :, 0:16] = wT.transpose(1, 0, 2, 3)[:, :, :, None, :]
    return rep.reshape(4, P, 2, P)


def local_layout(wqkv, q_scale, k_scale, wo, ln_g, ln_b, w1, b1, w2, b2):
    n, hid, chunks = wqkv.shape[0], w2.shape[1], 3
    half = np.zeros((n, P, 2, chunks * P), w1.dtype)
    half[:, :, 0, :hid], half[:, :, 1, :hid] = w1[:, :, :hid], w1[:, :, hid:]
    bias = np.zeros((n, 2, chunks * P), b1.dtype)
    bias[:, 0, :hid], bias[:, 1, :hid] = b1[:, :hid], b1[:, hid:]
    down = np.zeros((n, chunks * P, P), w2.dtype)
    down[:, :hid] = w2
    small = np.concatenate([ln_g[:, None], ln_b[:, None], bias.reshape(n, 2 * chunks, P)], axis=1).transpose(0, 2, 1)
    qk = np.stack([q_scale, k_scale], axis=1)
    scales = np.stack([qk, np.concatenate([qk[:, :, 32:], qk[:, :, :32]], axis=2)], axis=1)
    return {
        "w_qk": np.ascontiguousarray(wqkv[:, :, :1024]),
        "w_v": np.ascontiguousarray(wqkv[:, :, 1024:]),
        "w_o": np.ascontiguousarray(wo.reshape(n, 4, P, P).transpose(0, 2, 1, 3)),
        "w1": half.reshape(n, P, 2, chunks, P),
        "w2": np.ascontiguousarray(down.reshape(n, chunks, P, P).transpose(0, 2, 1, 3)),
        "small": np.ascontiguousarray(small),
        "b2": np.ascontiguousarray(np.broadcast_to(b2[:, None, :], (n, P, P))),
        "scales": np.ascontiguousarray(np.broadcast_to(scales[:, None], (n, P, 2, 2, 64))),
    }


def macaron(nc, d, out_d):
    with ExitStack() as st:
        c = open_ctx(nc, st, {k[6:]: d[k] for k in d if k.startswith("const_")})
        local = {k[6:]: d[k] for k in d if k.startswith("local_")}
        load_x(nc, c, d["x"])
        gelu_ffn(nc, c, d["ffn_w1"], d["ffn_b1"], d["ffn_w2"], d["ffn_b2"])
        distance_attention(nc, c, d["dist_wk"], d["dist_wv"], d["dist_wo"], d["dist_rep"], c.const["sel"], c.const["masks"])
        gelu_ffn(nc, c, d["ffn_w1"], d["ffn_b1"], d["ffn_w2"], d["ffn_b2"])
        local_layers(nc, c, local)
        causal_attention(nc, c, d["causal_gain"], d["causal_shift"], d["causal_w"], d["causal_wo"], d["causal_bias"])
        local_layers(nc, c, local)
        store_x(nc, c, out_d)


def kernel(**inputs):
    import concourse.bacc as bacc
    from concourse.bass_utils import run_bass_kernel_spmd

    a = {k: np.asarray(v) for k, v in inputs.items()}
    flipped = lambda m: np.ascontiguousarray(m.T)
    rows = lambda r: np.ascontiguousarray(np.broadcast_to(r, (P, r.shape[0])))
    causal_w, causal_wo = causal_layout(a["L1_attn_w_qkv"], a["L1_attn_w_out"])
    names = ["wqkv", "q_scale", "k_scale", "wo", "ln_g", "ln_b", "w1", "b1", "w2", "b2"]
    data = {
        "x": a["L0_attn_x"].reshape(NT * P, P),
        "ffn_w1": a["L0_ffn_w1"], "ffn_b1": flipped(a["L0_ffn_b1"].reshape(-1, P)),
        "ffn_w2": a["L0_ffn_w2"], "ffn_b2": rows(a["L0_ffn_b2"]),
        "dist_wk": flipped(a["L0_attn_W_k"]), "dist_wv": flipped(a["L0_attn_W_v"]),
        "dist_wo": flipped(a["L0_attn_W_o"]), "dist_rep": distance_layout(a["L0_attn_W_k"]),
        "causal_gain": a["L1_attn_ln_gamma"].reshape(P, 1), "causal_shift": a["L1_attn_ln_beta"].reshape(P, 1),
        "causal_w": causal_w, "causal_wo": causal_wo, "causal_bias": rows(a["L1_attn_b_out"]),
    }
    data.update({"local_" + k: v for k, v in local_layout(*[a["L1_ffn_" + n] for n in names]).items()})
    data.update({"const_" + k: v for k, v in host_constants().items()})

    nc = bacc.Bacc("TRN2", target_bir_lowering=False, num_devices=1)
    arrays = {f"in_{k}_dram": np.ascontiguousarray(v) for k, v in data.items()}
    d = {k: nc.dram_tensor(f"in_{k}_dram", v.shape, mybir.dt.from_np(v.dtype), kind="ExternalInput").ap()
         for k, v in data.items()}
    out_d = nc.dram_tensor("out_0_dram", (NT * P, P), F32, kind="ExternalOutput").ap()
    macaron(nc, d, out_d)
    result = run_bass_kernel_spmd(nc, [arrays], core_ids=[0])
    return result.results[0]["out_0_dram"].reshape(B, S, P)
```
